# Optimizing a Trainium2 kernel written in Bass

```python
import numpy as np
import jax
import jax.numpy as jnp

def _softmax(x, axis=-1):
    return jax.nn.softmax(x, axis=axis)

def _gelu(x):
    return jax.nn.gelu(x, approximate=True)

def _silu(x):
    return jax.nn.silu(x)

def _sigmoid(x):
    return jax.nn.sigmoid(x)

def _layernorm(x, axis=-1, eps=1e-05):
    m = jnp.mean(x, axis=axis, keepdims=True)
    v = jnp.var(x, axis=axis, keepdims=True)
    return (x - m) / jnp.sqrt(v + eps)

def _scatter_add(tgt, idx, src, axis=0):
    return tgt.at[idx].add(src)

def _segment_sum(src, seg, n):
    return jax.ops.segment_sum(src, seg, n)
kernel_name = 'mk_decoder_postln_d1_seqx_r8_4dee4f'

def setup_inputs(seed: int=0):
    np.random.seed(seed)
    _w = jnp.asarray

    def _rec_inputs():
        import jax
        import jax.numpy as jnp
        _rk = jax.random.key(seed)
        x = -0.0003929 + 0.9999 * jax.random.normal(jax.random.fold_in(_rk, 1), (16, 56, 128), jnp.float32)
        _lenS = 56 - jax.random.randint(jax.random.fold_in(_rk, 7), (16,), 0, max(1, 56 // 4) + 1, jnp.int32)
        _lenS2 = 1500 - jax.random.randint(jax.random.fold_in(_rk, 8), (16,), 0, max(1, 1500 // 4) + 1, jnp.int32)
        _ctx_768P = jax.random.normal(jax.random.fold_in(_rk, 11), (16, 16, 96), jnp.float32)
        _ctx_768c = jax.random.dirichlet(jax.random.fold_in(_rk, 511), 0.3 * jnp.ones((16,), jnp.float32), (16, 1500))
        _ctx_768t = jnp.einsum('bsk,bkd->bsd', _ctx_768c, _ctx_768P)
        _ctx_768t = _ctx_768t * jax.lax.rsqrt(jnp.mean(jnp.square(_ctx_768t)) + 1e-12) * 0.953939
        ctx_768 = -7.36909e-05 + 0.999899 * (_ctx_768t + 0.3 * jax.random.normal(jax.random.fold_in(_rk, 611), (16, 1500, 96), jnp.float32))
        return (x, ctx_768)
    x, ctx_768 = _rec_inputs()

    def _L0_attn_setup():
        import jax, jax.numpy as jnp
        import numpy as np
        B, L, D = (2, 256, 128)
        K, M, A = (32, 4, 4)
        H = D // K
        CK = 4
        TOTAL = 2 * D + K

        def _glorot(k, shape):
            lim = np.sqrt(6.0 / (shape[0] + shape[1]))
            return jax.random.uniform(k, shape, jnp.float32, -lim, lim)
        key = jax.random.key(seed)
        ks = jax.random.split(key, 8)
        grid = np.linspace(-np.pi / 3, np.pi / 3, M, dtype=np.float32)
        theta = np.tile(grid.reshape(1, 1, 1, 1, M), (1, 1, K, H, 1)).astype(np.float32)
        dr = np.geomspace(0.001, 0.1, K - A).astype(np.float32)
        ar = np.geomspace(0.01, 0.1, A).astype(np.float32)
        return {'x': jax.random.normal(ks[0], (B, L, D), jnp.float32), 'in_proj_w': _glorot(ks[1], (D, TOTAL)), 'conv_w': jax.random.normal(ks[2], (CK, 1, TOTAL), jnp.float32) * 0.1, 'conv_b': jnp.zeros((TOTAL,), jnp.float32), 'theta': jnp.asarray(theta), 'decay_slopes': jnp.asarray(np.log(np.exp(dr) - 1.0)), 'anchor_slopes': jnp.asarray(np.log(np.exp(ar) - 1.0)), 'score_scale': jnp.ones((K,), jnp.float32), 'deriv_logits': jnp.asarray([5.0, 0.0, 0.0], jnp.float32), 'norm_scale': jnp.ones((2 * H * M,), jnp.float32), 'W_re': _glorot(ks[3], (H * M, H)), 'W_im': _glorot(ks[4], (H * M, H)), 'out_proj_w': _glorot(ks[5], (D, D))}
    _L0_attn_all = _L0_attn_setup()
    _L0_attn_in = {k: v for k, v in _L0_attn_all.items() if k in ('in_proj_w', 'conv_w', 'conv_b', 'theta', 'decay_slopes', 'anchor_slopes', 'score_scale', 'deriv_logits', 'norm_scale', 'W_re', 'W_im', 'out_proj_w')}
    del _L0_attn_all

    def _L0_xattn_setup():
        import jax, jax.numpy as jnp
        import numpy as np
        IMG_DIM, TXT_DIM, HID = (128, 96, 128)
        B, LQ, LK = (8, 256, 256)
        key = jax.random.key(seed)
        ks = jax.random.split(key, 8)
        s_img = 1.0 / np.sqrt(IMG_DIM)
        s_txt = 1.0 / np.sqrt(TXT_DIM)
        return {'image_features': jax.random.normal(ks[0], (B, LQ, IMG_DIM), jnp.float32), 'text_features': jax.random.normal(ks[1], (B, LK, TXT_DIM), jnp.float32), 'Wq': jax.random.uniform(ks[2], (IMG_DIM, HID), jnp.float32, -s_img, s_img), 'bq': jax.random.uniform(ks[3], (HID,), jnp.float32, -s_img, s_img), 'Wk': jax.random.uniform(ks[4], (TXT_DIM, HID), jnp.float32, -s_txt, s_txt), 'bk': jax.random.uniform(ks[5], (HID,), jnp.float32, -s_txt, s_txt), 'Wv': jax.random.uniform(ks[6], (TXT_DIM, HID), jnp.float32, -s_txt, s_txt), 'bv': jax.random.uniform(ks[7], (HID,), jnp.float32, -s_txt, s_txt)}
    _L0_xattn_all = _L0_xattn_setup()
    _L0_xattn_in = {k: v for k, v in _L0_xattn_all.items() if k in ('Wq', 'bq', 'Wk', 'bk', 'Wv', 'bv')}
    del _L0_xattn_all

    def _L0_ffn_setup():
        import jax, jax.numpy as jnp
        import numpy as np
        B, S, D, F, E = (2, 256, 128, 512, 8)
        LN_EPS = 1e-05

        def _layer_norm(x, gamma, beta):
            mu = jnp.mean(x, axis=-1, keepdims=True)
            var = jnp.mean(jnp.square(x - mu), axis=-1, keepdims=True)
            return (x - mu) * jax.lax.rsqrt(var + LN_EPS) * gamma + beta
        key = jax.random.key(seed)
        ks = jax.random.split(key, 8)

        def xavier(k, shape):
            fan_in, fan_out = (shape[-1], shape[-2])
            a = jnp.sqrt(6.0 / (fan_in + fan_out))
            return jax.random.uniform(k, shape, jnp.float32, -a, a)
        return {'tgt': jax.random.normal(ks[0], (B, S, D), jnp.float32), 'Wr': xavier(ks[1], (E, D)), 'br': jnp.zeros((E,), jnp.float32), 'W1': xavier(ks[2], (E, F, D)), 'b1': jnp.zeros((E, F), jnp.float32), 'W2': xavier(ks[3], (E, D, F)), 'b2': jnp.zeros((E, D), jnp.float32), 'gamma': jnp.ones((D,), jnp.float32), 'beta': jnp.zeros((D,), jnp.float32)}
    _L0_ffn_all = _L0_ffn_setup()
    _L0_ffn_in = {k: v for k, v in _L0_ffn_all.items() if k in ('Wr', 'br', 'W1', 'b1', 'W2', 'b2', 'gamma', 'beta')}
    del _L0_ffn_all
    return {'x': x, 'ctx_768': ctx_768, 'L0_attn_in_proj_w': _L0_attn_in['in_proj_w'], 'L0_attn_conv_w': _L0_attn_in['conv_w'], 'L0_attn_conv_b': _L0_attn_in['conv_b'], 'L0_attn_theta': _L0_attn_in['theta'], 'L0_attn_decay_slopes': _L0_attn_in['decay_slopes'], 'L0_attn_anchor_slopes': _L0_attn_in['anchor_slopes'], 'L0_attn_score_scale': _L0_attn_in['score_scale'], 'L0_attn_deriv_logits': _L0_attn_in['deriv_logits'], 'L0_attn_norm_scale': _L0_attn_in['norm_scale'], 'L0_attn_W_re': _L0_attn_in['W_re'], 'L0_attn_W_im': _L0_attn_in['W_im'], 'L0_attn_out_proj_w': _L0_attn_in['out_proj_w'], 'L0_xattn_Wq': _L0_xattn_in['Wq'], 'L0_xattn_bq': _L0_xattn_in['bq'], 'L0_xattn_Wk': _L0_xattn_in['Wk'], 'L0_xattn_bk': _L0_xattn_in['bk'], 'L0_xattn_Wv': _L0_xattn_in['Wv'], 'L0_xattn_bv': _L0_xattn_in['bv'], 'L0_ffn_Wr': _L0_ffn_in['Wr'], 'L0_ffn_br': _L0_ffn_in['br'], 'L0_ffn_W1': _L0_ffn_in['W1'], 'L0_ffn_b1': _L0_ffn_in['b1'], 'L0_ffn_W2': _L0_ffn_in['W2'], 'L0_ffn_b2': _L0_ffn_in['b2'], 'L0_ffn_gamma': _L0_ffn_in['gamma'], 'L0_ffn_beta': _L0_ffn_in['beta']}

def reference(x, ctx_768, L0_attn_in_proj_w, L0_attn_conv_w, L0_attn_conv_b, L0_attn_theta, L0_attn_decay_slopes, L0_attn_anchor_slopes, L0_attn_score_scale, L0_attn_deriv_logits, L0_attn_norm_scale, L0_attn_W_re, L0_attn_W_im, L0_attn_out_proj_w, L0_xattn_Wq, L0_xattn_bq, L0_xattn_Wk, L0_xattn_bk, L0_xattn_Wv, L0_xattn_bv, L0_ffn_Wr, L0_ffn_br, L0_ffn_W1, L0_ffn_b1, L0_ffn_W2, L0_ffn_b2, L0_ffn_gamma, L0_ffn_beta):
    import jax
    import jax.numpy as jnp

    def _L0_attn_ref(x, in_proj_w, conv_w, conv_b, theta, decay_slopes, anchor_slopes, score_scale, deriv_logits, norm_scale, W_re, W_im, out_proj_w):
        import jax, jax.numpy as jnp
        import numpy as np
        B, L, D = (2, 256, 128)
        K, M, A = (32, 4, 4)
        H = D // K
        CK = 4
        TOTAL = 2 * D + K

        def _glorot(k, shape):
            lim = np.sqrt(6.0 / (shape[0] + shape[1]))
            return jax.random.uniform(k, shape, jnp.float32, -lim, lim)
        b, l, d = x.shape
        z = x @ in_proj_w
        zp = jnp.pad(z, ((0, 0), (CK - 1, 0), (0, 0)))
        z = jax.lax.conv_general_dilated(zp, conv_w, (1,), 'VALID', dimension_numbers=('NWC', 'WIO', 'NWC'), feature_group_count=TOTAL) + conv_b
        x_val = z[..., :D].reshape(b, l, K, H)
        x_gate = jax.nn.silu(z[..., D:2 * D])
        s_raw = z[..., -K:].reshape(b, l, K, 1)
        pos = jnp.arange(l, dtype=jnp.float32)
        d_slopes = jax.nn.softplus(decay_slopes).reshape(1, 1, K - A, 1)
        dist_d = jnp.maximum(jnp.float32(l - 1) - pos, 0.0)[None, :, None, None]
        w_decay = jnp.exp(-d_slopes * dist_d)
        a_slopes = jax.nn.softplus(anchor_slopes).reshape(1, 1, A, 1)
        w_anchor = jnp.exp(-a_slopes * pos[None, :, None, None])
        time_weight = jnp.concatenate([w_decay, w_anchor], axis=2)
        p = jnp.exp(jnp.clip(score_scale[None, None, :, None] * s_raw, -20.0, 20.0))
        x5 = x_val[..., None]
        phi = x5 * theta
        cos_b, sin_b = (jnp.cos(phi), jnp.sin(phi))
        w = jax.nn.softmax(deriv_logits)
        poly = w[0] + w[1] * x5 - w[2] * jnp.square(x5)
        re_m = poly * cos_b
        im_m = poly * sin_b
        p_w = (p * time_weight)[..., None]
        flat = (b, l, K * H * M)
        merged = jnp.concatenate([(p_w * re_m).reshape(flat), (p_w * im_m).reshape(flat), jnp.broadcast_to(p_w, (b, l, K, H, M)).reshape(flat)], axis=-1)
        num_re, num_im, den = jnp.split(jnp.cumsum(merged, axis=1), 3, axis=-1)
        inv_den = 1.0 / jnp.maximum(den, jnp.float32(0.0001))
        re = (num_re * inv_den).reshape(b, l, K, H * M)
        im = (num_im * inv_den).reshape(b, l, K, H * M)
        mean_sq = (jnp.sum(jnp.square(re), -1) + jnp.sum(jnp.square(im), -1)) / (2.0 * H * M)
        rs = jax.lax.rsqrt(mean_sq[..., None] + 1e-05)
        y = re * rs * norm_scale[:H * M] @ W_re + im * rs * norm_scale[H * M:] @ W_im
        y = y.reshape(b, l, D)
        return y * x_gate @ out_proj_w

    def _L0_xattn_ref(image_features, text_features, Wq, bq, Wk, bk, Wv, bv):
        import jax, jax.numpy as jnp
        import numpy as np
        IMG_DIM, TXT_DIM, HID = (128, 96, 128)
        B, LQ, LK = (8, 256, 256)
        query = jnp.einsum('bqi,ih->bqh', image_features, Wq) + bq
        key = jnp.einsum('bkt,th->bkh', text_features, Wk) + bk
        value = jnp.einsum('bkt,th->bkh', text_features, Wv) + bv
        scale = 1.0 / jnp.sqrt(jnp.asarray(HID, query.dtype))
        scores = jnp.einsum('bqh,bkh->bqk', query, key) * scale
        weights = jax.nn.softmax(scores, axis=-1)
        attended = jnp.einsum('bqk,bkh->bqh', weights, value)
        return attended

    def _L0_ffn_ref(tgt, Wr, br, W1, b1, W2, b2, gamma, beta):
        import jax, jax.numpy as jnp
        import numpy as np
        B, S, D, F, E = (2, 256, 128, 512, 8)
        LN_EPS = 1e-05

        def _layer_norm(x, gamma, beta):
            mu = jnp.mean(x, axis=-1, keepdims=True)
            var = jnp.mean(jnp.square(x - mu), axis=-1, keepdims=True)
            return (x - mu) * jax.lax.rsqrt(var + LN_EPS) * gamma + beta
        logits = jnp.einsum('bsd,ed->bse', tgt, Wr) + br
        top_v, top_i = jax.lax.top_k(logits, 2)
        top_w = jax.nn.softmax(top_v, axis=-1)
        n_exp = logits.shape[-1]
        router_w = jnp.sum(jax.nn.one_hot(top_i, n_exp, dtype=top_w.dtype) * top_w[..., None], axis=-2)
        h = jnp.einsum('bsd,efd->bsef', tgt, W1) + b1
        h = jax.nn.relu(h)
        o = jnp.einsum('bsef,edf->bsed', h, W2) + b2
        tgt2 = jnp.einsum('bsed,bse->bsd', o, router_w)
        return _layer_norm(tgt + tgt2, gamma, beta)
    x = _layernorm(x + _L0_attn_ref(x, L0_attn_in_proj_w, L0_attn_conv_w, L0_attn_conv_b, L0_attn_theta, L0_attn_decay_slopes, L0_attn_anchor_slopes, L0_attn_score_scale, L0_attn_deriv_logits, L0_attn_norm_scale, L0_attn_W_re, L0_attn_W_im, L0_attn_out_proj_w), axis=-1)
    x = _layernorm(x + _L0_xattn_ref(x, ctx_768, L0_xattn_Wq, L0_xattn_bq, L0_xattn_Wk, L0_xattn_bk, L0_xattn_Wv, L0_xattn_bv), axis=-1)
    x = _layernorm(x + _L0_ffn_ref(x, L0_ffn_Wr, L0_ffn_br, L0_ffn_W1, L0_ffn_b1, L0_ffn_W2, L0_ffn_b2, L0_ffn_gamma, L0_ffn_beta), axis=-1)
    return x

_drawn_inputs = setup_inputs


def setup_inputs(seed=0):
    import zlib

    import numpy as np

    out = dict(_drawn_inputs(seed))
    spreads = {'L0_attn_conv_b': (0.0, 0.1),
     'L0_attn_score_scale': (1.0, 0.6),
     'L0_attn_norm_scale': (1.0, 0.2),
     'L0_ffn_br': (0.0, 0.1),
     'L0_ffn_b1': (0.0, 0.1),
     'L0_ffn_b2': (0.0, 0.1),
     'L0_ffn_gamma': (1.0, 0.2),
     'L0_ffn_beta': (0.0, 0.1)}
    factors = {'L0_attn_theta': 3.11,
     'L0_attn_decay_slopes': 64.0,
     'L0_attn_anchor_slopes': 64.0,
     'L0_attn_W_im': 3.052,
     'L0_xattn_bq': 8.0,
     'L0_xattn_bk': 64.0}
    for name, (base, spread) in spreads.items():
        noise = np.random.default_rng([zlib.crc32(name.encode()), seed]).standard_normal(out[name].shape)
        drawn = base * np.exp(spread * noise) if base else spread * noise
        out[name] = jnp.asarray(drawn.astype(out[name].dtype))
    for name, factor in factors.items():
        out[name] = (out[name] * factor).astype(out[name].dtype)
    return out
```

```python
from contextlib import ExitStack
from math import log, pi, sqrt

import numpy as np

import concourse.bass as bass
from concourse import mybir

ALU = mybir.AluOpType
ACT = mybir.ActivationFunctionType
AX = mybir.AxisListType
F32 = mybir.dt.float32
F16 = mybir.dt.float16
U32 = mybir.dt.uint32

B, L, D = 16, 56, 128
K, H, M = 32, 4, 4
TAPS = 4
SK, DC = 1500, 96
E, F = 8, 512
T = B * L
HALVES = 2
HB = B // HALVES
HW = HB * L
PAIRS = B // 2
PT = 2 * L
PPH = PAIRS // HALVES
GAP = 64
GT = GAP + L
KP, KC = 125, 12
SN = 500
SB = SK // SN
FC = F // 128
HT = 128
WS = 16.0
MAGIC = 1.5 * 2.0 ** 23
LN_EPS = 1e-5
V_DOWN = 20

FIRST = [("w_in", 3 * D), ("conv_b", 3)]
SMALL = [("theta", M), ("slope", 1), ("dist", L), ("score_scale", 1), ("deriv", 3), ("norm_scale", 2 * M),
         ("w_ri", 2 * M * H), ("group_mask", D), ("ident", D), ("w_out", D), ("w_q", D), ("b_q", 1),
         ("w_k", DC + 1), ("w_v", D), ("w_r", E), ("b_r", E), ("gamma", D), ("beta", D), ("b_1", E * FC),
         ("b_2", D), ("iota", E)]


def places(names):
    at, n = {}, 0
    for name, width in names:
        at[name] = (n, n + width)
        n += width
    return at, n


class Own:

    def __init__(self, eng, sem):
        self.eng, self.sem, self.base, self.n = eng, sem, 0, 0

    def turn(self, base):
        self.base, self.n = base, 0

    def mark(self, ins):
        ins.then_inc(self.sem, 1)
        self.n += 1
        return self.base + self.n

    def need(self, value):
        self.eng.wait_ge(self.sem, value)


def decoder_kernel(nc, x_T, x_tok, ctx, ctx_T, first, conv_w, small, w_1, w_2, out):
    with ExitStack() as stack:
        def sb(name, shape, dt=F32):
            return stack.enter_context(nc.sbuf_tensor(name, shape, dt))

        def sem(name):
            return stack.enter_context(nc.semaphore(name))

        bank = stack.enter_context(nc.psum_tensor("bank", [128, 8, 512], F32))

        at1, n1 = places(FIRST)
        at2, n2 = places(SMALL)
        first_sb = sb("first_sb", [128, n1])
        small_sb = sb("small_sb", [128, n2])
        convw_sb = sb("convw_sb", [128, TAPS, 3 * D])

        def par(name, rows=128):
            a, b = at1[name] if name in at1 else at2[name]
            return (first_sb if name in at1 else small_sb)[0:rows, a:b]

        ident = par("ident")
        w_conv = sb("w_conv", [128, TAPS, 3 * D])
        w_blk = sb("w_blk", [128, 2 * M, D])
        w_rin = sb("w_rin", [128, 2 * M, H])
        w_v = sb("w_v", [DC + 1, D + 1])
        time_w = sb("time_w", [128, L])
        reset = sb("reset", [128, M * HW])
        cst = sb("cst", [128, 4])
        sp = sb("sp", [128, 4])
        dsm = sb("dsm", [128, 12])
        theta_t = sb("theta_t", [128, M])
        sbias = sb("sbias", [128, 1])
        gbias = sb("gbias", [128, 1])
        qbias = sb("qbias", [128, 1])

        xpad = sb("xpad", [128, B, L + TAPS - 1])
        xtok = sb("xtok", [PT, PAIRS, D])
        x1 = sb("x1", [PT, PAIRS, D])
        x1T = sb("x1T", [128, T])
        x2 = sb("x2", [PT, PAIRS, D])
        x2T = sb("x2T", [128, T])
        x2h = sb("x2h", [128, T], F16)
        x2l = sb("x2l", [128, T], F16)

        xv = sb("xv", [128, HALVES, HW])
        xg = sb("xg", [128, HALVES, HW])
        sc = sb("sc", [128, HALVES, HW])
        gate = sb("gate", [128, HALVES, HW])
        q0 = sb("q0", [128, HW])
        ph = sb("ph", [128, M, HW])
        pc = sb("pc", [128, M, HW])
        work = max((2 * M + 1) * HW, FC * PAIRS * HT)
        terms = sb("terms", [128, work])
        sums = sb("sums", [128, work])
        squares = sb("squares", [128, 2 * M * HW])
        y_gated = sb("y_gated", [128, HALVES, HW])

        ctx_slot = sb("ctx_slot", [KP, 2, 2, KC, DC + 1])
        ctxT_slot = sb("ctxT_slot", [DC + 1, 2, 2, SK])
        q_sb = sb("q_sb", [128, PT])
        qk_sb = sb("qk_sb", [DC + 1, PT])
        neg_max = sb("neg_max", [128, 1])
        u_sb = sb("u_sb", [GT, DC + 1])
        uT_sb = sb("uT_sb", [DC + 1, PT])
        rden = sb("rden", [PT, 1])
        res = sb("res", [PT, D])
        x2_now = sb("x2_now", [PT, D])
        stat = sb("stat", [PT, PAIRS, 6])
        mv = sb("mv", [PT, PAIRS, 2])
        lnv = sb("lnv", [PT, PAIRS])
        rstd = sb("rstd", [PT, PAIRS])
        exp_sb = squares[0:GT, 0:SK]
        expT_sb = ph[0:KP].rearrange("p m w -> p (m w)")[:, 0:KC * GT].rearrange("p (c q) -> p c q", c=KC)

        w_raw = sb("w_raw", [128, 2, 2, F])
        w1h = sb("w1h", [128, 2, F], F16)
        w1l = sb("w1l", [128, 2, F], F16)
        w2h = sb("w2h", [128, 2, FC, D], F16)
        w2l = sb("w2l", [128, 2, FC, D], F16)
        hid = pc[:]
        nh = 2 * FC * PAIRS * HT
        hh = terms[:, 0:nh // 2].bitcast(F16).rearrange("p (s f j t) -> p s f j t", s=2, f=FC, j=PAIRS)
        hl = sums[:, 0:nh // 2].bitcast(F16).rearrange("p (s f j t) -> p s f j t", s=2, f=FC, j=PAIRS)
        x2b = sb("x2b", [PT, PAIRS, D])
        carrier = sb("carrier", [128, 1])
        b1_now = sb("b1_now", [128, 2, FC])
        logit = sb("logit", [PT, PAIRS, E])
        top = sb("top", [PT, PAIRS, 8])
        topi = sb("topi", [PT, PAIRS, 8], U32)
        topf = sb("topf", [PT, PAIRS, 2])
        tsm = sb("tsm", [PT, 6, PAIRS])
        rw = sb("rw", [PT, PAIRS, E])
        rws = sb("rws", [PT, PAIRS, E])
        rwT = sb("rwT", [E, T])
        acc = xtok

        s_in = sem("first_params_loaded")
        s_cw = sem("conv_weights_loaded")
        s_xT = sem("x_transposed_loaded")
        s_par = sem("small_params_loaded")
        s_xtok = sem("x_tokens_loaded")
        s_ctx = [sem(f"ctx_loaded_{s}") for s in range(2)]
        s_ctxT = [sem(f"ctxT_loaded_{s}") for s in range(2)]
        s_w = [sem(f"expert_weights_loaded_{s}") for s in range(4)]
        s_zero = sem("pads_set")
        s_cst = sem("constants_set")
        s_ones = sem("context_ones_set")
        s_convw = sem("conv_folded")
        s_z = sem("z_done")
        s_zact = sem("z_read")
        s_score = sem("score_clipped")
        s_p = sem("score_exp")
        s_sp = sem("small_act")
        s_sd = sem("small_dve")
        s_gate = sem("gate_read")
        s_phase = sem("phase_reduced")
        s_trig = sem("sines_done")
        s_turns = sem("whole_turns_done")
        s_poly = sem("weighted_polynomial_done")
        s_im = sem("sin_terms_done")
        s_sum = sem("sums_done")
        s_sq = sem("squares_done")
        s_blk = sem("group_weights_ready")
        s_y = sem("y_done")
        s_ss = sem("square_sums_done")
        s_v = sem("variance_ready")
        s_f = sem("factor_ready")
        s_yg = sem("y_gated_ready")
        s_o = sem("mix_out_done")
        s_var = sem("mix_variance_ready")
        s_rstd = sem("mix_rstd_ready")
        s_x1 = sem("x1_ready")
        s_x1t = sem("x1_turned")
        s_x1T = sem("x1T_ready")
        own_v, own_a, own_g = sem("vector_own"), sem("scalar_own"), sem("gpsimd_own")
        loop_v, loop_a, loop_g = sem("vector_attend_own"), sem("scalar_attend_own"), sem("gpsimd_attend_own")
        a_q, a_qsb, a_qk, a_qksb = sem("q_done"), sem("q_read"), sem("qk_done"), sem("qk_read")
        a_s, a_max, a_exp, a_t = sem("scores_done"), sem("max_done"), sem("weights_done"), sem("weights_turned")
        a_et, a_pv, a_u = sem("turned_read"), sem("context_sum_done"), sem("context_sum_read")
        a_ut, a_utsb, a_r = sem("context_sum_turned"), sem("context_sum_turned_read"), sem("values_done")
        a_res, a_rstd, a_x2 = sem("attended_stats_ready"), sem("attend_rstd_ready"), sem("x2_ready")
        a_x2t, a_x2T, a_x2s = sem("x2_turned"), sem("x2T_ready"), sem("x2_split")
        m_wl = sem("expert_weights_split")
        m_log, m_logit, m_e = sem("logits_done"), sem("routing_dve"), sem("routing_exp")
        m_rw, m_rt, m_rwT = (sem("router_weights_ready"), sem("router_weights_turned"),
                              sem("router_weights_T_ready"))
        m_l1, m_relu, m_hl = sem("hidden_done"), sem("relu_done"), sem("hidden_split")
        m_b1, m_x2b = sem("b1_ready"), sem("x2_plus_beta_ready")
        m_l2, m_acc = sem("expert_out_done"), sem("expert_out_added")
        m_pad = sem("hidden_pads_set")
        mo_v = sem("vector_experts_own")
        f_var, f_rstd, f_out = sem("final_variance_ready"), sem("final_rstd_ready"), sem("final_ready")
        s_store = sem("stored")

        block = stack.enter_context(nc.Block())

        Y_BANK, SS_BANK, O_BANK, T_BANK = (6, 0), (7, 1), (2, 3), (5, 4)

        C_EPS, C_HALFPI, C_FACTOR, C_ONE = range(4)

        @block.sync
        def _(sp_):
            sp_.dma_start(first_sb[:], first).then_inc(s_in, 16)
            sp_.dma_start(convw_sb[:].rearrange("p k n -> p (k n)"), conv_w.partition_broadcast(128)).then_inc(s_cw, 16)
            sp_.wait_ge(s_zero, 1)
            sp_.dma_start(xpad[:, :, TAPS - 1:], x_T.rearrange("p (b l) -> p b l", b=B)).then_inc(s_xT, 16)
            sp_.dma_start(small_sb[:], small).then_inc(s_par, 16)
            sp_.dma_start(xtok[:], x_tok.rearrange("(i p) d -> p i d", p=PT)).then_inc(s_xtok, 16)

            def ctx_pair(i, s):
                for j in range(2):
                    sp_.dma_start(ctxT_slot[0:DC, s, j, :], ctx_T[2 * i + j]).then_inc(s_ctxT[s], 16)

            def ctx_rows(i, s):
                for j in range(2):
                    sp_.dma_start(ctx_slot[:, s, j, :, 0:DC],
                                  ctx[2 * i + j]).then_inc(s_ctx[s], 16)

            def load_w(which, e, s):
                src = (w_1, w_2)[which][e]
                sp_.dma_start(w_raw[:, s, which, :], src).then_inc(s_w[2 * which + s], 16)

            for s in range(2):
                ctx_pair(s, s)
                ctx_rows(s, s)
            for s in range(2):
                load_w(0, s, s)
                load_w(1, s, s)
            with sp_.Fori(0, PAIRS // 2 - 1) as t:
                for s in range(2):
                    sp_.wait_ge(a_s, 2 * t + s + 1)
                    ctx_pair(2 * t + s + 2, s)
                    sp_.wait_ge(a_pv, 2 * t + s + 1)
                    ctx_rows(2 * t + s + 2, s)
            with sp_.Fori(0, E // 2 - 1) as t:
                for s in range(2):
                    for which in range(2):
                        sp_.wait_ge(m_wl, 4 * t + 2 * s + 1 + which)
                        load_w(which, 2 * t + s + 2, s)
            for half in range(HALVES):
                w = slice(half * PPH, (half + 1) * PPH)
                sp_.wait_ge(f_out, half + 1)
                sp_.dma_start(out.rearrange("(i p) d -> p i d", p=PT)[:, w, :], x1[:, w, :]).then_inc(s_store, 16)
            sp_.wait_ge(s_store, 16 * HALVES)

        @block.tensor
        def _(pe):
            def project(c):
                for g in range(3):
                    for k in range(TAPS):
                        mm = pe.matmul(bank[:, 3 * c + g, 0:HW], w_conv[:, k, g * D:(g + 1) * D],
                                       xpad[:, HB * c:HB * (c + 1), k:k + L], start=(k == 0), stop=(k == TAPS - 1))
                    mm.then_inc(s_z, 1)

            pe.wait_ge(s_xT, 16)
            pe.wait_ge(s_convw, 1)
            project(0)
            project(1)
            for c in range(HALVES):
                pe.wait_ge(s_blk, 1)
                for n in range(2):
                    pe.wait_ge(s_sum, 3 * c + 1 + n)
                    if c and n == 0:
                        pe.wait_ge(s_zact, 3)
                    for m in range(M):
                        j = n * M + m
                        mm = pe.matmul(bank[:, Y_BANK[c], 0:HW], w_blk[:, j, :], sums[:, j * HW:(j + 1) * HW],
                                       start=(j == 0), stop=(j == 2 * M - 1))
                mm.then_inc(s_y, 1)
                for n in range(2):
                    pe.wait_ge(s_sq, 2 * c + 1 + n)
                    for m in range(M):
                        j = n * M + m
                        mm = pe.matmul(bank[:, SS_BANK[c], 0:HW], par("group_mask"),
                                       squares[:, j * HW:(j + 1) * HW], start=(j == 0), stop=(j == 2 * M - 1))
                mm.then_inc(s_ss, 1)
            for c in range(HALVES):
                pe.wait_ge(s_yg, c + 1)
                for j in range(PPH):
                    mm = pe.matmul(bank[0:PT, O_BANK[c], j * D:(j + 1) * D], y_gated[:, c, j * PT:(j + 1) * PT],
                                   par("w_out"), start=True, stop=True)
                mm.then_inc(s_o, 1)
            for c in range(HALVES):
                pe.wait_ge(s_x1, c + 1)
                for j in range(PPH):
                    mm = pe.transpose(bank[:, T_BANK[c], j * PT:(j + 1) * PT], x1[:, c * PPH + j, :],
                                      ident[0:PT, 0:PT])
                mm.then_inc(s_x1t, 1)

            def query(i):
                pe.matmul(bank[:, 7, 0:PT], par("w_q"), x1T[:, bass.ds(i * PT, PT)],
                          start=True, stop=True).then_inc(a_q, 1)

            def query_keys(i):
                pe.wait_ge(a_qsb, i + 1)
                pe.matmul(bank[0:DC + 1, 7, 128:128 + PT], par("w_k"), q_sb[:], start=True, stop=True).then_inc(a_qk, 1)

            def scores(i, s, turn):
                pe.wait_ge(a_qksb, i + 1)
                pe.wait_ge(s_ctxT[s], turn)
                for j, rows in ((0, GAP), (1, L)):
                    for n in range(SB):
                        mm = pe.matmul(bank[j * GAP:j * GAP + rows, n, 0:SN], qk_sb[:, j * L:j * L + rows],
                                       ctxT_slot[:, s, j, n * SN:(n + 1) * SN], start=True, stop=True)
                mm.then_inc(a_s, 1)

            def turn_weights(i):
                pe.wait_ge(a_exp, i + 1)
                for c in range(KC):
                    mm = pe.transpose(bank[0:KP, 3 + c // 4, (c % 4) * GT:(c % 4 + 1) * GT],
                                      exp_sb[:, c * KP:(c + 1) * KP], ident[0:GT, 0:GT])
                    if c % 4 == 3:
                        mm.then_inc(a_t, 1)

            def context_sum(i, s, turn, after_first):
                pe.wait_ge(a_et, 3 * i + 3)
                pe.wait_ge(s_ctx[s], turn)
                if after_first:
                    pe.wait_ge(a_res, i)
                for j, rows in ((0, GAP), (1, L)):
                    for c in range(KC):
                        mm = pe.matmul(bank[j * GAP:j * GAP + rows, 6, 0:DC + 1],
                                       expT_sb[:, c, j * GAP:j * GAP + rows], ctx_slot[:, s, j, c, :],
                                       start=(c == 0), stop=(c == KC - 1))
                mm.then_inc(a_pv, 1)

            def turn_sum(i):
                pe.wait_ge(a_u, i + 1)
                pe.transpose(bank[0:DC + 1, 7, 256:256 + GT], u_sb[:], ident[0:GT, 0:GT]).then_inc(a_ut, 1)

            def values(i):
                pe.wait_ge(a_utsb, i + 1)
                pe.matmul(bank[0:PT, 6, 128:128 + D + 1], uT_sb[:], w_v[:], start=True, stop=True).then_inc(a_r, 1)

            def turn_x2(i):
                pe.wait_ge(a_x2, i + 1)
                pe.transpose(bank[:, 7, 384:384 + PT], x2_now[:], ident[0:PT, 0:PT]).then_inc(a_x2t, 1)

            def attend_turn(i, s, ctx_now, ctxT_next, first=False, last=False):
                if not first:
                    context_sum(i - 1, 1 - s, ctx_now, True)
                if not first:
                    pe.wait_ge(a_x2T, i)
                if not last:
                    query(i + 1)
                turn_weights(i)
                if not first:
                    if not last:
                        pe.wait_ge(a_qsb, i + 2)
                    turn_sum(i - 1)
                if not last:
                    if not first:
                        pe.wait_ge(a_utsb, i)
                    query_keys(i + 1)
                if not first:
                    values(i - 1)
                if not last:
                    scores(i + 1, 1 - s, ctxT_next)
                if not first:
                    turn_x2(i - 1)

            pe.wait_ge(s_x1T, 2)
            pe.wait_ge(s_ones, 1)
            query(0)
            query_keys(0)
            scores(0, 0, 32)
            attend_turn(0, 0, None, 32, first=True)
            with pe.Fori(0, PAIRS // 2 - 1) as t:
                attend_turn(2 * t + 1, 1, 32 * t + 32, 32 * t + 64)
                attend_turn(2 * t + 2, 0, 32 * t + 32, 32 * t + 64)
            attend_turn(PAIRS - 1, 1, 16 * PAIRS, None, last=True)
            context_sum(PAIRS - 1, 1, 16 * PAIRS, True)
            pe.wait_ge(a_x2T, PAIRS)
            turn_sum(PAIRS - 1)
            values(PAIRS - 1)
            turn_x2(PAIRS - 1)

            def hidden(e, s, first=False):
                pe.wait_ge(m_wl, 2 * e + 1)
                for f in range(FC):
                    fs = slice(f * 128, (f + 1) * 128)
                    if not (first and f < 2):
                        pe.wait_ge(m_relu, 8 * e + 2 * f - 2)
                    for n, (w, x) in enumerate(((w1h, x2h), (w1h, x2l), (w1l, x2h))):
                        for c in range(HALVES):
                            mm = pe.matmul(bank[:, 2 * (f % 2) + c, 0:HW], w[:, s, fs],
                                           x[:, c * HW:(c + 1) * HW], start=(n == 0), stop=(n == 2))
                            if n == 2:
                                mm.then_inc(m_l1, 1)

            def outs(e, s):
                pe.wait_ge(m_wl, 2 * e + 2)
                pe.wait_ge(m_hl, 8 * e + 8)
                for half in range(HALVES):
                    pe.wait_ge(m_acc, 2 * e + 1 + half)
                    for j in range(PPH):
                        for f in range(FC):
                            for n, (h_, w_) in enumerate(((hh, w2h), (hh, w2l), (hl, w2h))):
                                mm = pe.matmul(bank[:, 4 + 2 * s + half, j * D:(j + 1) * D],
                                               h_[:, s, f, half * PPH + j, :], w_[:, s, f, :],
                                               start=(f == 0 and n == 0), stop=(f == FC - 1 and n == 2))
                    mm.then_inc(m_l2, 1)

            pe.wait_ge(a_x2T, PAIRS + 1)
            for i in range(PAIRS):
                mm = pe.matmul(bank[0:PT, 4, i * E:(i + 1) * E], x2T[:, i * PT:(i + 1) * PT], par("w_r"),
                               start=True, stop=True)
            mm.then_inc(m_log, 1)
            pe.wait_ge(a_x2s, 2 * PAIRS)
            hidden(0, 0, first=True)
            pe.wait_ge(m_rw, 1)
            for i in range(PAIRS):
                mm = pe.transpose(bank[0:E, 4 + i // PPH, (i % PPH) * PT:(i % PPH + 1) * PT], rw[:, i, :],
                                  ident[0:PT, 0:PT])
            mm.then_inc(m_rt, 1)
            pe.wait_ge(m_rwT, 1)
            for i in range(PAIRS):
                mm = pe.matmul(bank[0:PT, 6 + i // PPH, (i % PPH) * D:(i % PPH + 1) * D],
                               rwT[:, i * PT:(i + 1) * PT], par("b_2", E), start=True, stop=True)
            mm.then_inc(m_l2, 2)
            pe.wait_ge(m_pad, 2)
            with pe.Fori(0, E // 2 - 1) as t:
                for s in range(2):
                    hidden(2 * t + s + 1, 1 - s)
                    outs(2 * t + s, s)
            hidden(E - 1, 1)
            outs(E - 2, 0)
            outs(E - 1, 1)

        @block.scalar
        def _(act):
            own = Own(act, own_a)
            act.preload_act_table_set("natural_log_exp_and_others")
            act.wait_ge(s_sd, 1)
            nc.scalar.activation(sp[:, 1:2], sp[:, 0:1], ACT.Exp, scale=-1.0).then_inc(s_sp, 1)
            nc.scalar.activation(dsm[:, 4:7], dsm[:, 0:3], ACT.Exp).then_inc(s_sp, 1)
            act.wait_ge(s_sp, 1)
            act.wait_ge(s_cst, 1)
            nc.scalar.activation(sp[:, 2:3], sp[:, 1:2], ACT.Ln, bias=cst[:, C_ONE:C_ONE + 1]).then_inc(s_sp, 1)
            act.wait_ge(s_sd, 2)
            nc.scalar.activation(time_w[:], par("dist"), ACT.Exp, scale=sp[:, 3:4]).then_inc(s_sp, 1)
            act.wait_ge(s_in, 16)
            for c in range(HALVES):
                act.wait_ge(s_z, 3 * c + 1)
                nc.scalar.activation(xv[:, c, :], bank[:, 3 * c, 0:HW], ACT.Identity,
                                     bias=par("conv_b")[:, 0:1]).then_inc(s_zact, 1)
                act.wait_ge(s_z, 3 * c + 2)
                gr = own.mark(nc.scalar.activation(xg[:, c, :], bank[:, 3 * c + 1, 0:HW], ACT.Identity,
                                                   bias=par("conv_b")[:, 1:2]))
                act.wait_ge(s_z, 3 * c + 3)
                act.wait_ge(s_sd, 3)
                nc.scalar.activation(sc[:, c, :], bank[:, 3 * c + 2, 0:HW], ACT.Identity, bias=sbias[:],
                                     scale=par("score_scale")).then_inc(s_zact, 2)
                own.need(gr)
                nc.scalar.activation(gate[:, c, :], xg[:, c, :], ACT.Tanh, scale=0.5).then_inc(s_gate, 1)
                act.wait_ge(s_score, c + 1)
                nc.scalar.activation(sc[:, c, :], sc[:, c, :], ACT.Exp).then_inc(s_p, 1)

            def sines(c):
                act.wait_ge(s_phase, c + 1)
                if c:
                    act.wait_ge(s_sum, 3 * c - 2)
                a = own.mark(nc.scalar.activation(pc[:], ph[:], ACT.Abs))
                own.need(a)
                nc.scalar.activation(pc[:], pc[:], ACT.Sin, scale=-1.0,
                                     bias=cst[:, C_HALFPI:C_HALFPI + 1]).then_inc(s_trig, 1)
                nc.scalar.activation(ph[:], ph[:], ACT.Sin).then_inc(s_trig, 1)

            def square(c):
                for n in range(2):
                    act.wait_ge(s_sum, 3 * c + 1 + n)
                    if c:
                        act.wait_ge(s_ss, c)
                    w = slice(n * M * HW, (n + 1) * M * HW)
                    nc.scalar.activation(squares[:, w], sums[:, w], ACT.Square).then_inc(s_sq, 1)

            def factor(c):
                act.wait_ge(s_v, c + 1)
                a = own.mark(nc.scalar.activation(sc[:, c, :], sc[:, c, :], ACT.Ln, scale=2.0 ** -V_DOWN))
                own.need(a)
                nc.scalar.activation(sc[:, c, :], sc[:, c, :], ACT.Exp, scale=-0.5,
                                     bias=cst[:, C_FACTOR:C_FACTOR + 1]).then_inc(s_f, 1)

            def inv_std(own_, var, tmp, to, done):
                a = own_.mark(nc.scalar.activation(tmp, var, ACT.Ln, bias=cst[0:PT, C_EPS:C_EPS + 1]))
                own_.need(a)
                nc.scalar.activation(to, tmp, ACT.Exp, scale=-0.5).then_inc(done, 1)

            act.preload_act_table_set("trig_and_small")
            sines(0)
            square(0)
            sines(1)
            square(1)
            act.preload_act_table_set("natural_log_exp_and_others")
            factor(0)
            factor(1)
            for c in range(HALVES):
                w = slice(c * PPH, (c + 1) * PPH)
                act.wait_ge(s_var, c + 1)
                inv_std(own, mv[:, w, 1], lnv[:, w], rstd[:, w], s_rstd)
            for c in range(HALVES):
                act.wait_ge(s_x1t, c + 1)
                nc.scalar.copy(x1T[:, c * HW:(c + 1) * HW], bank[:, T_BANK[c], 0:HW]).then_inc(s_x1T, 1)

            loop = Own(act, loop_a)

            def queries(i):
                act.wait_ge(a_q, i + 1)
                nc.scalar.activation(q_sb[:], bank[:, 7, 0:PT], ACT.Identity, bias=qbias[:],
                                     scale=1.0 / sqrt(D)).then_inc(a_qsb, 1)

            def attend_turn(i, first=False, last=False):
                act.wait_ge(a_max, i + 1)
                nc.scalar.activation(exp_sb.rearrange("q (n k) -> q n k", n=SB), bank[0:GT, 0:SB, 0:SN], ACT.Exp,
                                     bias=neg_max[0:GT, :]).then_inc(a_exp, 1)
                if not last:
                    queries(i + 1)
                act.wait_ge(a_t, 3 * i + 1)
                nc.scalar.copy(expT_sb[:, 0:4, :], bank[0:KP, 3, 0:4 * GT].rearrange("p (c q) -> p c q", c=4)
                               ).then_inc(a_et, 1)
                if not first:
                    after_sum(i - 1)

            def after_sum(i):
                act.wait_ge(a_ut, i + 1)
                nc.scalar.copy(uT_sb[:].rearrange("d (j l) -> d j l", j=2),
                               bank[0:DC + 1, 7, 256:256 + 2 * GAP].rearrange("d (j l) -> d j l", j=2)[:, :, 0:L]
                               ).then_inc(a_utsb, 1)
                act.wait_ge(a_res, i + 1)
                inv_std(loop, mv[:, 0, 1:2], lnv[:, 0:1], rstd[:, 0:1], a_rstd)

            act.wait_ge(s_sd, 4)
            queries(0)
            attend_turn(0, first=True)
            with act.Fori(0, PAIRS // 2 - 1) as t:
                loop.turn(2 * t)
                attend_turn(2 * t + 1)
                attend_turn(2 * t + 2)
            loop.turn(PAIRS - 2)
            attend_turn(PAIRS - 1, last=True)
            after_sum(PAIRS - 1)

            def relu(e, s, first=False):
                nc.scalar.copy(b1_now[:, s, :], b1_at(e)).then_inc(m_b1, 1)
                for f in range(FC):
                    for c in range(HALVES):
                        g = 2 * f + c
                        if g == 0:
                            act.wait_ge(m_b1, e + 1)
                        act.wait_ge(m_l1, 8 * e + g + 1)
                        if g == 0 and not first:
                            act.wait_ge(m_l2, 2 * e)
                        nc.scalar.activation(hh[:, s, f, c * PPH:(c + 1) * PPH, 0:PT], bank[:, g % 4, 0:HW]
                                             .rearrange("p (j t) -> p j t", j=PPH), ACT.Relu, scale=1.0 / WS,
                                             bias=b1_now[:, s, f:f + 1])
                        if not (first and g < 4):
                            act.wait_ge(m_hl, 8 * e + g - 3)
                        nc.scalar.activation(hid[:, g % 4, :], bank[:, g % 4, 0:HW], ACT.Relu, scale=1.0 / WS,
                                             bias=b1_now[:, s, f:f + 1]).then_inc(m_relu, 1)

            def b1_at(e):
                a = at2["b_1"][0]
                return small_sb[:, bass.ds(a + FC * e, FC)]

            act.wait_ge(m_e, 1)
            nc.scalar.activation(tsm[:, 1, :], tsm[:, 0, :], ACT.Exp).then_inc(m_e, 1)
            relu(0, 0, first=True)
            act.wait_ge(m_rt, 1)
            nc.scalar.copy(rwT[:].rearrange("e (h t) -> e h t", h=2), bank[0:E, 4:6, 0:HW]).then_inc(m_rwT, 1)
            with act.Fori(0, E // 2 - 1) as t:
                for s in range(2):
                    relu(2 * t + s + 1, 1 - s)
            relu(E - 1, 1)
            for n in range(4):
                w = slice((n % 2) * PPH, (n % 2 + 1) * PPH)
                act.wait_ge(f_var, n + 1)
                inv_std(own, mv[:, w, 1], lnv[:, w], rstd[:, w], f_rstd)

        @block.vector
        def _(dve):
            own = Own(dve, own_v)
            V = nc.vector
            own.mark(V.memset(reset[:], 1.0))
            ones = own.mark(V.memset(w_v[:, D:D + 1], 0.0))
            V.memset(cst[:, C_EPS:C_EPS + 1], LN_EPS)
            V.memset(cst[:, C_HALFPI:C_HALFPI + 1], pi / 2)
            V.memset(cst[:, C_FACTOR:C_FACTOR + 1], -0.5 * V_DOWN * log(2.0) - log(2.0))
            V.memset(cst[:, C_ONE:C_ONE + 1], 1.0).then_inc(s_cst, 1)
            own.need(ones)
            own.mark(V.memset(reset[:].rearrange("p (n l) -> p n l", l=L)[:, :, 0:1], 0.0))
            own.mark(V.memset(w_v[DC:DC + 1, D:D + 1], 1.0))
            dve.wait_ge(s_in, 16)
            dve.wait_ge(s_cw, 16)
            V.tensor_tensor(w_conv[:], par("w_in").unsqueeze(1).broadcast_to([128, TAPS, 3 * D]), convw_sb[:],
                            ALU.mult).then_inc(s_convw, 1)
            dve.wait_ge(s_par, 16)
            own.mark(V.scalar_tensor_tensor(sp[:, 0:1], par("slope"), -1.0, par("slope"), ALU.mult, ALU.max))
            a = own.mark(V.tensor_reduce(dsm[:, 3:4], par("deriv"), AX.X, ALU.max))
            own.need(a)
            V.tensor_scalar(dsm[:, 0:3], par("deriv"), dsm[:, 3:4], None, ALU.subtract).then_inc(s_sd, 1)
            own.mark(V.tensor_scalar(theta_t[:], par("theta"), 1.0 / (2 * pi), None, ALU.mult))
            dve.wait_ge(s_sp, 3)
            a = own.mark(V.scalar_tensor_tensor(sp[:, 3:4], par("slope"), 0.0, sp[:, 2:3], ALU.max, ALU.add))
            own.need(a)
            V.tensor_scalar(sp[:, 3:4], sp[:, 3:4], -1.0, None, ALU.mult).then_inc(s_sd, 1)
            V.tensor_tensor(sbias[:], par("conv_b")[:, 2:3], par("score_scale"), ALU.mult).then_inc(s_sd, 1)
            V.tensor_scalar(qbias[:], par("b_q"), 1.0 / sqrt(D), None, ALU.mult).then_inc(s_sd, 1)
            a = own.mark(V.tensor_reduce(dsm[:, 7:8], dsm[:, 4:7], AX.X, ALU.add))
            own.need(a)
            a = own.mark(V.reciprocal(dsm[:, 7:8], dsm[:, 7:8]))
            own.need(a)
            a = own.mark(V.tensor_scalar(dsm[:, 8:11], dsm[:, 4:7], dsm[:, 7:8], None, ALU.mult))
            own.need(a)
            a = own.mark(V.tensor_scalar(dsm[:, 11:12], dsm[:, 10:11], -1.0, None, ALU.mult))
            a = own.mark(V.tensor_copy(w_v[:, 0:D], par("w_v", DC + 1)))
            a = own.mark(V.tensor_tensor(w_rin[:], par("w_ri").rearrange("p (j h) -> p j h", j=2 * M),
                                         par("norm_scale").unsqueeze(2).broadcast_to([128, 2 * M, H]), ALU.mult))
            own.need(a)
            for j in range(2 * M):
                ins = V.tensor_tensor(w_blk[:, j, :].rearrange("p (k h) -> p k h", k=K),
                                      w_rin[:, j, :].unsqueeze(1).broadcast_to([128, K, H]),
                                      par("group_mask").rearrange("p (k h) -> p k h", k=K), ALU.mult)
            ins.then_inc(s_blk, 1)

            W = M * HW

            def gates(c):
                dve.wait_ge(s_zact, 3 * c + 3)
                V.tensor_scalar(sc[:, c, :], sc[:, c, :], 20.0, -20.0, ALU.min, ALU.max).then_inc(s_score, 1)
                dve.wait_ge(s_gate, c + 1)
                own.mark(V.scalar_tensor_tensor(gate[:, c, :], gate[:, c, :], 1.0, xg[:, c, :], ALU.add, ALU.mult))

            def weights(c):
                pw = terms[:, 2 * W:2 * W + HW]
                a = own.mark(V.tensor_scalar(q0[:], xv[:, c, :], dsm[:, 11:12], dsm[:, 9:10], ALU.mult, ALU.add))
                own.need(a)
                a = own.mark(V.tensor_tensor(q0[:], q0[:], xv[:, c, :], ALU.mult))
                dve.wait_ge(s_p, c + 1)
                dve.wait_ge(s_sp, 4)
                b = own.mark(V.tensor_tensor(pw.rearrange("p (b l) -> p b l", b=HB),
                                             sc[:, c, :].rearrange("p (b l) -> p b l", b=HB),
                                             time_w[:].unsqueeze(1).broadcast_to([128, HB, L]), ALU.mult))
                own.need(b)
                V.scalar_tensor_tensor(q0[:], q0[:], dsm[:, 8:9], pw, ALU.add, ALU.mult).then_inc(s_poly, 1)

            def phases(c):
                dve.wait_ge(s_turns, c + 1)
                for m in range(M):
                    a = own.mark(V.scalar_tensor_tensor(ph[:, m, :], xv[:, c, :], par("theta")[:, m:m + 1],
                                                        ph[:, m, :], ALU.mult, ALU.subtract))
                own.need(a)
                V.tensor_scalar(ph[:], ph[:], 3.1415925, -3.1415925, ALU.min, ALU.max).then_inc(s_phase, 1)

            def run_sums(c):
                dve.wait_ge(s_trig, 2 * c + 1)
                a = own.mark(V.tensor_tensor(terms[:, 0:W].rearrange("p (m w) -> p m w", m=M), pc[:],
                                             q0[:].unsqueeze(1).broadcast_to([128, M, HW]), ALU.mult))
                own.need(a)
                if c:
                    dve.wait_ge(s_y, c)
                    dve.wait_ge(s_sq, 2 * c)
                V.tensor_tensor_scan(sums[:, 0:W], reset[:], terms[:, 0:W], 0.0, ALU.mult, ALU.add).then_inc(s_sum, 1)
                b = own.mark(V.tensor_tensor_scan(sums[:, 2 * W:2 * W + HW], reset[:, 0:HW],
                                                  terms[:, 2 * W:2 * W + HW], 0.0, ALU.mult, ALU.add))
                dve.wait_ge(s_im, c + 1)
                V.tensor_tensor_scan(sums[:, W:2 * W], reset[:], terms[:, W:2 * W], 0.0, ALU.mult,
                                     ALU.add).then_inc(s_sum, 2)
                own.need(b)
                a = own.mark(V.tensor_scalar(sc[:, c, :], sums[:, 2 * W:2 * W + HW], 1e-4, sqrt(LN_EPS),
                                             ALU.max, ALU.mult))
                own.need(a)
                return own.mark(V.tensor_tensor(sc[:, c, :], sc[:, c, :], sc[:, c, :], ALU.mult))

            def split(which, e, s, turn, own_):
                raw = w_raw[:, s, which, :]
                high, low = ((w1h[:, s, :], w1l[:, s, :]),
                             (w2h[:, s].rearrange("p f d -> p (f d)"), w2l[:, s].rearrange("p f d -> p (f d)")))[which]
                dve.wait_ge(s_w[2 * which + s], turn)
                a = own_.mark(V.tensor_scalar(high, raw, WS, None, ALU.mult))
                own_.need(a)
                V.scalar_tensor_tensor(low, raw, WS, high, ALU.mult, ALU.subtract).then_inc(m_wl, 1)

            gates(0)
            gates(1)
            weights(0)
            phases(0)
            dens = [run_sums(0)]
            weights(1)
            phases(1)
            dens.append(run_sums(1))
            split(0, 0, 0, 16, own)
            split(1, 0, 0, 16, own)
            split(0, 1, 1, 16, own)
            for c in range(HALVES):
                dve.wait_ge(s_ss, c + 1)
                own.need(dens[c])
                V.scalar_tensor_tensor(sc[:, c, :], bank[:, SS_BANK[c], 0:HW], 1.0 / (2 * H * M), sc[:, c, :],
                                       ALU.mult, ALU.add).then_inc(s_v, 1)
            for c in range(HALVES):
                dve.wait_ge(s_f, c + 1)
                a = own.mark(V.tensor_tensor(gate[:, c, :], gate[:, c, :], sc[:, c, :], ALU.mult))
                own.need(a)
                V.tensor_tensor(y_gated[:, c, :], bank[:, Y_BANK[c], 0:HW], gate[:, c, :], ALU.mult).then_inc(s_yg, 1)
            dve.wait_ge(s_xtok, 16)
            for c in range(HALVES):
                w = slice(c * PPH, (c + 1) * PPH)
                dve.wait_ge(s_o, c + 1)
                a = own.mark(V.tensor_tensor(x1[:, w, :], bank[0:PT, O_BANK[c], 0:PPH * D]
                                             .rearrange("p (j d) -> p j d", j=PPH), xtok[:, w, :], ALU.add))
                own.need(a)
                for j in range(c * PPH, (c + 1) * PPH):
                    a = own.mark(V.bn_stats(stat[:, j, :], x1[:, j, :]))
                own.need(a)
                for j in range(c * PPH, (c + 1) * PPH):
                    ins = V.bn_aggr(mv[:, j, :], stat[:, j, :])
                ins.then_inc(s_var, 1)
            for c in range(HALVES):
                dve.wait_ge(s_rstd, c + 1)
                for j in range(c * PPH, (c + 1) * PPH):
                    ins = V.tensor_scalar(x1[:, j, :], x1[:, j, :], mv[:, j, 0:1], rstd[:, j:j + 1],
                                          ALU.subtract, ALU.mult)
                ins.then_inc(s_x1, 1)

            V.memset(carrier[:], 0.0).then_inc(a_x2T, 1)
            loop = Own(dve, loop_v)

            def query_keys(i):
                dve.wait_ge(a_qk, i + 1)
                V.tensor_copy(qk_sb[:], bank[0:DC + 1, 7, 128:128 + PT]).then_inc(a_qksb, 1)

            def maximum(i):
                dve.wait_ge(a_s, i + 1)
                V.tensor_reduce(neg_max[0:GT, :], bank[0:GT, 0:SB, 0:SN], AX.XY, ALU.max,
                                negate=True).then_inc(a_max, 1)

            def x2T_copy(i):
                dve.wait_ge(a_x2t, i + 1)
                V.tensor_copy(x2T[:, bass.ds(i * PT, PT)], bank[:, 7, 384:384 + PT]).then_inc(a_x2T, 1)

            def sum_copy(i):
                dve.wait_ge(a_pv, i + 1)
                V.tensor_copy(u_sb[:], bank[0:GT, 6, 0:DC + 1]).then_inc(a_u, 1)

            def turned_copy(i):
                for n in (1, 2):
                    dve.wait_ge(a_t, 3 * i + n + 1)
                    V.tensor_copy(expT_sb[:, 4 * n:4 * n + 4, :], bank[0:KP, 3 + n, 0:4 * GT]
                                  .rearrange("p (c q) -> p c q", c=4)).then_inc(a_et, 1)

            def attended(i, second):
                dve.wait_ge(a_r, i + 1)
                a = loop.mark(V.reciprocal(rden[:], bank[0:PT, 6, 128 + D:128 + D + 1]))
                loop.need(a)
                a = loop.mark(V.scalar_tensor_tensor(res[:], bank[0:PT, 6, 128:128 + D], rden[:, 0:1],
                                                     x1[:, bass.ds(i, 1), :].rearrange("p i d -> p (i d)"),
                                                     ALU.mult, ALU.add))
                loop.need(a)
                a = loop.mark(V.bn_stats(stat[:, 0, :], res[:]))
                loop.need(a)
                V.tensor_copy(carrier[:, 0:1], cst[:, 0:1])
                V.bn_aggr(mv[:, 0, :], stat[:, 0, :]).then_inc(a_res, 1)
                dve.wait_ge(a_rstd, i + 1)
                if second:
                    dve.wait_ge(a_x2s, 2 * i - 1)
                V.tensor_scalar(x2_now[:], res[:], mv[:, 0, 0:1], rstd[:, 0:1], ALU.subtract,
                                ALU.mult).then_inc(a_x2, 1)

            def attend_turn(i, first=False, second=False, last=False):
                maximum(i)
                if not first and not second:
                    x2T_copy(i - 2)
                if not first:
                    sum_copy(i - 1)
                turned_copy(i)
                if not last:
                    query_keys(i + 1)
                if not first:
                    attended(i - 1, not second)

            query_keys(0)
            attend_turn(0, first=True)
            attend_turn(1, second=True)
            with dve.Fori(1, PAIRS // 2 - 1) as t:
                loop.turn(6 * t - 3)
                attend_turn(2 * t)
                attend_turn(2 * t + 1)
            loop.turn(3 * (PAIRS - 3))
            attend_turn(PAIRS - 2)
            attend_turn(PAIRS - 1, last=True)
            x2T_copy(PAIRS - 2)
            sum_copy(PAIRS - 1)
            attended(PAIRS - 1, True)
            x2T_copy(PAIRS - 1)

            def hidden_low(e, s):
                for f in range(FC):
                    for c in range(HALVES):
                        g = 2 * f + c
                        dve.wait_ge(m_relu, 8 * e + g + 1)
                        w = slice(c * PPH, (c + 1) * PPH)
                        V.tensor_tensor(hl[:, s, f, w, 0:PT], hid[:, g % 4, :].rearrange("p (j t) -> p j t", j=PPH),
                                        hh[:, s, f, w, 0:PT], ALU.subtract).then_inc(m_hl, 1)

            def add_outs(e, s):
                for half in range(HALVES):
                    dve.wait_ge(m_l2, 2 * e + half + 3)
                    dve.wait_ge(m_acc, 2 * e + half + 3)
                    for j in range(PPH):
                        i = half * PPH + j
                        wt = rws[:, i, bass.ds(e, 1)]
                        ins = V.scalar_tensor_tensor(acc[:, i, :], bank[0:PT, 4 + 2 * s + half, j * D:(j + 1) * D],
                                                     wt, acc[:, i, :], ALU.mult, ALU.add)
                    ins.then_inc(m_acc, 1)

            weight_own = Own(dve, mo_v)
            dve.wait_ge(m_log, 1)
            a = own.mark(V.tensor_tensor(logit[:], bank[0:PT, 4, 0:PAIRS * E].rearrange("p (i e) -> p i e", i=PAIRS),
                                         par("b_r", PT).unsqueeze(1).broadcast_to([PT, PAIRS, E]), ALU.add))
            own.need(a)
            for i in range(PAIRS):
                a = own.mark(V.max(top[:, i, :], logit[:, i, :]))
            own.need(a)
            for i in range(PAIRS):
                b = own.mark(V.max_index(topi[:, i, :], top[:, i, :], logit[:, i, :]))
            V.tensor_tensor(tsm[:, 0, :], top[:, :, 1], top[:, :, 0], ALU.subtract).then_inc(m_e, 1)
            own.need(b)
            a = own.mark(V.tensor_copy(topf[:], topi[:, :, 0:2]))
            dve.wait_ge(m_e, 2)
            a = own.mark(V.tensor_scalar(tsm[:, 2, :], tsm[:, 1, :], 1.0, None, ALU.add))
            own.need(a)
            a = own.mark(V.reciprocal(tsm[:, 3, :], tsm[:, 2, :]))
            own.need(a)
            a = own.mark(V.tensor_tensor(tsm[:, 4, :], tsm[:, 1, :], tsm[:, 3, :], ALU.mult))
            iota = par("iota", PT).unsqueeze(1).broadcast_to([PT, PAIRS, E])

            def spread(x):
                return x.unsqueeze(2).broadcast_to([PT, PAIRS, E])

            own.mark(V.tensor_tensor(rw[:], iota, spread(topf[:, :, 0]), ALU.is_equal))
            b = own.mark(V.tensor_tensor(rws[:], iota, spread(topf[:, :, 1]), ALU.is_equal))
            own.need(b)
            own.mark(V.tensor_tensor(rw[:], rw[:], spread(tsm[:, 3, :]), ALU.mult))
            b = own.mark(V.tensor_tensor(rws[:], rws[:], spread(tsm[:, 4, :]), ALU.mult))
            own.need(b)
            a = own.mark(V.tensor_tensor(rw[:], rw[:], rws[:], ALU.add))
            own.need(a)
            V.tensor_scalar(rws[:], rw[:], 1.0 / WS, None, ALU.mult).then_inc(m_rw, 1)
            hidden_low(0, 0)
            dve.wait_ge(m_l2, 2)
            for half in range(HALVES):
                w = slice(half * PPH, (half + 1) * PPH)
                ins = V.tensor_tensor(acc[:, w, :], bank[0:PT, 6 + half, :].rearrange("p (j d) -> p j d", j=PPH),
                                      x2[:, w, :], ALU.add)
            ins.then_inc(m_acc, 4)
            with dve.Fori(0, E // 2 - 1) as t:
                for s in range(2):
                    e = 2 * t + s
                    if s == 0:
                        weight_own.turn(4 * t)
                    dve.wait_ge(m_l2, 2 * e + 2)
                    split(1, e + 1, 1 - s, 16 * t + 16 * (1 + s), weight_own)
                    dve.wait_ge(m_l1, 8 * e + 8)
                    split(0, e + 2, s, 16 * t + 32, weight_own)
                    hidden_low(e + 1, 1 - s)
                    add_outs(e, s)
            dve.wait_ge(m_l2, 2 * (E - 2) + 2)
            weight_own.turn(4 * (E // 2 - 1))
            split(1, E - 1, 1, 16 * (E // 2), weight_own)
            hidden_low(E - 1, 1)
            add_outs(E - 2, 0)
            add_outs(E - 1, 1)
            for n in range(2):
                for half in range(HALVES):
                    if n == 0:
                        dve.wait_ge(m_acc, 2 * E + 3 + half)
                    for j in range(half * PPH, (half + 1) * PPH):
                        a = own.mark(V.bn_stats(stat[:, j, :], acc[:, j, :]))
                    own.need(a)
                    for j in range(half * PPH, (half + 1) * PPH):
                        ins = V.bn_aggr(mv[:, j, :], stat[:, j, :])
                    ins.then_inc(f_var, 1)
                for half in range(HALVES):
                    w = slice(half * PPH, (half + 1) * PPH)
                    dve.wait_ge(f_rstd, 2 * n + half + 1)
                    to = (acc, x1)[n]
                    for j in range(half * PPH, (half + 1) * PPH):
                        ins = V.tensor_scalar(to[:, j, :], acc[:, j, :], mv[:, j, 0:1], rstd[:, j:j + 1],
                                              ALU.subtract, ALU.mult)
                    if n:
                        ins.then_inc(f_out, 1)
                        continue
                    a = own.mark(ins)
                    own.need(a)
                    a = own.mark(V.tensor_tensor(acc[:, w, :], acc[:, w, :], par("gamma", PT).unsqueeze(1)
                                                 .broadcast_to([PT, PPH, D]), ALU.mult))
                    own.need(a)
                    if half == 0:
                        dve.wait_ge(m_x2b, 1)
                    a = own.mark(V.tensor_tensor(acc[:, w, :], acc[:, w, :], x2b[:, w, :], ALU.add))
                    own.need(a)

        @block.gpsimd
        def _(pool):
            own = Own(pool, own_g)
            G = nc.gpsimd
            G.memset(xpad[:, :, 0:TAPS - 1], 0.0).then_inc(s_zero, 1)
            for s in range(2):
                a = own.mark(G.memset(ctx_slot[:, s, :, :, DC:DC + 1], 1.0))
            own.need(a)
            G.memset(ctxT_slot[DC:DC + 1], 1.0).then_inc(s_ones, 1)
            pool.wait_ge(s_ones, 1)
            pool.wait_ge(s_cst, 1)
            for c in range(HALVES):
                pool.wait_ge(s_zact, 3 * c + 1)
                pool.wait_ge(s_sd, 2)
                if c:
                    pool.wait_ge(s_im, c)
                for m in range(M):
                    a = own.mark(G.tensor_scalar(ph[:, m, :], xv[:, c, :], theta_t[:, m:m + 1], MAGIC,
                                                 ALU.mult, ALU.add))
                own.need(a)
                G.tensor_scalar(ph[:], ph[:], -MAGIC, 2 * pi, ALU.add, ALU.mult).then_inc(s_turns, 1)
                pool.wait_ge(s_trig, 2 * c + 2)
                pool.wait_ge(s_poly, c + 1)
                if c:
                    pool.wait_ge(s_sum, 3 * c)
                W = M * HW
                ins = G.tensor_tensor(terms[:, W:2 * W].rearrange("p (m w) -> p m w", m=M), ph[:],
                                      q0[:].unsqueeze(1).broadcast_to([128, M, HW]), ALU.mult)
                ins.then_inc(s_im, 1)

            loop = Own(pool, loop_g)

            def keep(i):
                pool.wait_ge(a_x2, i + 1)
                G.tensor_copy(x2[:, bass.ds(i, 1), :].rearrange("p i d -> p (i d)"), x2_now[:]).then_inc(a_x2s, 1)
                pool.wait_ge(a_x2T, i + 2)
                xs = bass.ds(i * PT, PT)
                a = loop.mark(G.tensor_copy(x2h[:, xs], x2T[:, xs]))
                loop.need(a)
                G.tensor_tensor(x2l[:, xs], x2T[:, xs], x2h[:, xs], ALU.subtract).then_inc(a_x2s, 1)

            with pool.Fori(0, PAIRS) as i:
                loop.turn(i)
                keep(i)

            pool.wait_ge(a_x2s, 2 * PAIRS)
            G.tensor_tensor(x2b[:], x2[:], par("beta", PT).unsqueeze(1).broadcast_to([PT, PAIRS, D]),
                            ALU.add).then_inc(m_x2b, 1)
            for x in (hh, hl):
                G.memset(x.rearrange("p s f j t -> p (s f j) t")[:, :, PT:HT], 0.0).then_inc(m_pad, 1)

    return nc


def kernel(x, ctx_768, L0_attn_in_proj_w, L0_attn_conv_w, L0_attn_conv_b, L0_attn_theta, L0_attn_decay_slopes,
           L0_attn_anchor_slopes, L0_attn_score_scale, L0_attn_deriv_logits, L0_attn_norm_scale, L0_attn_W_re,
           L0_attn_W_im, L0_attn_out_proj_w, L0_xattn_Wq, L0_xattn_bq, L0_xattn_Wk, L0_xattn_bk, L0_xattn_Wv,
           L0_xattn_bv, L0_ffn_Wr, L0_ffn_br, L0_ffn_W1, L0_ffn_b1, L0_ffn_W2, L0_ffn_b2, L0_ffn_gamma,
           L0_ffn_beta):
    import concourse.bacc as bacc
    from concourse.bass_utils import run_bass_kernel_spmd

    def f32(a):
        return np.asarray(a)

    def rows(a):
        return np.broadcast_to(f32(a).reshape(1, -1), (128, f32(a).size))

    def pad(a):
        a = f32(a)
        return np.concatenate([a, np.zeros((128 - a.shape[0], a.shape[1]), a.dtype)])

    x = f32(x)
    w_in, cw, cb = f32(L0_attn_in_proj_w), f32(L0_attn_conv_w).reshape(TAPS, -1), f32(L0_attn_conv_b).reshape(1, -1)
    w_in, cw, cb = (np.concatenate([a[:, :2 * D], np.repeat(a[:, 2 * D:], H, axis=1)], axis=1) for a in (w_in, cw, cb))
    group = np.arange(128) // H
    pos = np.arange(L)
    dist = np.where((np.arange(128) < H * (K - 4))[:, None], (L - 1 - pos)[None], pos[None]).astype(np.float32)
    w_ri = np.concatenate([f32(L0_attn_W_re).reshape(H, M, H), f32(L0_attn_W_im).reshape(H, M, H)], axis=1)
    ns = f32(L0_attn_norm_scale).reshape(2, H, M).transpose(1, 0, 2).reshape(H, 2 * M)
    small = {
        "theta": f32(L0_attn_theta).reshape(128, M),
        "slope": np.repeat(np.concatenate([f32(L0_attn_decay_slopes), f32(L0_attn_anchor_slopes)]), H)[:, None],
        "dist": dist,
        "score_scale": np.repeat(f32(L0_attn_score_scale), H)[:, None],
        "deriv": rows(L0_attn_deriv_logits),
        "norm_scale": np.tile(ns, (K, 1)),
        "w_ri": np.tile(w_ri.reshape(H, 2 * M * H), (K, 1)),
        "group_mask": (group[:, None] == group[None]).astype(np.float32),
        "ident": np.eye(128, dtype=np.float32),
        "w_out": f32(L0_attn_out_proj_w),
        "w_q": f32(L0_xattn_Wq),
        "b_q": f32(L0_xattn_bq)[:, None],
        "w_k": np.concatenate([f32(L0_xattn_Wk), f32(L0_xattn_bk)[None]]).T,
        "w_v": pad(np.concatenate([f32(L0_xattn_Wv), f32(L0_xattn_bv)[None]])),
        "w_r": f32(L0_ffn_Wr).T,
        "b_r": rows(L0_ffn_br),
        "gamma": rows(L0_ffn_gamma),
        "beta": rows(L0_ffn_beta),
        "b_1": f32(L0_ffn_b1).reshape(E * FC, 128).T,
        "b_2": pad(L0_ffn_b2),
        "iota": rows(np.arange(E, dtype=np.float32)),
    }
    ctx = f32(ctx_768)
    arrays = {
        "x_T": x.reshape(T, D).T,
        "x_tok": x.reshape(T, D),
        "ctx": ctx.reshape(B, KP, KC, DC),
        "ctx_T": ctx.reshape(B, KP, KC, DC).transpose(0, 3, 2, 1).reshape(B, DC, SK),
        "first": np.concatenate([w_in, cb.reshape(3, 128).T], axis=1),
        "conv_w": cw.reshape(-1),
        "small": np.concatenate([small[name] for name, _ in SMALL], axis=1),
        "w_1": f32(L0_ffn_W1).transpose(0, 2, 1),
        "w_2": f32(L0_ffn_W2).reshape(E, D, FC, 128).transpose(0, 3, 2, 1).reshape(E, 128, FC * D),
    }
    arrays = {name: np.ascontiguousarray(a) for name, a in arrays.items()}
    nc = bacc.Bacc("TRN2", target_bir_lowering=False, num_devices=1)
    args = [nc.dram_tensor(name, a.shape, mybir.dt.from_np(a.dtype), kind="ExternalInput").ap()
            for name, a in arrays.items()]
    out = nc.dram_tensor("out", (T, D), F32, kind="ExternalOutput").ap()
    decoder_kernel(nc, *args, out)
    ran = run_bass_kernel_spmd(nc, [arrays], core_ids=[0])
    return ran.results[0]["out"].reshape(B, L, D)
```

```python
from contextlib import ExitStack
from math import log, pi, sqrt

import numpy as np

import concourse.bass as bass
from concourse import mybir

ALU = mybir.AluOpType
ACT = mybir.ActivationFunctionType
AX = mybir.AxisListType
F32 = mybir.dt.float32
F16 = mybir.dt.float16
U32 = mybir.dt.uint32

B, L, D = 16, 56, 128
K, H, M = 32, 4, 4
TAPS = 4
SK, DC = 1500, 96
E, F = 8, 512
T = B * L
HALVES = 2
HB = B // HALVES
HW = HB * L
PAIRS = B // 2
PT = 2 * L
PPH = PAIRS // HALVES
GAP = 64
GT = GAP + L
KP, KC = 125, 12
SN = 500
SB = SK // SN
FC = F // 128
HT = 128
WS = 16.0
MAGIC = 1.5 * 2.0 ** 23
LN_EPS = 1e-5
V_DOWN = 20

FIRST = [("w_in", 3 * D), ("conv_b", 3), ("theta", M), ("slope", 1), ("dist", L), ("score_scale", 1), ("deriv", 3)]
SMALL = [("norm_scale", 2 * M), ("w_ri", 2 * M * H), ("group_mask", D), ("ident", D), ("w_out", D), ("w_q", D), ("b_q", 1),
         ("w_k", DC + 1), ("w_v", D), ("w_r", E), ("b_r", E), ("gamma", D), ("beta", D), ("b_1", E * FC),
         ("b_2", D), ("iota", E)]


def places(names):
    at, n = {}, 0
    for name, width in names:
        at[name] = (n, n + width)
        n += width
    return at, n


class Own:

    def __init__(self, eng, sem):
        self.eng, self.sem, self.base, self.n = eng, sem, 0, 0

    def turn(self, base):
        self.base, self.n = base, 0

    def mark(self, ins):
        ins.then_inc(self.sem, 1)
        self.n += 1
        return self.base + self.n

    def need(self, value):
        self.eng.wait_ge(self.sem, value)


def decoder_kernel(nc, x_T, x_tok, ctx, ctx_T, first, conv_w, small, w_1, w_2, out):
    with ExitStack() as stack:
        def sb(name, shape, dt=F32):
            return stack.enter_context(nc.sbuf_tensor(name, shape, dt))

        def sem(name):
            return stack.enter_context(nc.semaphore(name))

        bank = stack.enter_context(nc.psum_tensor("bank", [128, 8, 512], F32))

        at1, n1 = places(FIRST)
        at2, n2 = places(SMALL)
        first_sb = sb("first_sb", [128, n1])
        small_sb = sb("small_sb", [128, n2])
        convw_sb = sb("convw_sb", [128, 3, TAPS, D])

        def par(name, rows=128):
            a, b = at1[name] if name in at1 else at2[name]
            return (first_sb if name in at1 else small_sb)[0:rows, a:b]

        ident = par("ident")
        w_conv = sb("w_conv", [128, 3, TAPS, D])
        w_blk = sb("w_blk", [128, 2 * M, D])
        w_rin = sb("w_rin", [128, 2 * M, H])
        time_w = sb("time_w", [128, L])
        reset = sb("reset", [128, M * HW])
        cst = sb("cst", [128, 4])
        sp = sb("sp", [128, 4])
        dsm = sb("dsm", [128, 12])
        theta_t = sb("theta_t", [128, M])
        sbias = sb("sbias", [128, 1])
        qbias = sb("qbias", [128, 1])

        xpad = sb("xpad", [128, B, L + TAPS - 1])
        xtok = sb("xtok", [PT, PAIRS, D])
        x1 = sb("x1", [PT, PAIRS, D])
        x1T = sb("x1T", [128, T])
        rows_late = sb("rows_late", [128, 2 * PAIRS * D])
        x2 = rows_late[0:PT, 0:PAIRS * D].rearrange("p (i d) -> p i d", i=PAIRS)
        x2b = rows_late[0:PT, PAIRS * D:].rearrange("p (i d) -> p i d", i=PAIRS)
        turned_late = sb("turned_late", [128, 2 * T])
        x2T = turned_late[:, 0:T]
        x2h = turned_late[:, T:T + T // 2].bitcast(F16)
        x2l = turned_late[:, T + T // 2:].bitcast(F16)

        xv = sb("xv", [128, HALVES, HW])
        xg = sb("xg", [128, HALVES, HW])
        sc = sb("sc", [128, HALVES, HW])
        gate = sb("gate", [128, HALVES, HW])
        ph_0 = sb("ph_0", [128, M, HW])
        pc_0 = sb("pc_0", [128, M, HW])
        ph = [ph_0[:], turned_late[:, 0:M * HW].rearrange("p (m w) -> p m w", m=M)]
        pc = [pc_0[:], rows_late[:, 0:M * HW].rearrange("p (m w) -> p m w", m=M)]
        work = max((2 * M + 1) * HW, FC * PAIRS * HT)
        terms = sb("terms", [128, work])
        sums = sb("sums", [128, work])
        squares = sb("squares", [128, 2 * M * HW])
        y_gated = sb("y_gated", [128, HALVES, HW])
        poly = [sb("poly_0", [128, HW])[:], y_gated[:, 1, :]]

        ctx_slot = sb("ctx_slot", [KP, 2, 2, KC, DC])
        ctxT_slot = sb("ctxT_slot", [DC + 1, 2, 2, SK])
        q_sb = sb("q_sb", [128, PT])
        qk_sb = sb("qk_sb", [DC + 1, PT])
        neg_max = sb("neg_max", [128, 1])
        u_sb = sb("u_sb", [GT, DC + 1])
        uT_sb = sb("uT_sb", [DC + 1, PT])
        den = sb("den", [GT, 2])
        rden = sb("rden", [GT, 2])
        res = sb("res", [PT, D])
        x2_now = sb("x2_now", [PT, D])
        stat = sb("stat", [PT, PAIRS, 6])
        mv = sb("mv", [PT, PAIRS, 2])
        lnv = sb("lnv", [PT, PAIRS])
        rstd = sb("rstd", [PT, PAIRS])
        exp_sb = [squares[0:GT, s * SK:(s + 1) * SK] for s in range(2)]
        expT_sb = ph_0[0:KP].rearrange("p m w -> p (m w)")[:, 0:KC * GT].rearrange("p (c q) -> p c q", c=KC)

        w_raw = sb("w_raw", [128, 2, 2, F])
        w1h = sb("w1h", [128, 2, F], F16)
        w1l = sb("w1l", [128, 2, F], F16)
        w2h = sb("w2h", [128, 2, FC, D], F16)
        w2l = sb("w2l", [128, 2, FC, D], F16)
        hid = pc_0[:]
        nh = 2 * FC * PAIRS * HT
        hh = terms[:, 0:nh // 2].bitcast(F16).rearrange("p (s f j t) -> p s f j t", s=2, f=FC, j=PAIRS)
        hl = sums[:, 0:nh // 2].bitcast(F16).rearrange("p (s f j t) -> p s f j t", s=2, f=FC, j=PAIRS)
        carrier = sb("carrier", [128, 1])
        b1_now = sb("b1_now", [128, 2, FC])
        logit = sb("logit", [PT, PAIRS, E])
        top = sb("top", [PT, PAIRS, 8])
        topi = sb("topi", [PT, PAIRS, 8], U32)
        topf = sb("topf", [PT, PAIRS, 2])
        tsm = sb("tsm", [PT, 6, PAIRS])
        rw = sb("rw", [PT, PAIRS, E])
        rws = sb("rws", [PT, PAIRS, E])
        rwT = sb("rwT", [E, T])
        nmr = sb("nmr", [PT, PAIRS])
        rstd2 = sb("rstd2", [PT, PAIRS])
        acc = xtok

        s_in = sem("first_params_loaded")
        s_cw = [sem(f"conv_weights_loaded_{g}") for g in range(3)]
        s_xT = [sem(f"x_transposed_loaded_{c}") for c in range(HALVES)]
        s_par = sem("small_params_loaded")
        s_xtok = sem("x_tokens_loaded")
        s_ctx = [sem(f"ctx_loaded_{s}") for s in range(2)]
        s_ctxT = [sem(f"ctxT_loaded_{s}") for s in range(2)]
        s_w = [sem(f"expert_weights_loaded_{s}") for s in range(4)]
        s_cst = sem("constants_set")
        s_ones = sem("context_ones_set")
        s_convw = sem("conv_folded")
        s_z = sem("z_done")
        s_xv = sem("values_read")
        s_sc = sem("scores_read")
        s_warm = sem("ones_for_warming")
        s_score = sem("score_clipped")
        s_p = sem("score_exp")
        s_sp = sem("small_act")
        s_sd = sem("small_dve")
        s_gate = sem("gate_read")
        s_phase = sem("phase_reduced")
        s_trig = sem("sines_done")
        s_turns = sem("whole_turns_done")
        s_poly = sem("weighted_polynomial_done")
        s_im = sem("sin_terms_done")
        s_sum = sem("sums_done")
        s_sq = sem("squares_done")
        s_blk = sem("group_weights_ready")
        s_y = sem("y_done")
        s_ss = sem("square_sums_done")
        s_v = sem("variance_ready")
        s_f = sem("factor_ready")
        s_yg = sem("y_gated_ready")
        s_o = sem("mix_out_done")
        s_var = sem("mix_variance_ready")
        s_rstd = sem("mix_rstd_ready")
        s_x1 = sem("x1_ready")
        s_x1t = sem("x1_turned")
        s_x1T = sem("x1T_ready")
        own_v, own_a, own_g = sem("vector_own"), sem("scalar_own"), sem("gpsimd_own")
        loop_v, loop_a, loop_g = sem("vector_attend_own"), sem("scalar_attend_own"), sem("gpsimd_attend_own")
        a_q, a_qsb, a_qk, a_qksb = sem("q_done"), sem("q_read"), sem("qk_done"), sem("qk_read")
        a_s, a_max, a_exp, a_t = sem("scores_done"), sem("max_done"), sem("weights_done"), sem("weights_turned")
        a_et, a_pv, a_u = sem("turned_read"), sem("context_sum_done"), sem("context_sum_read")
        a_ut, a_utsb, a_r = sem("context_sum_turned"), sem("context_sum_turned_read"), sem("values_done")
        a_vr, a_rden = sem("values_read_off_psum"), sem("inverse_sum_ready")
        a_res, a_rstd, a_x2 = sem("attended_stats_ready"), sem("attend_rstd_ready"), sem("x2_ready")
        a_x2t, a_x2T, a_x2s = sem("x2_turned"), sem("x2T_ready"), sem("x2_split")
        m_wl = sem("expert_weights_split")
        m_log, m_logit, m_e = sem("logits_done"), sem("routing_dve"), sem("routing_exp")
        m_rw, m_rt, m_rwT = (sem("router_weights_ready"), sem("router_weights_turned"),
                              sem("router_weights_T_ready"))
        m_l1, m_relu, m_hl = sem("hidden_done"), sem("relu_done"), sem("hidden_split")
        m_b1, m_x2b = sem("b1_ready"), sem("x2_plus_beta_ready")
        m_l2, m_acc = sem("expert_out_done"), sem("expert_out_added")
        m_pad = sem("hidden_pads_set")
        mo_v = sem("vector_experts_own")
        f_bias = sem("final_bias_ready")
        f_last = sem("final_last_ready")
        m_last = sem("last_expert_out_done")
        f_var, f_rstd, f_out = sem("final_variance_ready"), sem("final_rstd_ready"), sem("final_ready")
        s_store = sem("stored")

        block = stack.enter_context(nc.Block())

        VALUE, GATE, SCORE = range(3)
        Z_ORDER = [(0, VALUE), (0, SCORE), (1, VALUE), (1, SCORE), (0, GATE), (1, GATE)]
        Z = {cg: n for n, cg in enumerate(Z_ORDER)}
        Y_BANK, SS_BANK, O_BANK, T_BANK = (6, 4), (7, 5), (3, 6), (6, 6)

        def part(e, n):
            return (n % FC, n // FC) if isinstance(e, int) and e in (0, E - 1) else (n // HALVES, n % HALVES)

        LAST_BANK = (6, 7, 0, 1)

        C_EPS, C_HALFPI, C_FACTOR, C_ONE = range(4)

        @block.sync
        def _(sp_):
            sp_.dma_start(first_sb[:], first).then_inc(s_in, 16)

            def taps(g):
                sp_.dma_start(convw_sb[:, g].rearrange("p k n -> p (k n)"),
                              conv_w[g * TAPS * D:(g + 1) * TAPS * D].partition_broadcast(128)).then_inc(s_cw[g], 16)

            taps(VALUE)
            def tokens(c):
                sp_.dma_start(xpad[:, c * HB:(c + 1) * HB], x_T[:, c * HB:(c + 1) * HB]).then_inc(s_xT[c], 16)

            tokens(0)
            taps(SCORE)
            tokens(1)
            taps(GATE)
            sp_.dma_start(small_sb[:], small).then_inc(s_par, 16)
            sp_.dma_start(xtok[:], x_tok).then_inc(s_xtok, 16)

            def ctx_pair(i, s):
                for j in range(2):
                    sp_.dma_start(ctxT_slot[0:DC, s, j, :], ctx_T[2 * i + j]).then_inc(s_ctxT[s], 16)

            def ctx_rows(i, s):
                for j in range(2):
                    sp_.dma_start(ctx_slot[:, s, j],
                                  ctx[2 * i + j]).then_inc(s_ctx[s], 16)

            def load_w(which, e, s):
                src = (w_1, w_2)[which][e]
                sp_.dma_start(w_raw[:, s, which, :], src).then_inc(s_w[2 * which + s], 16)

            for s in range(2):
                ctx_pair(s, s)
                ctx_rows(s, s)
            for s in range(2):
                load_w(0, s, s)
                load_w(1, s, s)
            def next_ctx(i, s):
                sp_.wait_ge(a_s, i + 2)
                ctx_pair(i + 3, 1 - s)
                sp_.wait_ge(a_pv, i + 1)
                ctx_rows(i + 2, s)

            sp_.wait_ge(a_s, 1)
            ctx_pair(2, 0)
            with sp_.Fori(0, PAIRS // 2 - 2) as t:
                next_ctx(2 * t, 0)
                next_ctx(2 * t + 1, 1)
            next_ctx(PAIRS - 4, 0)
            sp_.wait_ge(a_pv, PAIRS - 2)
            ctx_rows(PAIRS - 1, 1)
            with sp_.Fori(0, E // 2 - 1) as t:
                for s in range(2):
                    for which in range(2):
                        sp_.wait_ge(m_wl, 4 * t + 2 * s + 1 + which)
                        load_w(which, 2 * t + s + 2, s)
            for a, b, ready, count in ((0, 4, f_out, 2), (4, 6, f_out, 3), (6, 8, f_last, 1)):
                sp_.wait_ge(ready, count)
                sp_.dma_start(out[:, a:b, :], x1[:, a:b, :]).then_inc(s_store, 16)
            sp_.wait_ge(s_store, 16 * 3)

        @block.tensor
        def _(pe):
            def keep_warm(n, to=O_BANK[0]):
                for _ in range(n):
                    mm = pe.matmul(bank[:, to, 0:HW // 2], reset[:, 0:D], reset[:, 0:HW // 2], start=True,
                                   stop=True)
                return mm

            pe.wait_ge(s_warm, 1)
            keep_warm(4).then_inc(s_warm, 1)
            for c, g in Z_ORDER:
                if g == VALUE:
                    pe.wait_ge(s_xT[c], 16)
                pe.wait_ge(s_convw, (VALUE, SCORE, GATE).index(g) + 1)
                for k in range(TAPS):
                    mm = pe.matmul(bank[:, Z[c, g], 0:HW], w_conv[:, g, k, :],
                                   xpad[:, HB * c:HB * (c + 1), k:k + L], start=(k == 0), stop=(k == TAPS - 1))
                mm.then_inc(s_z, 1)

            def group_sums(c, n):
                pe.wait_ge(s_blk, 1)
                pe.wait_ge(s_sum, 3 * c + 1 + n)
                if c and n == 0:
                    pe.wait_ge(s_gate, 2)
                for j in range(n * M, n * M + M):
                    mm = pe.matmul(bank[:, Y_BANK[c], 0:HW], w_blk[:, j, :], sums[:, j * HW:(j + 1) * HW],
                                   start=(j == 0), stop=(j == 2 * M - 1))
                mm.then_inc(s_y, 1)

            def group_squares(c, first, last):
                for j in range(first, last):
                    if j % M == 0:
                        pe.wait_ge(s_sq, 2 * c + 1 + j // M)
                    mm = pe.matmul(bank[:, SS_BANK[c], 0:HW], par("group_mask"), squares[:, j * HW:(j + 1) * HW],
                                   start=(j == 0), stop=(j == 2 * M - 1))
                if last == 2 * M:
                    mm.then_inc(s_ss, 1)

            def project_out(c):
                pe.wait_ge(s_yg, c + 1)
                for j in range(PPH):
                    mm = pe.matmul(bank[0:PT, O_BANK[c], j * D:(j + 1) * D], y_gated[:, c, j * PT:(j + 1) * PT],
                                   par("w_out"), start=True, stop=True)
                mm.then_inc(s_o, 1)

            def turn_x1(c):
                pe.wait_ge(s_x1, c + 1)
                for j in range(PPH):
                    mm = pe.transpose(bank[:, T_BANK[c], j * PT:(j + 1) * PT], x1[:, c * PPH + j, :],
                                      ident[0:PT, 0:PT])
                mm.then_inc(s_x1t, 1)

            group_sums(0, 0)
            group_squares(0, 0, M)
            group_sums(0, 1)
            group_squares(0, M, 2 * M)
            group_sums(1, 0)
            group_sums(1, 1)
            project_out(0)

            def query(i):
                pe.matmul(bank[:, 7, 0:PT], par("w_q"), x1T[:, bass.ds(i * PT, PT)],
                          start=True, stop=True).then_inc(a_q, 1)

            def query_keys(i):
                pe.wait_ge(a_qsb, i + 1)
                pe.matmul(bank[0:DC + 1, 7, 128:128 + PT], par("w_k"), q_sb[:], start=True, stop=True).then_inc(a_qk, 1)

            def scores(i, s, turn):
                pe.wait_ge(a_qksb, i + 1)
                pe.wait_ge(s_ctxT[s], turn)
                for j, rows in ((0, GAP), (1, L)):
                    for n in range(SB):
                        mm = pe.matmul(bank[j * GAP:j * GAP + rows, n, 0:SN], qk_sb[:, j * L:j * L + rows],
                                       ctxT_slot[:, s, j, n * SN:(n + 1) * SN], start=True, stop=True)
                mm.then_inc(a_s, 1)

            def turn_weights(s, third):
                for c in range(4 * third, 4 * third + 4):
                    mm = pe.transpose(bank[0:KP, 3 + third, (c % 4) * GT:(c % 4 + 1) * GT],
                                      exp_sb[s][:, c * KP:(c + 1) * KP], ident[0:GT, 0:GT])
                mm.then_inc(a_t, 1)

            def context_sum(i, s, turn):
                pe.wait_ge(a_et, 3 * i + 3)
                pe.wait_ge(s_ctx[s], turn)
                for j, rows in ((0, GAP), (1, L)):
                    for c in range(KC):
                        mm = pe.matmul(bank[j * GAP:j * GAP + rows, 6, 0:DC],
                                       expT_sb[:, c, j * GAP:j * GAP + rows], ctx_slot[:, s, j, c, :],
                                       start=(c == 0), stop=(c == KC - 1))
                mm.then_inc(a_pv, 1)

            def turn_sum(i):
                pe.wait_ge(a_u, i + 1)
                pe.transpose(bank[0:DC + 1, 7, 256:256 + GT], u_sb[:], ident[0:GT, 0:GT]).then_inc(a_ut, 1)

            def values(i):
                pe.wait_ge(a_utsb, i + 1)
                pe.matmul(bank[0:PT, 6, 128:128 + D], uT_sb[:], par("w_v", DC + 1), start=True,
                          stop=True).then_inc(a_r, 1)

            def turn_x2(i):
                pe.wait_ge(a_x2, i + 1)
                pe.transpose(bank[:, 7, 384:384 + PT], x2_now[:], ident[0:PT, 0:PT]).then_inc(a_x2t, 1)

            def attend_turn(i, s, ctxT_next, ctx_last, stage=2, more=True, last=False):
                pe.wait_ge(a_exp, i + 1)
                if not last:
                    scores(i + 1, 1 - s, ctxT_next)
                if stage == 1:
                    turn_x1(1)
                if more:
                    if stage == 2:
                        pe.wait_ge(a_x2T, i - 1)
                    query(i + 2)
                if stage:
                    if stage == 1:
                        pe.wait_ge(s_x1T, 2)
                    if stage == 2:
                        pe.wait_ge(a_vr, i - 1)
                    context_sum(i - 1, 1 - s, ctx_last)
                if more:
                    query_keys(i + 2)
                turn_weights(s, 0)
                turn_weights(s, 1)
                if stage:
                    if more:
                        pe.wait_ge(a_qksb, i + 3)
                    turn_sum(i - 1)
                turn_weights(s, 2)
                if stage:
                    values(i - 1)
                if stage == 2:
                    turn_x2(i - 2)

            group_squares(1, 0, M + 1)
            turn_x1(0)
            group_squares(1, M + 1, M + 2)
            pe.wait_ge(s_x1T, 1)
            query(0)
            group_squares(1, M + 2, M + 3)
            query_keys(0)
            group_squares(1, M + 3, 2 * M)
            pe.wait_ge(s_ones, 1)
            scores(0, 0, 32)
            query(1)
            project_out(1)
            query_keys(1)
            pe.wait_ge(a_qksb, 2)
            keep_warm(3)
            attend_turn(0, 0, 32, None, stage=0)
            pe.wait_ge(a_qksb, 3)
            attend_turn(1, 1, 64, 32, stage=1)
            with pe.Fori(1, PAIRS // 2 - 1) as t:
                attend_turn(2 * t, 0, 32 * t + 32, 32 * t)
                attend_turn(2 * t + 1, 1, 32 * t + 64, 32 * t + 32)
            attend_turn(PAIRS - 2, 0, 16 * PAIRS, 16 * PAIRS - 32, more=False)
            attend_turn(PAIRS - 1, 1, None, 16 * PAIRS, more=False, last=True)

            def hidden(e, s, n):
                f, c = part(e, n)
                for k, (w, x) in enumerate(((w1h, x2h), (w1h, x2l), (w1l, x2h))):
                    mm = pe.matmul(bank[:, n % 4, 0:HW], w[:, s, f * 128:(f + 1) * 128],
                                   x[:, c * HW:(c + 1) * HW], start=(k == 0), stop=(k == 2))
                mm.then_inc(m_l1, 1)

            def outs(e, s, n, last=False):
                half = n // 2
                if n == 0:
                    pe.wait_ge(m_wl, 2 * e + 2)
                if last and n % 2 == 0:
                    pe.wait_ge(m_hl, 8 * e + 4 + 4 * half)
                elif n == 0:
                    pe.wait_ge(m_hl, 8 * e + 8)
                if last and n < 2:
                    pe.wait_ge(m_acc, 2 * e + 1 + n)
                elif not last and n % 2 == 0:
                    pe.wait_ge(m_acc, 2 * e + 1 + half)
                for i in (2 * n, 2 * n + 1):
                    to, j = (LAST_BANK[n], i % 2) if last else (4 + 2 * s + half, i % PPH)
                    for f in range(FC):
                        for k, (h_, w_) in enumerate(((hh, w2h), (hh, w2l), (hl, w2h))):
                            mm = pe.matmul(bank[:, to, j * D:(j + 1) * D], h_[:, s, f, i, :],
                                           w_[:, s, f, :], start=(f == 0 and k == 0), stop=(f == FC - 1 and k == 2))
                if last:
                    mm.then_inc(m_last, 1)
                elif n % 2:
                    mm.then_inc(m_l2, 1)

            def logits(i):
                return pe.matmul(bank[0:PT, 4, i * E:(i + 1) * E], x2T[:, i * PT:(i + 1) * PT], par("w_r"),
                                 start=True, stop=True)

            pe.wait_ge(m_wl, 1)
            pe.wait_ge(a_x2s, PAIRS)
            hidden(0, 0, 0)
            hidden(0, 0, 1)
            pe.wait_ge(a_vr, PAIRS - 1)
            context_sum(PAIRS - 1, 1, 16 * PAIRS)
            pe.wait_ge(a_x2T, PAIRS - 1)
            turn_x2(PAIRS - 2)
            hidden(0, 0, 2)
            keep_warm(2, 5)
            pe.wait_ge(a_x2T, PAIRS)
            turn_sum(PAIRS - 1)
            hidden(0, 0, 3)
            values(PAIRS - 1)
            for i in range(PAIRS - 1):
                logits(i)
            keep_warm(2, 5)
            turn_x2(PAIRS - 1)
            keep_warm(1, 5)
            pe.wait_ge(a_x2T, PAIRS + 1)
            logits(PAIRS - 1).then_inc(m_log, 1)
            keep_warm(2, 5)
            pe.wait_ge(a_x2s, 2 * PAIRS)
            for n in range(4, 8):
                pe.wait_ge(m_relu, n - 3)
                hidden(0, 0, n)
            pe.wait_ge(m_rw, 1)
            for i in range(PAIRS):
                mm = pe.transpose(bank[0:E, 4 + i // PPH, (i % PPH) * PT:(i % PPH + 1) * PT], rw[:, i, :],
                                  ident[0:PT, 0:PT])
            mm.then_inc(m_rt, 1)
            keep_warm(3, 7)
            pe.wait_ge(m_rwT, 1)
            for i in range(PAIRS):
                mm = pe.matmul(bank[0:PT, 6 + i // PPH, (i % PPH) * D:(i % PPH + 1) * D],
                               rwT[:, i * PT:(i + 1) * PT], par("b_2", E), start=True, stop=True)
            mm.then_inc(m_l2, 2)

            def two_hidden(e, s, n):
                for k in (2 * n, 2 * n + 1):
                    pe.wait_ge(m_relu, 8 * e + k - 3)
                    hidden(e, s, k)

            def expert_turn(e, s):
                pe.wait_ge(m_wl, 2 * e + 3)
                for n in range(4):
                    two_hidden(e + 1, 1 - s, n)
                    outs(e, s, n)

            pe.wait_ge(m_pad, 2)
            with pe.Fori(0, E // 2 - 1) as t:
                expert_turn(2 * t, 0)
                expert_turn(2 * t + 1, 1)
            pe.wait_ge(m_wl, 2 * E - 1)
            two_hidden(E - 1, 1, 0)
            outs(E - 2, 0, 0)
            two_hidden(E - 1, 1, 1)
            outs(E - 2, 0, 1)
            two_hidden(E - 1, 1, 2)
            outs(E - 1, 1, 0, last=True)
            two_hidden(E - 1, 1, 3)
            outs(E - 1, 1, 1, last=True)
            outs(E - 2, 0, 2)
            outs(E - 2, 0, 3)
            outs(E - 1, 1, 2, last=True)
            outs(E - 1, 1, 3, last=True)

        @block.scalar
        def _(act):
            own = Own(act, own_a)
            act.preload_act_table_set("natural_log_exp_and_others")
            act.wait_ge(s_sd, 1)
            nc.scalar.activation(sp[:, 1:2], sp[:, 0:1], ACT.Exp, scale=-1.0).then_inc(s_sp, 1)
            nc.scalar.activation(dsm[:, 4:7], dsm[:, 0:3], ACT.Exp).then_inc(s_sp, 1)
            act.wait_ge(s_sp, 1)
            act.wait_ge(s_cst, 1)
            nc.scalar.activation(sp[:, 2:3], sp[:, 1:2], ACT.Ln, bias=cst[:, C_ONE:C_ONE + 1]).then_inc(s_sp, 1)
            act.wait_ge(s_sd, 2)
            nc.scalar.activation(time_w[:], par("dist"), ACT.Exp, scale=sp[:, 3:4]).then_inc(s_sp, 1)
            act.wait_ge(s_in, 16)

            def read_values(c):
                act.wait_ge(s_z, Z[c, VALUE] + 1)
                nc.scalar.activation(xv[:, c, :], bank[:, Z[c, VALUE], 0:HW], ACT.Identity,
                                     bias=par("conv_b")[:, 0:1]).then_inc(s_xv, 1)

            def read_scores(c):
                act.wait_ge(s_z, Z[c, SCORE] + 1)
                act.wait_ge(s_sd, 3)
                nc.scalar.activation(sc[:, c, :], bank[:, Z[c, SCORE], 0:HW], ACT.Identity, bias=sbias[:],
                                     scale=par("score_scale")).then_inc(s_sc, 1)

            def exponentials(c):
                act.wait_ge(s_score, c + 1)
                nc.scalar.activation(sc[:, c, :], sc[:, c, :], ACT.Exp).then_inc(s_p, 1)

            def read_gates(c):
                act.wait_ge(s_z, Z[c, GATE] + 1)
                gr = own.mark(nc.scalar.activation(xg[:, c, :], bank[:, Z[c, GATE], 0:HW], ACT.Identity,
                                                   bias=par("conv_b")[:, 1:2]))
                own.need(gr)
                nc.scalar.activation(gate[:, c, :], xg[:, c, :], ACT.Tanh, scale=0.5).then_inc(s_gate, 1)

            def cosines(c):
                act.wait_ge(s_phase, c + 1)
                a = own.mark(nc.scalar.activation(pc[c], ph[c], ACT.Abs))
                own.need(a)
                nc.scalar.activation(pc[c], pc[c], ACT.Sin, scale=-1.0,
                                     bias=cst[:, C_HALFPI:C_HALFPI + 1]).then_inc(s_trig, 1)

            def sines(c):
                nc.scalar.activation(ph[c], ph[c], ACT.Sin).then_inc(s_trig, 1)

            def square(c, n):
                act.wait_ge(s_sum, 3 * c + 1 + n)
                if c:
                    act.wait_ge(s_ss, c)
                w = slice(n * M * HW, (n + 1) * M * HW)
                nc.scalar.activation(squares[:, w], sums[:, w], ACT.Square).then_inc(s_sq, 1)

            def factor(c):
                act.wait_ge(s_v, c + 1)
                a = own.mark(nc.scalar.activation(sc[:, c, :], sc[:, c, :], ACT.Ln, scale=2.0 ** -V_DOWN))
                own.need(a)
                nc.scalar.activation(sc[:, c, :], sc[:, c, :], ACT.Exp, scale=-0.5,
                                     bias=cst[:, C_FACTOR:C_FACTOR + 1]).then_inc(s_f, 1)

            def inv_std(own_, var, tmp, to, done):
                a = own_.mark(nc.scalar.activation(tmp, var, ACT.Ln, bias=cst[0:PT, C_EPS:C_EPS + 1]))
                own_.need(a)
                nc.scalar.activation(to, tmp, ACT.Exp, scale=-0.5).then_inc(done, 1)

            def mix_inv_std(c):
                w = slice(c * PPH, (c + 1) * PPH)
                act.wait_ge(s_var, c + 1)
                inv_std(own, mv[:, w, 1], lnv[:, w], rstd[:, w], s_rstd)

            def x1T_copy(c):
                act.wait_ge(s_x1t, c + 1)
                nc.scalar.copy(x1T[:, c * HW:(c + 1) * HW], bank[:, T_BANK[c], 0:HW]).then_inc(s_x1T, 1)

            read_values(0)
            read_scores(0)
            read_values(1)
            exponentials(0)
            act.preload_act_table_set("trig_and_small")
            cosines(0)
            sines(0)
            read_scores(1)
            act.preload_act_table_set("exp_and_others")
            exponentials(1)
            read_gates(0)
            read_gates(1)
            square(0, 0)
            act.preload_act_table_set("trig_and_small")
            cosines(1)
            square(0, 1)
            sines(1)
            act.preload_act_table_set("natural_log_exp_and_others")
            square(1, 0)
            factor(0)
            square(1, 1)
            mix_inv_std(0)
            x1T_copy(0)

            loop = Own(act, loop_a)

            def queries(i):
                act.wait_ge(a_q, i + 1)
                nc.scalar.activation(q_sb[:], bank[:, 7, 0:PT], ACT.Identity, bias=qbias[:],
                                     scale=1.0 / sqrt(D)).then_inc(a_qsb, 1)

            def weights_exp(i, s):
                act.wait_ge(a_max, i + 1)
                nc.scalar.activation(exp_sb[s].rearrange("q (n k) -> q n k", n=SB), bank[0:GT, 0:SB, 0:SN], ACT.Exp,
                                     bias=neg_max[0:GT, :], accum_out=den[:, s:s + 1]).then_inc(a_exp, 1)

            def turned_sum(i):
                act.wait_ge(a_ut, i + 1)
                nc.scalar.copy(uT_sb[:].rearrange("d (j l) -> d j l", j=2),
                               bank[0:DC + 1, 7, 256:256 + 2 * GAP].rearrange("d (j l) -> d j l", j=2)[:, :, 0:L]
                               ).then_inc(a_utsb, 1)

            def attended_inv_std(i):
                act.wait_ge(a_res, i + 1)
                inv_std(loop, mv[:, 0, 1:2], lnv[:, 0:1], rstd[:, 0:1], a_rstd)

            def attend_turn(i, s, first=False, second=False, more=True, last=False):
                if second:
                    x1T_copy(1)
                if more:
                    queries(i + 2)
                if not last:
                    weights_exp(i + 1, 1 - s)
                act.wait_ge(a_t, 3 * i + 1)
                nc.scalar.copy(expT_sb[:, 0:4, :], bank[0:KP, 3, 0:4 * GT].rearrange("p (c q) -> p c q", c=4)
                               ).then_inc(a_et, 1)
                if not first:
                    turned_sum(i - 1)
                    attended_inv_std(i - 1)

            act.wait_ge(s_sd, 4)
            queries(0)
            factor(1)
            queries(1)
            weights_exp(0, 0)
            mix_inv_std(1)
            attend_turn(0, 0, first=True)
            attend_turn(1, 1, second=True)
            with act.Fori(1, PAIRS // 2 - 1) as t:
                loop.turn(2 * t - 1)
                attend_turn(2 * t, 0)
                attend_turn(2 * t + 1, 1)
            loop.turn(PAIRS - 3)
            attend_turn(PAIRS - 2, 0, more=False)
            attend_turn(PAIRS - 1, 1, more=False, last=True)

            def relu(e, s, n):
                f, c = part(e, n)
                if n == 0:
                    act.wait_ge(m_b1, e + 1)
                act.wait_ge(m_l1, 8 * e + n + 1)
                nc.scalar.activation(hh[:, s, f, c * PPH:(c + 1) * PPH, 0:PT], bank[:, n % 4, 0:HW]
                                     .rearrange("p (j t) -> p j t", j=PPH), ACT.Relu, scale=1.0 / WS,
                                     bias=b1_now[:, s, f:f + 1])

            def relu_again(e, s, n, wait=True):
                f, c = part(e, n)
                if wait:
                    act.wait_ge(m_hl, 8 * e + n - 3)
                nc.scalar.activation(hid[:, n % 4, :], bank[:, n % 4, 0:HW], ACT.Relu, scale=1.0 / WS,
                                     bias=b1_now[:, s, f:f + 1]).then_inc(m_relu, 1)

            def b1_copy(e, s):
                a = at2["b_1"][0]
                nc.scalar.copy(b1_now[:, s, :], small_sb[:, bass.ds(a + FC * e, FC)]).then_inc(m_b1, 1)

            def first_relu(n):
                relu(0, 0, n)
                relu_again(0, 0, n, wait=n > 3)

            b1_copy(0, 0)
            first_relu(0)
            first_relu(1)
            turned_sum(PAIRS - 1)
            first_relu(2)
            attended_inv_std(PAIRS - 1)
            first_relu(3)
            act.wait_ge(m_e, 1)
            nc.scalar.activation(tsm[:, 1, :], tsm[:, 0, :], ACT.Exp).then_inc(m_e, 1)
            for n in range(4, 8):
                first_relu(n)

            def expert_turn(e, s):
                b1_copy(e, s)
                for n in range(2 * FC):
                    if n == 0:
                        act.wait_ge(m_l2, 2 * e)
                    relu(e, s, n)
                    relu_again(e, s, n)

            with act.Fori(0, E // 2 - 1) as t:
                expert_turn(2 * t + 1, 1)
                expert_turn(2 * t + 2, 0)
            expert_turn(E - 1, 1)

            def final_inv_std(q, second):
                w = slice(2 * q, 2 * q + 2)
                act.wait_ge(f_var, 2 * q + 1 + second)
                inv_std(own, mv[:, w, 1], lnv[:, w], rstd2[:, w] if second else rstd[:, w], f_rstd)

            def final_norm(q):
                act.wait_ge(f_bias, q + 1)
                for j in (2 * q, 2 * q + 1):
                    ins = nc.scalar.activation(x1[:, j, :], acc[:, j, :], ACT.Identity, bias=nmr[:, j:j + 1],
                                               scale=rstd2[:, j:j + 1])
                ins.then_inc(f_out, 1)

            for q in range(4):
                final_inv_std(q, False)
                if q:
                    final_norm(q - 1)
                final_inv_std(q, True)

        @block.vector
        def _(dve):
            own = Own(dve, own_v)
            V = nc.vector
            V.memset(reset[:, 0:HW], 1.0).then_inc(s_warm, 1)
            own.mark(V.memset(reset[:, HW:], 1.0))
            V.memset(u_sb[:, DC:], 1.0)
            V.memset(cst[:, C_EPS:C_EPS + 1], LN_EPS)
            V.memset(cst[:, C_HALFPI:C_HALFPI + 1], pi / 2)
            V.memset(cst[:, C_FACTOR:C_FACTOR + 1], -0.5 * V_DOWN * log(2.0) - log(2.0))
            V.memset(cst[:, C_ONE:C_ONE + 1], 1.0).then_inc(s_cst, 1)
            def fold(g):
                dve.wait_ge(s_cw[g], 16)
                V.tensor_tensor(w_conv[:, g], par("w_in")[:, g * D:(g + 1) * D].unsqueeze(1)
                                .broadcast_to([128, TAPS, D]), convw_sb[:, g], ALU.mult).then_inc(s_convw, 1)

            dve.wait_ge(s_in, 16)
            fold(VALUE)
            own.mark(V.scalar_tensor_tensor(sp[:, 0:1], par("slope"), -1.0, par("slope"), ALU.mult, ALU.max))
            a = own.mark(V.tensor_reduce(dsm[:, 3:4], par("deriv"), AX.X, ALU.max))
            own.need(a)
            V.tensor_scalar(dsm[:, 0:3], par("deriv"), dsm[:, 3:4], None, ALU.subtract).then_inc(s_sd, 1)
            own.mark(V.tensor_scalar(theta_t[:], par("theta"), 1.0 / (2 * pi), None, ALU.mult))
            dve.wait_ge(s_sp, 3)
            a = own.mark(V.scalar_tensor_tensor(sp[:, 3:4], par("slope"), 0.0, sp[:, 2:3], ALU.max, ALU.add))
            own.need(a)
            V.tensor_scalar(sp[:, 3:4], sp[:, 3:4], -1.0, None, ALU.mult).then_inc(s_sd, 1)
            V.tensor_tensor(sbias[:], par("conv_b")[:, 2:3], par("score_scale"), ALU.mult).then_inc(s_sd, 1)
            a = own.mark(V.tensor_reduce(dsm[:, 7:8], dsm[:, 4:7], AX.X, ALU.add))
            own.need(a)
            a = own.mark(V.reciprocal(dsm[:, 7:8], dsm[:, 7:8]))
            own.need(a)
            a = own.mark(V.tensor_scalar(dsm[:, 8:11], dsm[:, 4:7], dsm[:, 7:8], None, ALU.mult))
            own.need(a)
            a = own.mark(V.tensor_scalar(dsm[:, 11:12], dsm[:, 10:11], -1.0, None, ALU.mult))
            fold(SCORE)
            fold(GATE)
            own.need(1)
            dve.wait_ge(s_warm, 2)
            own.mark(V.memset(reset[:].rearrange("p (n l) -> p n l", l=L)[:, :, 0:1], 0.0))
            dve.wait_ge(s_par, 16)
            V.tensor_scalar(qbias[:], par("b_q"), 1.0 / sqrt(D), None, ALU.mult).then_inc(s_sd, 1)
            a = own.mark(V.tensor_tensor(w_rin[:], par("w_ri").rearrange("p (j h) -> p j h", j=2 * M),
                                         par("norm_scale").unsqueeze(2).broadcast_to([128, 2 * M, H]), ALU.mult))
            own.need(a)
            for j in range(2 * M):
                ins = V.tensor_tensor(w_blk[:, j, :].rearrange("p (k h) -> p k h", k=K),
                                      w_rin[:, j, :].unsqueeze(1).broadcast_to([128, K, H]),
                                      par("group_mask").rearrange("p (k h) -> p k h", k=K), ALU.mult)
            ins.then_inc(s_blk, 1)

            W = M * HW

            def clip(c):
                dve.wait_ge(s_sc, c + 1)
                V.tensor_scalar(sc[:, c, :], sc[:, c, :], 20.0, -20.0, ALU.min, ALU.max).then_inc(s_score, 1)

            def gates(c):
                dve.wait_ge(s_gate, c + 1)
                own.mark(V.scalar_tensor_tensor(gate[:, c, :], gate[:, c, :], 1.0, xg[:, c, :], ALU.add, ALU.mult))

            def weights(c):
                pw = terms[:, 2 * W:2 * W + HW]
                q0 = poly[c]
                a = own.mark(V.tensor_scalar(q0, xv[:, c, :], dsm[:, 11:12], dsm[:, 9:10], ALU.mult, ALU.add))
                own.need(a)
                a = own.mark(V.tensor_tensor(q0, q0, xv[:, c, :], ALU.mult))
                dve.wait_ge(s_p, c + 1)
                dve.wait_ge(s_sp, 4)
                b = own.mark(V.tensor_tensor(pw.rearrange("p (b l) -> p b l", b=HB),
                                             sc[:, c, :].rearrange("p (b l) -> p b l", b=HB),
                                             time_w[:].unsqueeze(1).broadcast_to([128, HB, L]), ALU.mult))
                own.need(b)
                V.scalar_tensor_tensor(q0, q0, dsm[:, 8:9], pw, ALU.add, ALU.mult).then_inc(s_poly, 1)

            def turns(c):
                dve.wait_ge(s_xv, c + 1)
                for m in range(M):
                    a = own.mark(V.tensor_scalar(ph[c][:, m, :], xv[:, c, :], theta_t[:, m:m + 1], MAGIC,
                                                 ALU.mult, ALU.add))
                own.need(a)
                a = own.mark(V.tensor_scalar(ph[c], ph[c], -MAGIC, 2 * pi, ALU.add, ALU.mult))
                own.need(a)

            def phases(c, between=None):
                for m in range(M):
                    a = own.mark(V.scalar_tensor_tensor(ph[c][:, m, :], xv[:, c, :], par("theta")[:, m:m + 1],
                                                        ph[c][:, m, :], ALU.mult, ALU.subtract))
                if between:
                    between()
                own.need(a)
                V.tensor_scalar(ph[c], ph[c], 3.1415925, -3.1415925, ALU.min, ALU.max).then_inc(s_phase, 1)

            def cos_terms(c):
                dve.wait_ge(s_trig, 2 * c + 1)
                dve.wait_ge(s_poly, c + 1)
                a = own.mark(V.tensor_tensor(terms[:, 0:W].rearrange("p (m w) -> p m w", m=M), pc[c],
                                             poly[c].unsqueeze(1).broadcast_to([128, M, HW]), ALU.mult))
                return a

            def scan_re(c, terms_ready):
                own.need(terms_ready)
                if c:
                    dve.wait_ge(s_y, 2 * c - 1)
                    dve.wait_ge(s_sq, 2 * c - 1)
                V.tensor_tensor_scan(sums[:, 0:W], reset[:], terms[:, 0:W], 0.0, ALU.mult, ALU.add).then_inc(s_sum, 1)
                return own.mark(V.tensor_tensor_scan(sums[:, 2 * W:2 * W + HW], reset[:, 0:HW],
                                                     terms[:, 2 * W:2 * W + HW], 0.0, ALU.mult, ALU.add))

            def scan_im(c, weights_summed):
                dve.wait_ge(s_im, c + 1)
                if c:
                    dve.wait_ge(s_y, 2 * c)
                    dve.wait_ge(s_sq, 2 * c)
                V.tensor_tensor_scan(sums[:, W:2 * W], reset[:], terms[:, W:2 * W], 0.0, ALU.mult,
                                     ALU.add).then_inc(s_sum, 2)
                own.need(weights_summed)
                a = own.mark(V.tensor_scalar(sc[:, c, :], sums[:, 2 * W:2 * W + HW], 1e-4, sqrt(LN_EPS),
                                             ALU.max, ALU.mult))
                own.need(a)
                return own.mark(V.tensor_tensor(sc[:, c, :], sc[:, c, :], sc[:, c, :], ALU.mult))

            def split(which, e, s, turn, own_):
                raw = w_raw[:, s, which, :]
                high, low = ((w1h[:, s, :], w1l[:, s, :]),
                             (w2h[:, s].rearrange("p f d -> p (f d)"), w2l[:, s].rearrange("p f d -> p (f d)")))[which]
                dve.wait_ge(s_w[2 * which + s], turn)
                a = own_.mark(V.tensor_scalar(high, raw, WS, None, ALU.mult))
                own_.need(a)
                V.scalar_tensor_tensor(low, raw, WS, high, ALU.mult, ALU.subtract).then_inc(m_wl, 1)

            def variance(c):
                dve.wait_ge(s_ss, c + 1)
                own.need(dens[c])
                V.scalar_tensor_tensor(sc[:, c, :], bank[:, SS_BANK[c], 0:HW], 1.0 / (2 * H * M), sc[:, c, :],
                                       ALU.mult, ALU.add).then_inc(s_v, 1)

            def gated(c):
                dve.wait_ge(s_f, c + 1)
                a = own.mark(V.tensor_tensor(gate[:, c, :], gate[:, c, :], sc[:, c, :], ALU.mult))
                own.need(a)
                V.tensor_tensor(y_gated[:, c, :], bank[:, Y_BANK[c], 0:HW], gate[:, c, :], ALU.mult).then_inc(s_yg, 1)

            def mixed(c):
                w = slice(c * PPH, (c + 1) * PPH)
                dve.wait_ge(s_o, c + 1)
                a = own.mark(V.tensor_tensor(x1[:, w, :], bank[0:PT, O_BANK[c], 0:PPH * D]
                                             .rearrange("p (j d) -> p j d", j=PPH), xtok[:, w, :], ALU.add))
                own.need(a)
                for j in range(c * PPH, (c + 1) * PPH):
                    a = own.mark(V.bn_stats(stat[:, j, :], x1[:, j, :]))
                own.need(a)
                for j in range(c * PPH, (c + 1) * PPH):
                    ins = V.bn_aggr(mv[:, j, :], stat[:, j, :])
                ins.then_inc(s_var, 1)

            def mixed_norm(c):
                dve.wait_ge(s_rstd, c + 1)
                for j in range(c * PPH, (c + 1) * PPH):
                    ins = V.tensor_scalar(x1[:, j, :], x1[:, j, :], mv[:, j, 0:1], rstd[:, j:j + 1],
                                          ALU.subtract, ALU.mult)
                ins.then_inc(s_x1, 1)

            turns(0)
            phases(0, between=lambda: clip(0))
            weights(0)
            a = cos_terms(0)
            clip(1)
            b = scan_re(0, a)
            dve.wait_ge(s_turns, 1)
            phases(1)
            dens = [scan_im(0, b)]
            weights(1)
            a = cos_terms(1)
            b = scan_re(1, a)
            variance(0)
            gates(0)
            dens.append(scan_im(1, b))
            gated(0)
            gates(1)
            split(0, 0, 0, 16, own)
            dve.wait_ge(s_xtok, 16)
            mixed(0)
            mixed_norm(0)

            V.memset(carrier[:], 0.0).then_inc(a_x2T, 1)
            loop = Own(dve, loop_v)

            def query_keys(i):
                dve.wait_ge(a_qk, i + 1)
                V.tensor_copy(qk_sb[:], bank[0:DC + 1, 7, 128:128 + PT]).then_inc(a_qksb, 1)

            def maximum(i):
                dve.wait_ge(a_s, i + 1)
                V.tensor_reduce(neg_max[0:GT, :], bank[0:GT, 0:SB, 0:SN], AX.XY, ALU.max,
                                negate=True).then_inc(a_max, 1)

            def x2T_copy(i):
                dve.wait_ge(a_x2t, i + 1)
                V.tensor_copy(x2T[:, bass.ds(i * PT, PT)], bank[:, 7, 384:384 + PT]).then_inc(a_x2T, 1)

            def inverse(i, s):
                dve.wait_ge(a_exp, i + 1)
                V.reciprocal(rden[:, s:s + 1], den[:, s:s + 1]).then_inc(a_rden, 1)

            def sum_copy(i, s):
                dve.wait_ge(a_rden, i + 1)
                dve.wait_ge(a_pv, i + 1)
                V.tensor_scalar(u_sb[:, 0:DC], bank[0:GT, 6, 0:DC], rden[:, s:s + 1], None, ALU.mult).then_inc(a_u, 1)

            def turned_copy(i):
                for n in (1, 2):
                    dve.wait_ge(a_t, 3 * i + n + 1)
                    V.tensor_copy(expT_sb[:, 4 * n:4 * n + 4, :], bank[0:KP, 3 + n, 0:4 * GT]
                                  .rearrange("p (c q) -> p c q", c=4)).then_inc(a_et, 1)

            def attended(i, check=True):
                dve.wait_ge(a_r, i + 1)
                V.tensor_tensor(res[:], bank[0:PT, 6, 128:128 + D],
                                x1[:, bass.ds(i, 1), :].rearrange("p i d -> p (i d)"), ALU.add).then_inc(a_vr, 1)
                dve.wait_ge(a_vr, i + 1)
                a = loop.mark(V.bn_stats(stat[:, 0, :], res[:]))
                loop.need(a)
                V.tensor_copy(carrier[:, 0:1], cst[:, 0:1])
                V.bn_aggr(mv[:, 0, :], stat[:, 0, :]).then_inc(a_res, 1)
                dve.wait_ge(a_rstd, i + 1)
                if check:
                    dve.wait_ge(a_x2t, i)
                    dve.wait_ge(a_x2s, 2 * i - 1)
                V.tensor_scalar(x2_now[:], res[:], mv[:, 0, 0:1], rstd[:, 0:1], ALU.subtract,
                                ALU.mult).then_inc(a_x2, 1)

            def attend_turn(i, s, stage=2, more=True, last=False):
                if not last:
                    maximum(i + 1)
                inverse(i, s)
                if stage:
                    sum_copy(i - 1, 1 - s)
                if more:
                    query_keys(i + 2)
                turned_copy(i)
                if stage == 2:
                    x2T_copy(i - 2)
                if stage:
                    attended(i - 1, stage == 2)

            query_keys(0)
            variance(1)
            split(1, 0, 0, 16, own)
            gated(1)
            maximum(0)
            query_keys(1)
            mixed(1)
            mixed_norm(1)
            attend_turn(0, 0, stage=0)
            split(0, 1, 1, 16, own)
            attend_turn(1, 1, stage=1)
            with dve.Fori(1, PAIRS // 2 - 1) as t:
                loop.turn(2 * t - 1)
                attend_turn(2 * t, 0)
                attend_turn(2 * t + 1, 1)
            loop.turn(PAIRS - 3)
            attend_turn(PAIRS - 2, 0, more=False)
            attend_turn(PAIRS - 1, 1, more=False, last=True)

            def hidden_low(e, s, n):
                f, c = part(e, n)
                dve.wait_ge(m_relu, 8 * e + n + 1)
                w = slice(c * PPH, (c + 1) * PPH)
                V.tensor_tensor(hl[:, s, f, w, 0:PT], hid[:, n % 4, :].rearrange("p (j t) -> p j t", j=PPH),
                                hh[:, s, f, w, 0:PT], ALU.subtract).then_inc(m_hl, 1)

            def add_outs(e, s, half):
                dve.wait_ge(m_l2, 2 * e + half + 3)
                dve.wait_ge(m_acc, 2 * e + half + 3)
                for j in range(PPH):
                    i = half * PPH + j
                    ins = V.scalar_tensor_tensor(acc[:, i, :], bank[0:PT, 4 + 2 * s + half, j * D:(j + 1) * D],
                                                 rws[:, i, bass.ds(e, 1)], acc[:, i, :], ALU.mult, ALU.add)
                ins.then_inc(m_acc, 1)

            hidden_low(0, 0, 0)
            hidden_low(0, 0, 1)
            x2T_copy(PAIRS - 2)
            sum_copy(PAIRS - 1, 1)
            attended(PAIRS - 1)
            x2T_copy(PAIRS - 1)
            hidden_low(0, 0, 2)
            hidden_low(0, 0, 3)

            weight_own = Own(dve, mo_v)
            dve.wait_ge(m_log, 1)
            a = own.mark(V.tensor_tensor(logit[:], bank[0:PT, 4, 0:PAIRS * E].rearrange("p (i e) -> p i e", i=PAIRS),
                                         par("b_r", PT).unsqueeze(1).broadcast_to([PT, PAIRS, E]), ALU.add))
            own.need(a)
            for i in range(PAIRS):
                a = own.mark(V.max(top[:, i, :], logit[:, i, :]))
            own.need(a)
            V.tensor_tensor(tsm[:, 0, :], top[:, :, 1], top[:, :, 0], ALU.subtract).then_inc(m_e, 1)
            for i in range(PAIRS):
                b = own.mark(V.max_index(topi[:, i, :], top[:, i, :], logit[:, i, :]))
            own.need(b)
            a = own.mark(V.tensor_copy(topf[:], topi[:, :, 0:2]))
            dve.wait_ge(m_e, 2)
            a = own.mark(V.tensor_scalar(tsm[:, 2, :], tsm[:, 1, :], 1.0, None, ALU.add))
            own.need(a)
            a = own.mark(V.reciprocal(tsm[:, 3, :], tsm[:, 2, :]))
            own.need(a)
            a = own.mark(V.tensor_tensor(tsm[:, 4, :], tsm[:, 1, :], tsm[:, 3, :], ALU.mult))
            iota = par("iota", PT).unsqueeze(1).broadcast_to([PT, PAIRS, E])

            def spread(x):
                return x.unsqueeze(2).broadcast_to([PT, PAIRS, E])

            own.mark(V.tensor_tensor(rw[:], iota, spread(topf[:, :, 0]), ALU.is_equal))
            b = own.mark(V.tensor_tensor(rws[:], iota, spread(topf[:, :, 1]), ALU.is_equal))
            own.need(b)
            own.mark(V.tensor_tensor(rw[:], rw[:], spread(tsm[:, 3, :]), ALU.mult))
            b = own.mark(V.tensor_tensor(rws[:], rws[:], spread(tsm[:, 4, :]), ALU.mult))
            own.need(b)
            a = own.mark(V.tensor_tensor(rw[:], rw[:], rws[:], ALU.add))
            own.need(a)
            V.tensor_scalar(rws[:], rw[:], 1.0 / WS, None, ALU.mult).then_inc(m_rw, 1)
            hidden_low(0, 0, 4)
            hidden_low(0, 0, 5)
            dve.wait_ge(m_rt, 1)
            V.tensor_copy(rwT[:].rearrange("e (h t) -> e h t", h=2), bank[0:E, 4:6, 0:HW]).then_inc(m_rwT, 1)
            hidden_low(0, 0, 6)
            hidden_low(0, 0, 7)
            dve.wait_ge(m_l2, 2)
            for half in range(HALVES):
                w = slice(half * PPH, (half + 1) * PPH)
                ins = V.tensor_tensor(acc[:, w, :], bank[0:PT, 6 + half, :].rearrange("p (j d) -> p j d", j=PPH),
                                      x2[:, w, :], ALU.add)
            ins.then_inc(m_acc, 4)

            def expert_turn(e, s, w1_turn, w2_turn):
                hidden_low(e + 1, 1 - s, 0)
                dve.wait_ge(m_l2, 2 * e + 2)
                split(1, e + 1, 1 - s, w2_turn, weight_own)
                hidden_low(e + 1, 1 - s, 1)
                hidden_low(e + 1, 1 - s, 2)
                if w1_turn is not None:
                    dve.wait_ge(m_l1, 8 * e + 8)
                    split(0, e + 2, s, w1_turn, weight_own)
                hidden_low(e + 1, 1 - s, 3)
                hidden_low(e + 1, 1 - s, 4)
                hidden_low(e + 1, 1 - s, 5)
                add_outs(e, s, 0)
                hidden_low(e + 1, 1 - s, 6)
                hidden_low(e + 1, 1 - s, 7)
                add_outs(e, s, 1)

            with dve.Fori(0, E // 2 - 1) as t:
                weight_own.turn(4 * t)
                expert_turn(2 * t, 0, 16 * t + 32, 16 * t + 16)
                expert_turn(2 * t + 1, 1, 16 * t + 32, 16 * t + 32)

            def stats(q):
                for j in (2 * q, 2 * q + 1):
                    a = own.mark(V.bn_stats(stat[:, j, :], acc[:, j, :]))
                own.need(a)
                for j in (2 * q, 2 * q + 1):
                    a = V.bn_aggr(mv[:, j, :], stat[:, j, :])
                a.then_inc(f_var, 1)

            def last_outs(q):
                dve.wait_ge(m_last, q + 1)
                dve.wait_ge(m_acc, 2 * E + 1 + q // 2)
                for j in (2 * q, 2 * q + 1):
                    a = own.mark(V.scalar_tensor_tensor(acc[:, j, :], bank[0:PT, LAST_BANK[q], (j % 2) * D:
                                                                           (j % 2 + 1) * D],
                                                        rws[:, j, E - 1:E], acc[:, j, :], ALU.mult, ALU.add))
                own.need(a)
                stats(q)
                dve.wait_ge(f_var, 2 * q + 1)
                for j in (2 * q, 2 * q + 1):
                    a = own.mark(V.scalar_tensor_tensor(acc[:, j, :], acc[:, j, :], mv[:, j, 0:1], par("gamma", PT),
                                                        ALU.subtract, ALU.mult))
                return a

            def last_sum(q, normed):
                own.need(normed)
                dve.wait_ge(m_x2b, 1)
                dve.wait_ge(f_rstd, 2 * q + 1)
                for j in (2 * q, 2 * q + 1):
                    a = own.mark(V.scalar_tensor_tensor(acc[:, j, :], acc[:, j, :], rstd[:, j:j + 1], x2b[:, j, :],
                                                        ALU.mult, ALU.add))
                own.need(a)
                stats(q)

            def final_bias(q):
                w = slice(2 * q, 2 * q + 2)
                dve.wait_ge(f_rstd, 2 * q + 2)
                V.scalar_tensor_tensor(nmr[:, w], mv[:, w, 0], -1.0, rstd2[:, w], ALU.mult, ALU.mult).then_inc(f_bias, 1)

            weight_own.turn(4 * (E // 2 - 1))
            hidden_low(E - 1, 1, 0)
            dve.wait_ge(m_l2, 2 * (E - 2) + 2)
            split(1, E - 1, 1, 16 * (E // 2), weight_own)
            for n in range(1, 4):
                hidden_low(E - 1, 1, n)
            add_outs(E - 2, 0, 0)
            hidden_low(E - 1, 1, 4)
            hidden_low(E - 1, 1, 5)
            a = last_outs(0)
            hidden_low(E - 1, 1, 6)
            hidden_low(E - 1, 1, 7)
            last_sum(0, a)
            a = last_outs(1)
            final_bias(0)
            last_sum(1, a)
            add_outs(E - 2, 0, 1)
            a = last_outs(2)
            final_bias(1)
            last_sum(2, a)
            a = last_outs(3)
            final_bias(2)
            last_sum(3, a)
            dve.wait_ge(f_rstd, 8)
            for j in (PAIRS - 2, PAIRS - 1):
                ins = V.tensor_scalar(x1[:, j, :], acc[:, j, :], mv[:, j, 0:1], rstd2[:, j:j + 1],
                                      ALU.subtract, ALU.mult)
            ins.then_inc(f_last, 1)

        @block.gpsimd
        def _(pool):
            own = Own(pool, own_g)
            G = nc.gpsimd
            G.memset(ctxT_slot[DC:DC + 1], 1.0).then_inc(s_ones, 1)
            pool.wait_ge(s_ones, 1)
            pool.wait_ge(s_cst, 1)
            pool.wait_ge(s_xv, 2)
            pool.wait_ge(s_sd, 2)
            for m in range(M):
                a = own.mark(G.tensor_scalar(ph[1][:, m, :], xv[:, 1, :], theta_t[:, m:m + 1], MAGIC,
                                             ALU.mult, ALU.add))
            own.need(a)
            G.tensor_scalar(ph[1], ph[1], -MAGIC, 2 * pi, ALU.add, ALU.mult).then_inc(s_turns, 1)
            for c in range(HALVES):
                pool.wait_ge(s_trig, 2 * c + 2)
                pool.wait_ge(s_poly, c + 1)
                if c:
                    pool.wait_ge(s_sum, 3 * c)
                W = M * HW
                ins = G.tensor_tensor(terms[:, W:2 * W].rearrange("p (m w) -> p m w", m=M), ph[c],
                                      poly[c].unsqueeze(1).broadcast_to([128, M, HW]), ALU.mult)
                ins.then_inc(s_im, 1)

            loop = Own(pool, loop_g)

            def keep(i):
                pool.wait_ge(a_x2, i + 1)
                G.tensor_copy(x2[:, bass.ds(i, 1), :].rearrange("p i d -> p (i d)"), x2_now[:]).then_inc(a_x2s, 1)
                pool.wait_ge(a_x2T, i + 2)
                xs = bass.ds(i * PT, PT)
                a = loop.mark(G.tensor_copy(x2h[:, xs], x2T[:, xs]))
                loop.need(a)
                G.tensor_tensor(x2l[:, xs], x2T[:, xs], x2h[:, xs], ALU.subtract).then_inc(a_x2s, 1)

            with pool.Fori(0, PAIRS) as i:
                loop.turn(i)
                keep(i)

            pool.wait_ge(a_x2s, 2 * PAIRS)
            G.tensor_tensor(x2b, x2, par("beta", PT).unsqueeze(1).broadcast_to([PT, PAIRS, D]),
                            ALU.add).then_inc(m_x2b, 1)
            for x in (hh, hl):
                G.memset(x.rearrange("p s f j t -> p (s f j) t")[:, :, PT:HT], 0.0).then_inc(m_pad, 1)

    return nc


def kernel(x, ctx_768, L0_attn_in_proj_w, L0_attn_conv_w, L0_attn_conv_b, L0_attn_theta, L0_attn_decay_slopes,
           L0_attn_anchor_slopes, L0_attn_score_scale, L0_attn_deriv_logits, L0_attn_norm_scale, L0_attn_W_re,
           L0_attn_W_im, L0_attn_out_proj_w, L0_xattn_Wq, L0_xattn_bq, L0_xattn_Wk, L0_xattn_bk, L0_xattn_Wv,
           L0_xattn_bv, L0_ffn_Wr, L0_ffn_br, L0_ffn_W1, L0_ffn_b1, L0_ffn_W2, L0_ffn_b2, L0_ffn_gamma,
           L0_ffn_beta):
    import concourse.bacc as bacc
    from concourse.bass_utils import run_bass_kernel_spmd

    def f32(a):
        return np.asarray(a)

    def rows(a):
        return np.broadcast_to(f32(a).reshape(1, -1), (128, f32(a).size))

    def pad(a):
        a = f32(a)
        return np.concatenate([a, np.zeros((128 - a.shape[0], a.shape[1]), a.dtype)])

    x = f32(x)
    w_in, cw, cb = f32(L0_attn_in_proj_w), f32(L0_attn_conv_w).reshape(TAPS, -1), f32(L0_attn_conv_b).reshape(1, -1)
    w_in, cw, cb = (np.concatenate([a[:, :2 * D], np.repeat(a[:, 2 * D:], H, axis=1)], axis=1) for a in (w_in, cw, cb))
    group = np.arange(128) // H
    pos = np.arange(L)
    dist = np.where((np.arange(128) < H * (K - 4))[:, None], (L - 1 - pos)[None], pos[None]).astype(np.float32)
    w_ri = np.concatenate([f32(L0_attn_W_re).reshape(H, M, H), f32(L0_attn_W_im).reshape(H, M, H)], axis=1)
    ns = f32(L0_attn_norm_scale).reshape(2, H, M).transpose(1, 0, 2).reshape(H, 2 * M)
    small = {
        "w_in": w_in,
        "conv_b": cb.reshape(3, 128).T,
        "theta": f32(L0_attn_theta).reshape(128, M),
        "slope": np.repeat(np.concatenate([f32(L0_attn_decay_slopes), f32(L0_attn_anchor_slopes)]), H)[:, None],
        "dist": dist,
        "score_scale": np.repeat(f32(L0_attn_score_scale), H)[:, None],
        "deriv": rows(L0_attn_deriv_logits),
        "norm_scale": np.tile(ns, (K, 1)),
        "w_ri": np.tile(w_ri.reshape(H, 2 * M * H), (K, 1)),
        "group_mask": (group[:, None] == group[None]).astype(np.float32),
        "ident": np.eye(128, dtype=np.float32),
        "w_out": f32(L0_attn_out_proj_w),
        "w_q": f32(L0_xattn_Wq),
        "b_q": f32(L0_xattn_bq)[:, None],
        "w_k": np.concatenate([f32(L0_xattn_Wk), f32(L0_xattn_bk)[None]]).T,
        "w_v": pad(np.concatenate([f32(L0_xattn_Wv), f32(L0_xattn_bv)[None]])),
        "w_r": f32(L0_ffn_Wr).T,
        "b_r": rows(L0_ffn_br),
        "gamma": rows(L0_ffn_gamma),
        "beta": rows(L0_ffn_beta),
        "b_1": f32(L0_ffn_b1).reshape(E * FC, 128).T,
        "b_2": pad(L0_ffn_b2),
        "iota": rows(np.arange(E, dtype=np.float32)),
    }
    ctx = f32(ctx_768)
    arrays = {
        "x_T": np.pad(x.transpose(2, 0, 1), ((0, 0), (0, 0), (TAPS - 1, 0))),
        "x_tok": x.reshape(PAIRS, PT, D).transpose(1, 0, 2),
        "ctx": ctx.reshape(B, KP, KC, DC),
        "ctx_T": ctx.reshape(B, KP, KC, DC).transpose(0, 3, 2, 1).reshape(B, DC, SK),
        "first": np.concatenate([small[name] for name, _ in FIRST], axis=1),
        "conv_w": cw.reshape(TAPS, 3, D).transpose(1, 0, 2).reshape(-1),
        "small": np.concatenate([small[name] for name, _ in SMALL], axis=1),
        "w_1": f32(L0_ffn_W1).transpose(0, 2, 1),
        "w_2": f32(L0_ffn_W2).reshape(E, D, FC, 128).transpose(0, 3, 2, 1).reshape(E, 128, FC * D),
    }
    arrays = {name: np.ascontiguousarray(a) for name, a in arrays.items()}
    nc = bacc.Bacc("TRN2", target_bir_lowering=False, num_devices=1)
    args = [nc.dram_tensor(name, a.shape, mybir.dt.from_np(a.dtype), kind="ExternalInput").ap()
            for name, a in arrays.items()]
    out = nc.dram_tensor("out", (PT, PAIRS, D), F32, kind="ExternalOutput").ap()
    decoder_kernel(nc, *args, out)
    ran = run_bass_kernel_spmd(nc, [arrays], core_ids=[0])
    return ran.results[0]["out"].transpose(1, 0, 2).reshape(B, L, D)
```

```python
from contextlib import ExitStack
from math import log, pi, sqrt

import numpy as np

import concourse.bass as bass
from concourse import mybir

ALU = mybir.AluOpType
ACT = mybir.ActivationFunctionType
AX = mybir.AxisListType
F32 = mybir.dt.float32
F16 = mybir.dt.float16
U32 = mybir.dt.uint32

B, L, D = 16, 56, 128
K, H, M = 32, 4, 4
TAPS = 4
SK, DC = 1500, 96
E, F = 8, 512
T = B * L
HALVES = 2
HB = B // HALVES
HW = HB * L
PAIRS = B // 2
PT = 2 * L
PPH = PAIRS // HALVES
GAP = 64
GT = GAP + L
KP, KC = 125, 12
SN = 500
SB = SK // SN
FC = F // 128
HT = 128
WS = 16.0
MAGIC = 1.5 * 2.0 ** 23
LN_EPS = 1e-5
V_DOWN = 20

FIRST = [("w_in", 3 * D), ("conv_b", 3), ("theta", M), ("slope", 1), ("dist", L), ("score_scale", 1), ("deriv", 3)]
SMALL = [("norm_scale", 2 * M), ("w_ri", 2 * M * H), ("group_mask", D), ("ident", D), ("w_out", D), ("w_q", D),
         ("b_q", 1), ("w_k", DC + 1), ("w_v", D), ("w_r", E), ("b_r", E), ("gamma", D), ("beta", D), ("b_1", E * FC),
         ("b_2", D), ("iota", E)]


def places(names):
    at, n = {}, 0
    for name, width in names:
        at[name] = (n, n + width)
        n += width
    return at, n


class Own:

    def __init__(self, eng, sem):
        self.eng, self.sem, self.base, self.n = eng, sem, 0, 0

    def turn(self, base):
        self.base, self.n = base, 0

    def mark(self, ins):
        ins.then_inc(self.sem, 1)
        self.n += 1
        return self.base + self.n

    def need(self, value):
        self.eng.wait_ge(self.sem, value)


def decoder_kernel(nc, x_T, x_tok, ctx, ctx_T, first, conv_w, small, w_1, w_2, out):
    with ExitStack() as stack:
        def sb(name, shape, dt=F32):
            return stack.enter_context(nc.sbuf_tensor(name, shape, dt))

        def sem(name):
            return stack.enter_context(nc.semaphore(name))

        bank = stack.enter_context(nc.psum_tensor("bank", [128, 8, 512], F32))

        at1, n1 = places(FIRST)
        at2, n2 = places(SMALL)
        first_sb = sb("first_sb", [128, n1])
        small_sb = sb("small_sb", [128, n2])
        convw_sb = sb("convw_sb", [128, 3, TAPS, D])

        def par(name, rows=128):
            a, b = at1[name] if name in at1 else at2[name]
            return (first_sb if name in at1 else small_sb)[0:rows, a:b]

        ident = par("ident")
        w_conv = sb("w_conv", [128, 3, TAPS, D])
        w_blk = sb("w_blk", [128, 2 * M, D])
        w_rin = sb("w_rin", [128, 2 * M, H])
        time_w = sb("time_w", [128, L])
        reset = sb("reset", [128, M * HW])
        cst = sb("cst", [128, 4])
        sp = sb("sp", [128, 4])
        dsm = sb("dsm", [128, 12])
        theta_t = sb("theta_t", [128, M])
        sbias = sb("sbias", [128, 1])
        qbias = sb("qbias", [128, 1])

        xpad = sb("xpad", [128, B, L + TAPS - 1])
        xtok = sb("xtok", [PT, PAIRS, D])
        x1 = sb("x1", [PT, PAIRS, D])
        x1T = sb("x1T", [128, T])
        rows_late = sb("rows_late", [128, 2 * PAIRS * D])
        x2 = rows_late[0:PT, 0:PAIRS * D].rearrange("p (i d) -> p i d", i=PAIRS)
        x2b = rows_late[0:PT, PAIRS * D:].rearrange("p (i d) -> p i d", i=PAIRS)
        turned_late = sb("turned_late", [128, 2 * T])
        x2T = turned_late[:, 0:T]
        x2h = turned_late[:, T:T + T // 2].bitcast(F16)
        x2l = turned_late[:, T + T // 2:].bitcast(F16)

        xv = sb("xv", [128, HALVES, HW])
        xg = sb("xg", [128, HALVES, HW])
        sc = sb("sc", [128, HALVES, HW])
        gate = sb("gate", [128, HALVES, HW])
        ph_0 = sb("ph_0", [128, M, HW])
        pc_0 = sb("pc_0", [128, M, HW])
        ph = [ph_0[:], turned_late[:, 0:M * HW].rearrange("p (m w) -> p m w", m=M)]
        pc = [pc_0[:], rows_late[:, 0:M * HW].rearrange("p (m w) -> p m w", m=M)]
        work = max((2 * M + 1) * HW, FC * PAIRS * HT)
        terms = sb("terms", [128, work])
        sums = sb("sums", [128, work])
        squares = sb("squares", [128, 2 * M * HW])
        y_gated = sb("y_gated", [128, HALVES, HW])
        poly = [sb("poly_0", [128, HW])[:], y_gated[:, 1, :]]

        ctx_slot = sb("ctx_slot", [KP, 2, 2, KC, DC])
        ctxT_slot = sb("ctxT_slot", [DC + 1, 2, 2, SK])
        q_sb = sb("q_sb", [128, PT])
        qk_sb = sb("qk_sb", [DC + 1, PT])
        neg_max = sb("neg_max", [128, 1])
        u_sb = sb("u_sb", [GT, DC + 1])
        uT_sb = sb("uT_sb", [DC + 1, PT])
        den = sb("den", [GT, 2])
        rden = sb("rden", [GT, 2])
        res = sb("res", [PT, D])
        x2_now = sb("x2_now", [PT, D])
        stat = sb("stat", [PT, PAIRS, 6])
        mv = sb("mv", [PT, PAIRS, 2])
        lnv = sb("lnv", [PT, PAIRS])
        rstd = sb("rstd", [PT, PAIRS])
        exp_sb = [squares[0:GT, s * SK:(s + 1) * SK] for s in range(2)]
        expT_sb = ph_0[0:KP].rearrange("p m w -> p (m w)")[:, 0:KC * GT].rearrange("p (c q) -> p c q", c=KC)

        w_raw = sb("w_raw", [128, 2, 2, F])
        w1h = sb("w1h", [128, 2, F], F16)
        w1l = sb("w1l", [128, 2, F], F16)
        w2h = sb("w2h", [128, 2, FC, D], F16)
        w2l = sb("w2l", [128, 2, FC, D], F16)
        hid = pc_0[:]
        nh = 2 * FC * PAIRS * HT
        hh = terms[:, 0:nh // 2].bitcast(F16).rearrange("p (s f j t) -> p s f j t", s=2, f=FC, j=PAIRS)
        hl = sums[:, 0:nh // 2].bitcast(F16).rearrange("p (s f j t) -> p s f j t", s=2, f=FC, j=PAIRS)
        carrier = sb("carrier", [128, 1])
        b1_now = sb("b1_now", [128, 2, FC])
        logit = sb("logit", [PT, PAIRS, E])
        top = sb("top", [PT, PAIRS, 8])
        topi = sb("topi", [PT, PAIRS, 8], U32)
        topf = sb("topf", [PT, PAIRS, 2])
        tsm = sb("tsm", [PT, 6, PAIRS])
        rw = sb("rw", [PT, PAIRS, E])
        rws = sb("rws", [PT, PAIRS, E])
        rwT = sb("rwT", [E, T])
        nmr = sb("nmr", [PT, PAIRS])
        rstd2 = sb("rstd2", [PT, PAIRS])
        acc = xtok

        s_in = sem("first_params_loaded")
        s_cw = [sem(f"conv_weights_loaded_{g}") for g in range(3)]
        s_xT = [sem(f"x_transposed_loaded_{c}") for c in range(HALVES)]
        s_par = sem("small_params_loaded")
        s_xtok = sem("x_tokens_loaded")
        s_ctx = [sem(f"ctx_loaded_{s}") for s in range(2)]
        s_ctxT = [sem(f"ctxT_loaded_{s}") for s in range(2)]
        s_w = [sem(f"expert_weights_loaded_{s}") for s in range(4)]
        s_cst = sem("constants_set")
        s_ones = sem("context_ones_set")
        s_convw = sem("conv_folded")
        s_z = sem("z_done")
        s_xv = sem("values_read")
        s_sc = sem("scores_read")
        s_warm = sem("ones_for_warming")
        s_score = sem("score_clipped")
        s_p = sem("score_exp")
        s_sp = sem("small_act")
        s_sd = sem("small_dve")
        s_gate = sem("gate_read")
        s_phase = sem("phase_reduced")
        s_cos = sem("cosines_done")
        s_sin = sem("sines_done")
        s_turns = sem("whole_turns_done")
        s_poly = sem("weighted_polynomial_done")
        s_im = sem("sin_terms_done")
        s_re = sem("re_sums_done")
        s_ims = sem("im_sums_done")
        s_sq = sem("squares_done")
        s_fold = sem("squares_folded")
        s_qx = sem("polynomial_part_ready")
        s_blk = sem("group_weights_ready")
        s_y = sem("y_done")
        s_ss = sem("square_sums_done")
        s_v = sem("variance_ready")
        s_f = sem("factor_ready")
        s_yg = sem("y_gated_ready")
        s_o = sem("mix_out_done")
        s_var = sem("mix_variance_ready")
        s_rstd = sem("mix_rstd_ready")
        s_x1 = sem("x1_ready")
        s_x1t = sem("x1_turned")
        s_x1T = sem("x1T_ready")
        own_v, own_a, own_g = sem("vector_own"), sem("scalar_own"), sem("gpsimd_own")
        loop_v, loop_a, loop_g = sem("vector_attend_own"), sem("scalar_attend_own"), sem("gpsimd_attend_own")
        a_q, a_qsb, a_qk, a_qksb = sem("q_done"), sem("q_read"), sem("qk_done"), sem("qk_read")
        a_s, a_max, a_exp, a_t = sem("scores_done"), sem("max_done"), sem("weights_done"), sem("weights_turned")
        a_et, a_pv, a_u = sem("turned_read"), sem("context_sum_done"), sem("context_sum_read")
        a_ut, a_utsb, a_r = sem("context_sum_turned"), sem("context_sum_turned_read"), sem("values_done")
        a_vr, a_rden = sem("values_read_off_psum"), sem("inverse_sum_ready")
        a_res, a_rstd, a_x2 = sem("attended_stats_ready"), sem("attend_rstd_ready"), sem("x2_ready")
        a_x2t, a_x2T, a_x2s = sem("x2_turned"), sem("x2T_ready"), sem("x2_split")
        m_wl = sem("expert_weights_split")
        m_log, m_e = sem("logits_done"), sem("routing_exp")
        m_rw, m_rt, m_rwT = (sem("router_weights_ready"), sem("router_weights_turned"),
                              sem("router_weights_T_ready"))
        m_l1, m_relu, m_hl = sem("hidden_done"), sem("relu_done"), sem("hidden_split")
        m_b1, m_x2b = sem("b1_ready"), sem("x2_plus_beta_ready")
        m_l2, m_acc = sem("expert_out_done"), sem("expert_out_added")
        m_pad = sem("hidden_pads_set")
        mo_v = sem("vector_experts_own")
        f_bias = sem("final_bias_ready")
        f_last = sem("final_last_ready")
        f_var2, f_rstd2 = sem("last_variance_ready"), sem("last_rstd_ready")
        f_scaled, f_acc = sem("weighted_outs_ready"), sem("weighted_outs_added")
        m_last = sem("last_expert_out_done")
        f_var, f_rstd, f_out = sem("final_variance_ready"), sem("final_rstd_ready"), sem("final_ready")
        s_store = sem("stored")

        block = stack.enter_context(nc.Block())

        VALUE, GATE, SCORE = range(3)
        Z_ORDER = [(0, VALUE), (0, SCORE), (1, VALUE), (1, SCORE), (0, GATE), (1, GATE)]
        Z = {cg: n for n, cg in enumerate(Z_ORDER)}
        Y_BANK, SS_BANK, O_BANK, T_BANK = (6, 4), (7, 5), (3, 6), (6, 6)

        def part(e, n):
            return (n % FC, n // FC) if isinstance(e, int) and e in (0, E - 1) else (n // HALVES, n % HALVES)

        LAST_BANK = (6, 7, 0, 1)
        LAST_QUARTERS = tuple(range(2 * q, 2 * q + 2) for q in range(4))
        LAST_PARTS = (range(0, 2), range(2, PPH), range(PPH, PAIRS))

        C_EPS, C_HALFPI, C_FACTOR, C_ONE = range(4)

        @block.sync
        def _(sp_):
            sp_.dma_start(first_sb[:], first).then_inc(s_in, 16)

            def taps(g):
                sp_.dma_start(convw_sb[:, g].rearrange("p k n -> p (k n)"),
                              conv_w[g * TAPS * D:(g + 1) * TAPS * D].partition_broadcast(128)).then_inc(s_cw[g], 16)

            taps(VALUE)

            def tokens(c):
                sp_.dma_start(xpad[:, c * HB:(c + 1) * HB], x_T[:, c * HB:(c + 1) * HB]).then_inc(s_xT[c], 16)

            tokens(0)
            taps(SCORE)
            tokens(1)
            taps(GATE)
            sp_.dma_start(small_sb[:], small).then_inc(s_par, 16)
            sp_.dma_start(xtok[:], x_tok).then_inc(s_xtok, 16)

            def ctx_pair(i, s):
                for j in range(2):
                    sp_.dma_start(ctxT_slot[0:DC, s, j, :], ctx_T[2 * i + j]).then_inc(s_ctxT[s], 16)

            def ctx_rows(i, s):
                for j in range(2):
                    sp_.dma_start(ctx_slot[:, s, j],
                                  ctx[2 * i + j]).then_inc(s_ctx[s], 16)

            def load_w(which, e, s):
                src = (w_1, w_2)[which][e]
                sp_.dma_start(w_raw[:, s, which, :], src).then_inc(s_w[2 * which + s], 16)

            for s in range(2):
                ctx_pair(s, s)
                ctx_rows(s, s)
            for s in range(2):
                load_w(0, s, s)
                load_w(1, s, s)
            def next_ctx(i, s):
                sp_.wait_ge(a_s, i + 2)
                ctx_pair(i + 3, 1 - s)
                sp_.wait_ge(a_pv, i + 1)
                ctx_rows(i + 2, s)

            sp_.wait_ge(a_s, 1)
            ctx_pair(2, 0)
            with sp_.Fori(0, PAIRS // 2 - 2) as t:
                next_ctx(2 * t, 0)
                next_ctx(2 * t + 1, 1)
            next_ctx(PAIRS - 4, 0)
            sp_.wait_ge(a_pv, PAIRS - 2)
            ctx_rows(PAIRS - 1, 1)
            with sp_.Fori(0, E // 2 - 1) as t:
                for s in range(2):
                    for which in range(2):
                        sp_.wait_ge(m_wl, 4 * t + 2 * s + 1 + which)
                        load_w(which, 2 * t + s + 2, s)
            for half in range(HALVES):
                sp_.wait_ge(f_out, 2 + half)
                if half:
                    sp_.wait_ge(f_last, 1)
                w = slice(half * PPH, (half + 1) * PPH)
                sp_.dma_start(out[:, w, :], x1[:, w, :]).then_inc(s_store, 16)
            sp_.wait_ge(s_store, 16 * HALVES)

        @block.tensor
        def _(pe):
            def keep_warm(n, to=O_BANK[0]):
                for _ in range(n):
                    mm = pe.matmul(bank[:, to, 0:HW // 2], reset[:, 0:D], reset[:, 0:HW // 2], start=True,
                                   stop=True)
                return mm

            pe.wait_ge(s_warm, 1)
            keep_warm(4).then_inc(s_warm, 1)
            for c, g in Z_ORDER:
                if g == VALUE:
                    pe.wait_ge(s_xT[c], 16)
                pe.wait_ge(s_convw, (VALUE, SCORE, GATE).index(g) + 1)
                for k in range(TAPS):
                    mm = pe.matmul(bank[:, Z[c, g], 0:HW], w_conv[:, g, k, :],
                                   xpad[:, HB * c:HB * (c + 1), k:k + L], start=(k == 0), stop=(k == TAPS - 1))
                mm.then_inc(s_z, 1)

            def group_sums(c, n):
                pe.wait_ge(s_blk, 1)
                if c and n == 0:
                    pe.wait_ge(s_gate, 2)
                for j in range(n * M, n * M + M):
                    if j % 2 == 0:
                        pe.wait_ge((s_re, s_ims)[n], 2 * c + (j % M) // 2 + 1)
                    mm = pe.matmul(bank[:, Y_BANK[c], 0:HW], w_blk[:, j, :], sums[:, j * HW:(j + 1) * HW],
                                   start=(j == 0), stop=(j == 2 * M - 1))
                mm.then_inc(s_y, 1)

            def group_squares(c, first, last):
                for j in range(first, last):
                    n, m = divmod(j, M // 2)
                    if m == 0:
                        pe.wait_ge(s_fold, 2 * c + 1 + n)
                    mm = pe.matmul(bank[:, SS_BANK[c], 0:HW], par("group_mask"),
                                   squares[:, (n * M + m) * HW:(n * M + m + 1) * HW],
                                   start=(j == 0), stop=(j == M - 1))
                if last == M:
                    mm.then_inc(s_ss, 1)

            def project_out(c):
                pe.wait_ge(s_yg, c + 1)
                for j in range(PPH):
                    mm = pe.matmul(bank[0:PT, O_BANK[c], j * D:(j + 1) * D], y_gated[:, c, j * PT:(j + 1) * PT],
                                   par("w_out"), start=True, stop=True)
                mm.then_inc(s_o, 1)

            def turn_x1(c):
                pe.wait_ge(s_x1, c + 1)
                for j in range(PPH):
                    mm = pe.transpose(bank[:, T_BANK[c], j * PT:(j + 1) * PT], x1[:, c * PPH + j, :],
                                      ident[0:PT, 0:PT])
                mm.then_inc(s_x1t, 1)

            pe.wait_ge(s_phase, 1)
            keep_warm(8, to=SS_BANK[0])
            group_sums(0, 0)
            group_sums(0, 1)
            group_squares(0, 0, M)
            group_sums(1, 0)
            project_out(0)
            group_sums(1, 1)

            def query(i):
                pe.matmul(bank[:, 7, 0:PT], par("w_q"), x1T[:, bass.ds(i * PT, PT)],
                          start=True, stop=True).then_inc(a_q, 1)

            def query_keys(i):
                pe.wait_ge(a_qsb, i + 1)
                pe.matmul(bank[0:DC + 1, 7, 128:128 + PT], par("w_k"), q_sb[:], start=True, stop=True).then_inc(a_qk, 1)

            def scores(i, s, turn):
                pe.wait_ge(a_qksb, i + 1)
                pe.wait_ge(s_ctxT[s], turn)
                for j, rows in ((0, GAP), (1, L)):
                    for n in range(SB):
                        mm = pe.matmul(bank[j * GAP:j * GAP + rows, n, 0:SN], qk_sb[:, j * L:j * L + rows],
                                       ctxT_slot[:, s, j, n * SN:(n + 1) * SN], start=True, stop=True)
                mm.then_inc(a_s, 1)

            def turn_weights(s, third):
                for c in range(4 * third, 4 * third + 4):
                    mm = pe.transpose(bank[0:KP, 3 + third, (c % 4) * GT:(c % 4 + 1) * GT],
                                      exp_sb[s][:, c * KP:(c + 1) * KP], ident[0:GT, 0:GT])
                mm.then_inc(a_t, 1)

            def context_sum(i, s, turn):
                pe.wait_ge(a_et, 3 * i + 3)
                pe.wait_ge(s_ctx[s], turn)
                for j, rows in ((0, GAP), (1, L)):
                    for c in range(KC):
                        mm = pe.matmul(bank[j * GAP:j * GAP + rows, 6, 0:DC],
                                       expT_sb[:, c, j * GAP:j * GAP + rows], ctx_slot[:, s, j, c, :],
                                       start=(c == 0), stop=(c == KC - 1))
                mm.then_inc(a_pv, 1)

            def turn_sum(i):
                pe.wait_ge(a_u, i + 1)
                pe.transpose(bank[0:DC + 1, 7, 256:256 + GT], u_sb[:], ident[0:GT, 0:GT]).then_inc(a_ut, 1)

            def values(i):
                pe.wait_ge(a_utsb, i + 1)
                pe.matmul(bank[0:PT, 6, 128:128 + D], uT_sb[:], par("w_v", DC + 1), start=True,
                          stop=True).then_inc(a_r, 1)

            def turn_x2(i):
                pe.wait_ge(a_x2, i + 1)
                pe.transpose(bank[:, 7, 384:384 + PT], x2_now[:], ident[0:PT, 0:PT]).then_inc(a_x2t, 1)

            def attend_turn(i, s, ctxT_next, ctx_last, stage=2, more=True, last=False):
                pe.wait_ge(a_exp, i + 1)
                if not last:
                    scores(i + 1, 1 - s, ctxT_next)
                if stage == 1:
                    turn_x1(1)
                if more:
                    if stage == 2:
                        pe.wait_ge(a_x2T, i - 1)
                    query(i + 2)
                if stage:
                    if stage == 1:
                        pe.wait_ge(s_x1T, 2)
                    if stage == 2:
                        pe.wait_ge(a_vr, i - 1)
                    context_sum(i - 1, 1 - s, ctx_last)
                if more:
                    query_keys(i + 2)
                turn_weights(s, 0)
                turn_weights(s, 1)
                if stage:
                    if more:
                        pe.wait_ge(a_qksb, i + 3)
                    turn_sum(i - 1)
                turn_weights(s, 2)
                if stage:
                    values(i - 1)
                if stage == 2:
                    turn_x2(i - 2)

            group_squares(1, 0, 1)
            turn_x1(0)
            group_squares(1, 1, 2)
            pe.wait_ge(s_x1T, 1)
            query(0)
            group_squares(1, 2, 3)
            query_keys(0)
            group_squares(1, 3, M)
            pe.wait_ge(s_ones, 1)
            scores(0, 0, 32)
            query(1)
            project_out(1)
            query_keys(1)
            pe.wait_ge(a_qksb, 2)
            keep_warm(3)
            attend_turn(0, 0, 32, None, stage=0)
            pe.wait_ge(a_qksb, 3)
            attend_turn(1, 1, 64, 32, stage=1)
            with pe.Fori(1, PAIRS // 2 - 1) as t:
                attend_turn(2 * t, 0, 32 * t + 32, 32 * t)
                attend_turn(2 * t + 1, 1, 32 * t + 64, 32 * t + 32)
            attend_turn(PAIRS - 2, 0, 16 * PAIRS, 16 * PAIRS - 32, more=False)
            attend_turn(PAIRS - 1, 1, None, 16 * PAIRS, more=False, last=True)

            def hidden(e, s, n):
                f, c = part(e, n)
                for k, (w, x) in enumerate(((w1h, x2h), (w1h, x2l), (w1l, x2h))):
                    mm = pe.matmul(bank[:, n % 4, 0:HW], w[:, s, f * 128:(f + 1) * 128],
                                   x[:, c * HW:(c + 1) * HW], start=(k == 0), stop=(k == 2))
                mm.then_inc(m_l1, 1)

            def outs(e, s, n, last=False):
                half = n // 2
                if n == 0:
                    pe.wait_ge(m_wl, 2 * e + 2)
                if last and n % 2 == 0:
                    pe.wait_ge(m_hl, 8 * e + 4 + 4 * half)
                elif n == 0:
                    pe.wait_ge(m_hl, 8 * e + 8)
                if last and n < 2:
                    pe.wait_ge(m_acc, 2 * e + 1 + n)
                elif not last and n % 2 == 0:
                    pe.wait_ge(m_acc, 2 * e + 1 + half)
                for i in (2 * n, 2 * n + 1):
                    to, j = (LAST_BANK[n], i % 2) if last else (4 + 2 * s + half, i % PPH)
                    for f in range(FC):
                        for k, (h_, w_) in enumerate(((hh, w2h), (hh, w2l), (hl, w2h))):
                            mm = pe.matmul(bank[:, to, j * D:(j + 1) * D], h_[:, s, f, i, :],
                                           w_[:, s, f, :], start=(f == 0 and k == 0), stop=(f == FC - 1 and k == 2))
                if last:
                    mm.then_inc(m_last, 1)
                elif n % 2:
                    mm.then_inc(m_l2, 1)

            def logits(i):
                return pe.matmul(bank[0:PT, 4, i * E:(i + 1) * E], x2T[:, i * PT:(i + 1) * PT], par("w_r"),
                                 start=True, stop=True)

            pe.wait_ge(m_wl, 1)
            pe.wait_ge(a_x2s, PAIRS)
            hidden(0, 0, 0)
            hidden(0, 0, 1)
            pe.wait_ge(a_vr, PAIRS - 1)
            context_sum(PAIRS - 1, 1, 16 * PAIRS)
            pe.wait_ge(a_x2T, PAIRS - 1)
            turn_x2(PAIRS - 2)
            hidden(0, 0, 2)
            keep_warm(2, 5)
            pe.wait_ge(a_x2T, PAIRS)
            turn_sum(PAIRS - 1)
            hidden(0, 0, 3)
            values(PAIRS - 1)
            for i in range(PAIRS - 1):
                logits(i)
            keep_warm(2, 5)
            turn_x2(PAIRS - 1)
            keep_warm(1, 5)
            pe.wait_ge(a_x2T, PAIRS + 1)
            logits(PAIRS - 1).then_inc(m_log, 1)
            keep_warm(2, 5)
            pe.wait_ge(a_x2s, 2 * PAIRS)
            for n in range(4, 8):
                pe.wait_ge(m_relu, n - 3)
                hidden(0, 0, n)
            pe.wait_ge(m_rw, 1)
            for i in range(PAIRS):
                mm = pe.transpose(bank[0:E, 4 + i // PPH, (i % PPH) * PT:(i % PPH + 1) * PT], rw[:, i, :],
                                  ident[0:PT, 0:PT])
            mm.then_inc(m_rt, 1)
            keep_warm(3, 7)
            for i in range(PAIRS):
                if i % PPH == 0:
                    pe.wait_ge(m_rwT, i // PPH + 1)
                mm = pe.matmul(bank[0:PT, 6 + i // PPH, (i % PPH) * D:(i % PPH + 1) * D],
                               rwT[:, i * PT:(i + 1) * PT], par("b_2", E), start=True, stop=True)
            mm.then_inc(m_l2, 2)

            def two_hidden(e, s, n):
                for k in (2 * n, 2 * n + 1):
                    pe.wait_ge(m_relu, 8 * e + k - 3)
                    hidden(e, s, k)

            def expert_turn(e, s):
                pe.wait_ge(m_wl, 2 * e + 3)
                for n in range(4):
                    two_hidden(e + 1, 1 - s, n)
                    outs(e, s, n)

            pe.wait_ge(m_pad, 2)
            with pe.Fori(0, E // 2 - 1) as t:
                expert_turn(2 * t, 0)
                expert_turn(2 * t + 1, 1)
            pe.wait_ge(m_wl, 2 * E - 1)
            two_hidden(E - 1, 1, 0)
            outs(E - 2, 0, 0)
            two_hidden(E - 1, 1, 1)
            outs(E - 2, 0, 1)
            two_hidden(E - 1, 1, 2)
            outs(E - 1, 1, 0, last=True)
            two_hidden(E - 1, 1, 3)
            outs(E - 1, 1, 1, last=True)
            outs(E - 2, 0, 2)
            outs(E - 2, 0, 3)
            outs(E - 1, 1, 2, last=True)
            outs(E - 1, 1, 3, last=True)

        @block.scalar
        def _(act):
            own = Own(act, own_a)
            act.preload_act_table_set("natural_log_exp_and_others")
            act.wait_ge(s_sd, 1)
            nc.scalar.activation(sp[:, 1:2], sp[:, 0:1], ACT.Exp, scale=-1.0).then_inc(s_sp, 1)
            nc.scalar.activation(dsm[:, 4:7], dsm[:, 0:3], ACT.Exp).then_inc(s_sp, 1)
            act.wait_ge(s_sp, 1)
            act.wait_ge(s_cst, 1)
            nc.scalar.activation(sp[:, 2:3], sp[:, 1:2], ACT.Ln, bias=cst[:, C_ONE:C_ONE + 1]).then_inc(s_sp, 1)
            act.wait_ge(s_sd, 2)
            nc.scalar.activation(time_w[:], par("dist"), ACT.Exp, scale=sp[:, 3:4]).then_inc(s_sp, 1)
            act.wait_ge(s_in, 16)

            def read_values(c):
                act.wait_ge(s_z, Z[c, VALUE] + 1)
                nc.scalar.activation(xv[:, c, :], bank[:, Z[c, VALUE], 0:HW], ACT.Identity,
                                     bias=par("conv_b")[:, 0:1]).then_inc(s_xv, 1)

            def read_scores(c):
                act.wait_ge(s_z, Z[c, SCORE] + 1)
                act.wait_ge(s_sd, 3)
                nc.scalar.activation(sc[:, c, :], bank[:, Z[c, SCORE], 0:HW], ACT.Identity, bias=sbias[:],
                                     scale=par("score_scale")).then_inc(s_sc, 1)

            def exponentials(c):
                act.wait_ge(s_score, c + 1)
                nc.scalar.activation(sc[:, c, :], sc[:, c, :], ACT.Exp).then_inc(s_p, 1)

            def read_gates(c):
                act.wait_ge(s_z, Z[c, GATE] + 1)
                gr = own.mark(nc.scalar.activation(xg[:, c, :], bank[:, Z[c, GATE], 0:HW], ACT.Identity,
                                                   bias=par("conv_b")[:, 1:2]))
                own.need(gr)
                nc.scalar.activation(gate[:, c, :], xg[:, c, :], ACT.Tanh, scale=0.5).then_inc(s_gate, 1)

            def cosines(c):
                for k in range(2):
                    m = slice(2 * k, 2 * k + 2)
                    act.wait_ge(s_phase, 2 * c + k + 1)
                    a = own.mark(nc.scalar.activation(pc[c][:, m, :], ph[c][:, m, :], ACT.Abs))
                    own.need(a)
                    nc.scalar.activation(pc[c][:, m, :], pc[c][:, m, :], ACT.Sin, scale=-1.0,
                                         bias=cst[:, C_HALFPI:C_HALFPI + 1]).then_inc(s_cos, 1)

            def sines(c):
                for k in range(2):
                    m = slice(2 * k, 2 * k + 2)
                    nc.scalar.activation(ph[c][:, m, :], ph[c][:, m, :], ACT.Sin).then_inc(s_sin, 1)

            def square(c, n):
                act.wait_ge((s_re, s_ims)[n], 2 * c + 2)
                if c:
                    act.wait_ge(s_ss, c)
                w = slice(n * M * HW, (n + 1) * M * HW)
                nc.scalar.activation(squares[:, w], sums[:, w], ACT.Square).then_inc(s_sq, 1)

            def factor(c):
                act.wait_ge(s_v, c + 1)
                a = own.mark(nc.scalar.activation(sc[:, c, :], sc[:, c, :], ACT.Ln, scale=2.0 ** -V_DOWN))
                own.need(a)
                nc.scalar.activation(sc[:, c, :], sc[:, c, :], ACT.Exp, scale=-0.5,
                                     bias=cst[:, C_FACTOR:C_FACTOR + 1]).then_inc(s_f, 1)

            def inv_std(own_, var, tmp, to, done):
                a = own_.mark(nc.scalar.activation(tmp, var, ACT.Ln, bias=cst[0:PT, C_EPS:C_EPS + 1]))
                own_.need(a)
                nc.scalar.activation(to, tmp, ACT.Exp, scale=-0.5).then_inc(done, 1)

            def mix_inv_std(c):
                w = slice(c * PPH, (c + 1) * PPH)
                act.wait_ge(s_var, c + 1)
                inv_std(own, mv[:, w, 1], lnv[:, w], rstd[:, w], s_rstd)

            def x1T_copy(c):
                act.wait_ge(s_x1t, c + 1)
                nc.scalar.copy(x1T[:, c * HW:(c + 1) * HW], bank[:, T_BANK[c], 0:HW]).then_inc(s_x1T, 1)

            read_values(0)
            read_scores(0)
            read_values(1)
            exponentials(0)
            act.preload_act_table_set("trig_and_small")
            cosines(0)
            sines(0)
            read_scores(1)
            cosines(1)
            sines(1)
            act.preload_act_table_set("exp_and_others")
            exponentials(1)
            square(0, 0)
            square(0, 1)
            read_gates(0)
            read_gates(1)
            act.preload_act_table_set("natural_log_exp_and_others")
            factor(0)
            square(1, 0)
            square(1, 1)
            mix_inv_std(0)
            x1T_copy(0)

            loop = Own(act, loop_a)

            def queries(i):
                act.wait_ge(a_q, i + 1)
                nc.scalar.activation(q_sb[:], bank[:, 7, 0:PT], ACT.Identity, bias=qbias[:],
                                     scale=1.0 / sqrt(D)).then_inc(a_qsb, 1)

            def weights_exp(i, s):
                act.wait_ge(a_max, i + 1)
                nc.scalar.activation(exp_sb[s].rearrange("q (n k) -> q n k", n=SB), bank[0:GT, 0:SB, 0:SN], ACT.Exp,
                                     bias=neg_max[0:GT, :], accum_out=den[:, s:s + 1]).then_inc(a_exp, 1)

            def turned_sum(i):
                act.wait_ge(a_ut, i + 1)
                nc.scalar.copy(uT_sb[:].rearrange("d (j l) -> d j l", j=2),
                               bank[0:DC + 1, 7, 256:256 + 2 * GAP].rearrange("d (j l) -> d j l", j=2)[:, :, 0:L]
                               ).then_inc(a_utsb, 1)

            def attended_inv_std(i):
                act.wait_ge(a_res, i + 1)
                inv_std(loop, mv[:, 0, 1:2], lnv[:, 0:1], rstd[:, 0:1], a_rstd)

            def attend_turn(i, s, first=False, second=False, more=True, last=False):
                if second:
                    x1T_copy(1)
                if more:
                    queries(i + 2)
                if not last:
                    weights_exp(i + 1, 1 - s)
                act.wait_ge(a_t, 3 * i + 1)
                nc.scalar.copy(expT_sb[:, 0:4, :], bank[0:KP, 3, 0:4 * GT].rearrange("p (c q) -> p c q", c=4)
                               ).then_inc(a_et, 1)
                if not first:
                    turned_sum(i - 1)
                    attended_inv_std(i - 1)

            act.wait_ge(s_sd, 4)
            queries(0)
            factor(1)
            queries(1)
            weights_exp(0, 0)
            mix_inv_std(1)
            attend_turn(0, 0, first=True)
            attend_turn(1, 1, second=True)
            with act.Fori(1, PAIRS // 2 - 1) as t:
                loop.turn(2 * t - 1)
                attend_turn(2 * t, 0)
                attend_turn(2 * t + 1, 1)
            loop.turn(PAIRS - 3)
            attend_turn(PAIRS - 2, 0, more=False)
            attend_turn(PAIRS - 1, 1, more=False, last=True)

            def relu(e, s, n):
                f, c = part(e, n)
                if n == 0:
                    act.wait_ge(m_b1, e + 1)
                act.wait_ge(m_l1, 8 * e + n + 1)
                nc.scalar.activation(hh[:, s, f, c * PPH:(c + 1) * PPH, 0:PT], bank[:, n % 4, 0:HW]
                                     .rearrange("p (j t) -> p j t", j=PPH), ACT.Relu, scale=1.0 / WS,
                                     bias=b1_now[:, s, f:f + 1])

            def relu_again(e, s, n, wait=True):
                f, c = part(e, n)
                if wait:
                    act.wait_ge(m_hl, 8 * e + n - 3)
                nc.scalar.activation(hid[:, n % 4, :], bank[:, n % 4, 0:HW], ACT.Relu, scale=1.0 / WS,
                                     bias=b1_now[:, s, f:f + 1]).then_inc(m_relu, 1)

            def b1_copy(e, s):
                a = at2["b_1"][0]
                nc.scalar.copy(b1_now[:, s, :], small_sb[:, bass.ds(a + FC * e, FC)]).then_inc(m_b1, 1)

            def first_relu(n):
                relu(0, 0, n)
                relu_again(0, 0, n, wait=n > 3)

            b1_copy(0, 0)
            first_relu(0)
            first_relu(1)
            turned_sum(PAIRS - 1)
            first_relu(2)
            attended_inv_std(PAIRS - 1)
            first_relu(3)
            act.wait_ge(m_e, 1)
            nc.scalar.activation(tsm[:, 1, :], tsm[:, 0, :], ACT.Exp).then_inc(m_e, 1)
            for n in range(4, 8):
                first_relu(n)

            def expert_turn(e, s):
                b1_copy(e, s)
                for n in range(2 * FC):
                    if n == 0:
                        act.wait_ge(m_l2, 2 * e)
                    relu(e, s, n)
                    relu_again(e, s, n)

            with act.Fori(0, E // 2 - 1) as t:
                expert_turn(2 * t + 1, 1)
                expert_turn(2 * t + 2, 0)
            expert_turn(E - 1, 1)

            def final_inv_std(n, second):
                tiles = LAST_QUARTERS[n] if second else LAST_PARTS[n]
                w = slice(tiles[0], tiles[-1] + 1)
                act.wait_ge(f_var2 if second else f_var, n + 1)
                inv_std(own, mv[:, w, 1], lnv[:, w], rstd2[:, w] if second else rstd[:, w],
                        f_rstd2 if second else f_rstd)

            def final_norm(q):
                act.wait_ge(f_bias, q + 1)
                for j in LAST_QUARTERS[q]:
                    ins = nc.scalar.activation(x1[:, j, :], acc[:, j, :], ACT.Identity, bias=nmr[:, j:j + 1],
                                               scale=rstd2[:, j:j + 1])
                ins.then_inc(f_out, 1)

            def weighted_outs(q):
                act.wait_ge(m_l2, 2 * (E - 2) + 4)
                for j in (2 * q, 2 * q + 1):
                    ins = nc.scalar.activation(x1[:, j, :], bank[0:PT, 5, (j % PPH) * D:(j % PPH + 1) * D],
                                               ACT.Identity, scale=rws[:, j, E - 2:E - 1])
                ins.then_inc(f_scaled, 1)

            final_inv_std(0, False)
            final_inv_std(1, False)
            act.wait_ge(m_rw, 2)
            weighted_outs(2)
            final_inv_std(0, True)
            weighted_outs(3)
            final_norm(0)
            final_inv_std(1, True)
            final_inv_std(2, False)
            final_norm(1)
            final_inv_std(2, True)
            final_inv_std(3, True)
            final_norm(2)

        @block.vector
        def _(dve):
            own = Own(dve, own_v)
            V = nc.vector
            V.memset(reset[:, 0:HW], 1.0).then_inc(s_warm, 1)
            own.mark(V.memset(reset[:, HW:], 1.0))
            V.memset(u_sb[:, DC:], 1.0)
            V.memset(cst[:, C_EPS:C_EPS + 1], LN_EPS)
            V.memset(cst[:, C_HALFPI:C_HALFPI + 1], pi / 2)
            V.memset(cst[:, C_FACTOR:C_FACTOR + 1], -0.5 * V_DOWN * log(2.0) - log(2.0))
            V.memset(cst[:, C_ONE:C_ONE + 1], 1.0).then_inc(s_cst, 1)
            def fold(g):
                dve.wait_ge(s_cw[g], 16)
                V.tensor_tensor(w_conv[:, g], par("w_in")[:, g * D:(g + 1) * D].unsqueeze(1)
                                .broadcast_to([128, TAPS, D]), convw_sb[:, g], ALU.mult).then_inc(s_convw, 1)

            dve.wait_ge(s_in, 16)
            fold(VALUE)
            own.mark(V.scalar_tensor_tensor(sp[:, 0:1], par("slope"), -1.0, par("slope"), ALU.mult, ALU.max))
            a = own.mark(V.tensor_reduce(dsm[:, 3:4], par("deriv"), AX.X, ALU.max))
            own.need(a)
            V.tensor_scalar(dsm[:, 0:3], par("deriv"), dsm[:, 3:4], None, ALU.subtract).then_inc(s_sd, 1)
            own.mark(V.tensor_scalar(theta_t[:], par("theta"), 1.0 / (2 * pi), None, ALU.mult))
            dve.wait_ge(s_sp, 3)
            a = own.mark(V.scalar_tensor_tensor(sp[:, 3:4], par("slope"), 0.0, sp[:, 2:3], ALU.max, ALU.add))
            own.need(a)
            V.tensor_scalar(sp[:, 3:4], sp[:, 3:4], -1.0, None, ALU.mult).then_inc(s_sd, 1)
            V.tensor_tensor(sbias[:], par("conv_b")[:, 2:3], par("score_scale"), ALU.mult).then_inc(s_sd, 1)
            a = own.mark(V.tensor_reduce(dsm[:, 7:8], dsm[:, 4:7], AX.X, ALU.add))
            own.need(a)
            a = own.mark(V.reciprocal(dsm[:, 7:8], dsm[:, 7:8]))
            own.need(a)
            a = own.mark(V.tensor_scalar(dsm[:, 8:11], dsm[:, 4:7], dsm[:, 7:8], None, ALU.mult))
            own.need(a)
            a = own.mark(V.tensor_scalar(dsm[:, 11:12], dsm[:, 10:11], -1.0, None, ALU.mult))
            fold(SCORE)
            fold(GATE)
            own.need(1)
            dve.wait_ge(s_warm, 2)
            own.mark(V.memset(reset[:].rearrange("p (n l) -> p n l", l=L)[:, :, 0:1], 0.0))
            dve.wait_ge(s_par, 16)
            V.tensor_scalar(qbias[:], par("b_q"), 1.0 / sqrt(D), None, ALU.mult).then_inc(s_sd, 1)
            a = own.mark(V.tensor_tensor(w_rin[:], par("w_ri").rearrange("p (j h) -> p j h", j=2 * M),
                                         par("norm_scale").unsqueeze(2).broadcast_to([128, 2 * M, H]), ALU.mult))
            own.need(a)
            for j in range(2 * M):
                ins = V.tensor_tensor(w_blk[:, j, :].rearrange("p (k h) -> p k h", k=K),
                                      w_rin[:, j, :].unsqueeze(1).broadcast_to([128, K, H]),
                                      par("group_mask").rearrange("p (k h) -> p k h", k=K), ALU.mult)
            ins.then_inc(s_blk, 1)

            W = M * HW

            def clip(c):
                dve.wait_ge(s_sc, c + 1)
                V.tensor_scalar(sc[:, c, :], sc[:, c, :], 20.0, -20.0, ALU.min, ALU.max).then_inc(s_score, 1)

            def gates(c):
                dve.wait_ge(s_gate, c + 1)
                own.mark(V.scalar_tensor_tensor(gate[:, c, :], gate[:, c, :], 1.0, xg[:, c, :], ALU.add, ALU.mult))

            def weights(c):
                pw = terms[:, 2 * W:2 * W + HW]
                q0 = poly[c]
                if c == 0:
                    a = own.mark(V.tensor_scalar(q0, xv[:, c, :], dsm[:, 11:12], dsm[:, 9:10], ALU.mult, ALU.add))
                    own.need(a)
                    V.tensor_tensor(q0, q0, xv[:, c, :], ALU.mult)
                dve.wait_ge(s_p, c + 1)
                dve.wait_ge(s_sp, 4)
                b = own.mark(V.tensor_tensor(pw.rearrange("p (b l) -> p b l", b=HB),
                                             sc[:, c, :].rearrange("p (b l) -> p b l", b=HB),
                                             time_w[:].unsqueeze(1).broadcast_to([128, HB, L]), ALU.mult))
                own.need(b)
                if c:
                    dve.wait_ge(s_qx, 1)
                V.scalar_tensor_tensor(q0, q0, dsm[:, 8:9], pw, ALU.add, ALU.mult).then_inc(s_poly, 1)

            def phases(c, k, between=None):
                part_ = ph[c][:, 2 * k:2 * k + 2, :]
                if c == 0:
                    if k == 0:
                        dve.wait_ge(s_xv, 1)
                    for m in (2 * k, 2 * k + 1):
                        a = own.mark(V.tensor_scalar(ph[c][:, m, :], xv[:, c, :], theta_t[:, m:m + 1], MAGIC,
                                                     ALU.mult, ALU.add))
                    own.need(a)
                    a = own.mark(V.tensor_scalar(part_, part_, -MAGIC, 2 * pi, ALU.add, ALU.mult))
                    own.need(a)
                for m in (2 * k, 2 * k + 1):
                    a = own.mark(V.scalar_tensor_tensor(ph[c][:, m, :], xv[:, c, :], par("theta")[:, m:m + 1],
                                                        ph[c][:, m, :], ALU.mult, ALU.subtract))
                if between:
                    between()
                own.need(a)
                V.tensor_scalar(part_, part_, 3.1415925, -3.1415925, ALU.min, ALU.max).then_inc(s_phase, 1)

            W2 = 2 * HW

            def cos_terms(c, k):
                dve.wait_ge(s_cos, 2 * c + k + 1)
                dve.wait_ge(s_poly, c + 1)
                return own.mark(V.tensor_tensor(terms[:, k * W2:(k + 1) * W2].rearrange("p (m w) -> p m w", m=2),
                                                pc[c][:, 2 * k:2 * k + 2, :],
                                                poly[c].unsqueeze(1).broadcast_to([128, 2, HW]), ALU.mult))

            def scan(at, k):
                w = slice(at + k * W2, at + (k + 1) * W2)
                return V.tensor_tensor_scan(sums[:, w], reset[:, 0:W2], terms[:, w], 0.0, ALU.mult, ALU.add)

            def scan_re(c, terms_ready):
                for k in range(2):
                    own.need(terms_ready[k])
                    if c and k == 0:
                        dve.wait_ge(s_y, 2 * c - 1)
                        dve.wait_ge(s_sq, 2 * c - 1)
                    scan(0, k).then_inc(s_re, 1)
                return own.mark(V.tensor_tensor_scan(sums[:, 2 * W:2 * W + HW], reset[:, 0:HW],
                                                     terms[:, 2 * W:2 * W + HW], 0.0, ALU.mult, ALU.add))

            def scan_im(c, ks=(0, 1)):
                for k in ks:
                    dve.wait_ge(s_im, 2 * c + k + 1)
                    if c and k == 0:
                        dve.wait_ge(s_y, 2 * c)
                        dve.wait_ge(s_sq, 2 * c)
                    scan(W, k).then_inc(s_ims, 1)

            def denominator(c, weights_summed):
                own.need(weights_summed)
                a = own.mark(V.tensor_scalar(sc[:, c, :], sums[:, 2 * W:2 * W + HW], 1e-4, sqrt(LN_EPS),
                                             ALU.max, ALU.mult))
                own.need(a)
                return own.mark(V.tensor_tensor(sc[:, c, :], sc[:, c, :], sc[:, c, :], ALU.mult))

            def split(which, e, s, turn, own_):
                raw = w_raw[:, s, which, :]
                high, low = ((w1h[:, s, :], w1l[:, s, :]),
                             (w2h[:, s].rearrange("p f d -> p (f d)"), w2l[:, s].rearrange("p f d -> p (f d)")))[which]
                dve.wait_ge(s_w[2 * which + s], turn)
                a = own_.mark(V.tensor_scalar(high, raw, WS, None, ALU.mult))
                own_.need(a)
                V.scalar_tensor_tensor(low, raw, WS, high, ALU.mult, ALU.subtract).then_inc(m_wl, 1)

            def variance(c):
                dve.wait_ge(s_ss, c + 1)
                own.need(dens[c])
                V.scalar_tensor_tensor(sc[:, c, :], bank[:, SS_BANK[c], 0:HW], 1.0 / (2 * H * M), sc[:, c, :],
                                       ALU.mult, ALU.add).then_inc(s_v, 1)

            def gated(c):
                dve.wait_ge(s_f, c + 1)
                a = own.mark(V.tensor_tensor(gate[:, c, :], gate[:, c, :], sc[:, c, :], ALU.mult))
                own.need(a)
                V.tensor_tensor(y_gated[:, c, :], bank[:, Y_BANK[c], 0:HW], gate[:, c, :], ALU.mult).then_inc(s_yg, 1)

            def mixed(c):
                w = slice(c * PPH, (c + 1) * PPH)
                dve.wait_ge(s_o, c + 1)
                a = own.mark(V.tensor_tensor(x1[:, w, :], bank[0:PT, O_BANK[c], 0:PPH * D]
                                             .rearrange("p (j d) -> p j d", j=PPH), xtok[:, w, :], ALU.add))
                own.need(a)
                for j in range(c * PPH, (c + 1) * PPH):
                    a = own.mark(V.bn_stats(stat[:, j, :], x1[:, j, :]))
                own.need(a)
                for j in range(c * PPH, (c + 1) * PPH):
                    ins = V.bn_aggr(mv[:, j, :], stat[:, j, :])
                ins.then_inc(s_var, 1)

            def mixed_norm(c):
                dve.wait_ge(s_rstd, c + 1)
                for j in range(c * PPH, (c + 1) * PPH):
                    ins = V.tensor_scalar(x1[:, j, :], x1[:, j, :], mv[:, j, 0:1], rstd[:, j:j + 1],
                                          ALU.subtract, ALU.mult)
                ins.then_inc(s_x1, 1)

            phases(0, 0, between=lambda: clip(0))
            phases(0, 1)
            weights(0)
            terms_ready = [cos_terms(0, 0)]
            dve.wait_ge(s_turns, 1)
            phases(1, 0)
            terms_ready.append(cos_terms(0, 1))
            phases(1, 1)
            b = scan_re(0, terms_ready)
            clip(1)
            scan_im(0)
            dens = [denominator(0, b)]
            weights(1)
            terms_ready = [cos_terms(1, 0), cos_terms(1, 1)]
            gates(0)
            b = scan_re(1, terms_ready)
            variance(0)
            scan_im(1, [0])
            gated(0)
            scan_im(1, [1])
            dve.wait_ge(s_xtok, 16)
            mixed(0)
            dens.append(denominator(1, b))
            mixed_norm(0)
            gates(1)
            split(0, 0, 0, 16, own)

            V.memset(carrier[:], 0.0).then_inc(a_x2T, 1)
            loop = Own(dve, loop_v)

            def query_keys(i):
                dve.wait_ge(a_qk, i + 1)
                V.tensor_copy(qk_sb[:], bank[0:DC + 1, 7, 128:128 + PT]).then_inc(a_qksb, 1)

            def maximum(i):
                dve.wait_ge(a_s, i + 1)
                V.tensor_reduce(neg_max[0:GT, :], bank[0:GT, 0:SB, 0:SN], AX.XY, ALU.max,
                                negate=True).then_inc(a_max, 1)

            def x2T_copy(i):
                dve.wait_ge(a_x2t, i + 1)
                V.tensor_copy(x2T[:, bass.ds(i * PT, PT)], bank[:, 7, 384:384 + PT]).then_inc(a_x2T, 1)

            def inverse(i, s):
                dve.wait_ge(a_exp, i + 1)
                V.reciprocal(rden[:, s:s + 1], den[:, s:s + 1]).then_inc(a_rden, 1)

            def sum_copy(i, s):
                dve.wait_ge(a_rden, i + 1)
                dve.wait_ge(a_pv, i + 1)
                V.tensor_scalar(u_sb[:, 0:DC], bank[0:GT, 6, 0:DC], rden[:, s:s + 1], None, ALU.mult).then_inc(a_u, 1)

            def turned_copy(i):
                for n in (1, 2):
                    dve.wait_ge(a_t, 3 * i + n + 1)
                    V.tensor_copy(expT_sb[:, 4 * n:4 * n + 4, :], bank[0:KP, 3 + n, 0:4 * GT]
                                  .rearrange("p (c q) -> p c q", c=4)).then_inc(a_et, 1)

            def attended(i, check=True):
                dve.wait_ge(a_r, i + 1)
                V.tensor_tensor(res[:], bank[0:PT, 6, 128:128 + D],
                                x1[:, bass.ds(i, 1), :].rearrange("p i d -> p (i d)"), ALU.add).then_inc(a_vr, 1)
                dve.wait_ge(a_vr, i + 1)
                a = loop.mark(V.bn_stats(stat[:, 0, :], res[:]))
                loop.need(a)
                V.tensor_copy(carrier[:, 0:1], cst[:, 0:1])
                V.bn_aggr(mv[:, 0, :], stat[:, 0, :]).then_inc(a_res, 1)
                dve.wait_ge(a_rstd, i + 1)
                if check:
                    dve.wait_ge(a_x2t, i)
                    dve.wait_ge(a_x2s, 2 * i - 1)
                V.tensor_scalar(x2_now[:], res[:], mv[:, 0, 0:1], rstd[:, 0:1], ALU.subtract,
                                ALU.mult).then_inc(a_x2, 1)

            def attend_turn(i, s, stage=2, more=True, last=False):
                if not last:
                    maximum(i + 1)
                inverse(i, s)
                if stage:
                    sum_copy(i - 1, 1 - s)
                if more:
                    query_keys(i + 2)
                turned_copy(i)
                if stage == 2:
                    x2T_copy(i - 2)
                if stage:
                    attended(i - 1, stage == 2)

            query_keys(0)
            variance(1)
            split(1, 0, 0, 16, own)
            gated(1)
            maximum(0)
            query_keys(1)
            mixed(1)
            mixed_norm(1)
            attend_turn(0, 0, stage=0)
            split(0, 1, 1, 16, own)
            attend_turn(1, 1, stage=1)
            with dve.Fori(1, PAIRS // 2 - 1) as t:
                loop.turn(2 * t - 1)
                attend_turn(2 * t, 0)
                attend_turn(2 * t + 1, 1)
            loop.turn(PAIRS - 3)
            attend_turn(PAIRS - 2, 0, more=False)
            attend_turn(PAIRS - 1, 1, more=False, last=True)

            def hidden_low(e, s, n):
                f, c = part(e, n)
                dve.wait_ge(m_relu, 8 * e + n + 1)
                w = slice(c * PPH, (c + 1) * PPH)
                V.tensor_tensor(hl[:, s, f, w, 0:PT], hid[:, n % 4, :].rearrange("p (j t) -> p j t", j=PPH),
                                hh[:, s, f, w, 0:PT], ALU.subtract).then_inc(m_hl, 1)

            def add_outs(e, s, half):
                dve.wait_ge(m_l2, 2 * e + half + 3)
                dve.wait_ge(m_acc, 2 * e + half + 3)
                for j in range(PPH):
                    i = half * PPH + j
                    ins = V.scalar_tensor_tensor(acc[:, i, :], bank[0:PT, 4 + 2 * s + half, j * D:(j + 1) * D],
                                                 rws[:, i, bass.ds(e, 1)], acc[:, i, :], ALU.mult, ALU.add)
                ins.then_inc(m_acc, 1)

            hidden_low(0, 0, 0)
            hidden_low(0, 0, 1)
            x2T_copy(PAIRS - 2)
            sum_copy(PAIRS - 1, 1)
            attended(PAIRS - 1)
            x2T_copy(PAIRS - 1)
            hidden_low(0, 0, 2)

            weight_own = Own(dve, mo_v)
            dve.wait_ge(m_log, 1)
            a = own.mark(V.tensor_tensor(logit[:], bank[0:PT, 4, 0:PAIRS * E].rearrange("p (i e) -> p i e", i=PAIRS),
                                         par("b_r", PT).unsqueeze(1).broadcast_to([PT, PAIRS, E]), ALU.add))
            own.need(a)
            for i in range(PAIRS):
                a = own.mark(V.max(top[:, i, :], logit[:, i, :]))
            own.need(a)
            V.tensor_tensor(tsm[:, 0, :], top[:, :, 1], top[:, :, 0], ALU.subtract).then_inc(m_e, 1)
            for i in range(PAIRS):
                b = own.mark(V.max_index(topi[:, i, :], top[:, i, :], logit[:, i, :]))
            own.need(b)
            a = own.mark(V.tensor_copy(topf[:], topi[:, :, 0:2]))
            dve.wait_ge(m_e, 2)
            a = own.mark(V.tensor_scalar(tsm[:, 2, :], tsm[:, 1, :], 1.0, None, ALU.add))
            own.need(a)
            a = own.mark(V.reciprocal(tsm[:, 3, :], tsm[:, 2, :]))
            own.need(a)
            a = own.mark(V.tensor_tensor(tsm[:, 4, :], tsm[:, 1, :], tsm[:, 3, :], ALU.mult))
            iota = par("iota", PT).unsqueeze(1).broadcast_to([PT, PAIRS, E])

            def spread(x):
                return x.unsqueeze(2).broadcast_to([PT, PAIRS, E])

            own.mark(V.tensor_tensor(rw[:], iota, spread(topf[:, :, 0]), ALU.is_equal))
            b = own.mark(V.tensor_tensor(rws[:], iota, spread(topf[:, :, 1]), ALU.is_equal))
            own.need(b)
            own.mark(V.tensor_tensor(rw[:], rw[:], spread(tsm[:, 3, :]), ALU.mult))
            b = own.mark(V.tensor_tensor(rws[:], rws[:], spread(tsm[:, 4, :]), ALU.mult))
            own.need(b)
            V.tensor_tensor(rw[:], rw[:], rws[:], ALU.add).then_inc(m_rw, 1)
            dve.wait_ge(m_rw, 1)
            V.tensor_scalar(rws[:], rw[:], 1.0 / WS, None, ALU.mult).then_inc(m_rw, 1)
            hidden_low(0, 0, 3)
            hidden_low(0, 0, 4)
            dve.wait_ge(m_rt, 1)
            for half in range(HALVES):
                V.tensor_copy(rwT[:, half * HW:(half + 1) * HW], bank[0:E, 4 + half, 0:HW]).then_inc(m_rwT, 1)
            hidden_low(0, 0, 5)
            hidden_low(0, 0, 6)
            hidden_low(0, 0, 7)
            dve.wait_ge(m_l2, 2)
            for half in range(HALVES):
                w = slice(half * PPH, (half + 1) * PPH)
                V.tensor_tensor(acc[:, w, :], bank[0:PT, 6 + half, :].rearrange("p (j d) -> p j d", j=PPH),
                                x2[:, w, :], ALU.add).then_inc(m_acc, 2)

            def expert_turn(e, s, w1_turn, w2_turn):
                hidden_low(e + 1, 1 - s, 0)
                dve.wait_ge(m_l2, 2 * e + 2)
                split(1, e + 1, 1 - s, w2_turn, weight_own)
                hidden_low(e + 1, 1 - s, 1)
                hidden_low(e + 1, 1 - s, 2)
                if w1_turn is not None:
                    dve.wait_ge(m_l1, 8 * e + 8)
                    split(0, e + 2, s, w1_turn, weight_own)
                hidden_low(e + 1, 1 - s, 3)
                hidden_low(e + 1, 1 - s, 4)
                hidden_low(e + 1, 1 - s, 5)
                add_outs(e, s, 0)
                hidden_low(e + 1, 1 - s, 6)
                hidden_low(e + 1, 1 - s, 7)
                add_outs(e, s, 1)

            with dve.Fori(0, E // 2 - 1) as t:
                weight_own.turn(4 * t)
                expert_turn(2 * t, 0, 16 * t + 32, 16 * t + 16)
                expert_turn(2 * t + 1, 1, 16 * t + 32, 16 * t + 32)

            def stats(tiles, done):
                for j in tiles:
                    a = own.mark(V.bn_stats(stat[:, j, :], acc[:, j, :]))
                own.need(a)
                for j in tiles:
                    a = V.bn_aggr(mv[:, j, :], stat[:, j, :])
                a.then_inc(done, 1)

            def last_outs(part_):
                tiles = LAST_PARTS[part_]
                for j in tiles:
                    q = j // 2
                    if j % 2 == 0:
                        dve.wait_ge(m_last, q + 1)
                        if q < 2:
                            dve.wait_ge(m_acc, 2 * E + 1)
                        else:
                            dve.wait_ge(f_acc, q - 1)
                    a = own.mark(V.scalar_tensor_tensor(acc[:, j, :], bank[0:PT, LAST_BANK[q], (j % 2) * D:
                                                                           (j % 2 + 1) * D],
                                                        rws[:, j, E - 1:E], acc[:, j, :], ALU.mult, ALU.add))
                own.need(a)
                stats(tiles, f_var)
                dve.wait_ge(f_var, part_ + 1)
                for j in tiles:
                    a = own.mark(V.scalar_tensor_tensor(acc[:, j, :], acc[:, j, :], mv[:, j, 0:1], par("gamma", PT),
                                                        ALU.subtract, ALU.mult))
                return a

            def last_sum(part_, normed):
                dve.wait_ge(m_x2b, 1)
                own.need(normed)
                dve.wait_ge(f_rstd, part_ + 1)
                sums_done = []
                for j in LAST_PARTS[part_]:
                    a = own.mark(V.scalar_tensor_tensor(acc[:, j, :], acc[:, j, :], rstd[:, j:j + 1], x2b[:, j, :],
                                                        ALU.mult, ALU.add))
                    sums_done.append(a)
                for first in range(0, len(sums_done), 2):
                    own.need(sums_done[first + 1])
                    stats(LAST_PARTS[part_][first:first + 2], f_var2)

            def final_bias(q):
                w = slice(2 * q, 2 * q + 2)
                dve.wait_ge(f_rstd2, q + 1)
                V.scalar_tensor_tensor(nmr[:, w], mv[:, w, 0], -1.0, rstd2[:, w], ALU.mult, ALU.mult).then_inc(f_bias, 1)

            weight_own.turn(4 * (E // 2 - 1))
            hidden_low(E - 1, 1, 0)
            dve.wait_ge(m_l2, 2 * (E - 2) + 2)
            split(1, E - 1, 1, 16 * (E // 2), weight_own)
            for n in range(1, 4):
                hidden_low(E - 1, 1, n)
            add_outs(E - 2, 0, 0)
            a = last_outs(0)
            b = last_outs(1)
            last_sum(0, a)
            last_sum(1, b)
            final_bias(0)
            a = last_outs(2)
            final_bias(1)
            last_sum(2, a)
            final_bias(2)
            dve.wait_ge(f_rstd2, 4)
            for j in LAST_QUARTERS[3]:
                ins = V.tensor_scalar(x1[:, j, :], acc[:, j, :], mv[:, j, 0:1], rstd2[:, j:j + 1],
                                      ALU.subtract, ALU.mult)
            ins.then_inc(f_last, 1)

        @block.gpsimd
        def _(pool):
            own = Own(pool, own_g)
            G = nc.gpsimd
            G.memset(ctxT_slot[DC:DC + 1], 1.0).then_inc(s_ones, 1)
            pool.wait_ge(s_ones, 1)
            pool.wait_ge(s_cst, 1)
            pool.wait_ge(s_xv, 2)
            pool.wait_ge(s_sd, 2)
            for m in range(M):
                a = own.mark(G.tensor_scalar(ph[1][:, m, :], xv[:, 1, :], theta_t[:, m:m + 1], MAGIC,
                                             ALU.mult, ALU.add))
            own.need(a)
            G.tensor_scalar(ph[1], ph[1], -MAGIC, 2 * pi, ALU.add, ALU.mult).then_inc(s_turns, 1)

            def sin_terms(c):
                for k in range(2):
                    pool.wait_ge(s_sin, 2 * c + k + 1)
                    if k == 0:
                        pool.wait_ge(s_poly, c + 1)
                    if c:
                        pool.wait_ge(s_ims, 2 * c - 1 + k)
                    at = M * HW + 2 * k * HW
                    G.tensor_tensor(terms[:, at:at + 2 * HW].rearrange("p (m w) -> p m w", m=2),
                                    ph[c][:, 2 * k:2 * k + 2, :], poly[c].unsqueeze(1).broadcast_to([128, 2, HW]),
                                    ALU.mult).then_inc(s_im, 1)

            def fold(c):
                for n in range(2):
                    pool.wait_ge(s_sq, 2 * c + 1 + n)
                    at = n * M * HW
                    G.tensor_tensor(squares[:, at:at + 2 * HW], squares[:, at:at + 2 * HW],
                                    squares[:, at + 2 * HW:at + 4 * HW], ALU.add).then_inc(s_fold, 1)

            sin_terms(0)
            a = own.mark(G.tensor_scalar(poly[1], xv[:, 1, :], dsm[:, 11:12], dsm[:, 9:10], ALU.mult, ALU.add))
            own.need(a)
            G.tensor_tensor(poly[1], poly[1], xv[:, 1, :], ALU.mult).then_inc(s_qx, 1)
            fold(0)
            sin_terms(1)
            fold(1)

            loop = Own(pool, loop_g)

            def keep(i):
                pool.wait_ge(a_x2, i + 1)
                G.tensor_copy(x2[:, bass.ds(i, 1), :].rearrange("p i d -> p (i d)"), x2_now[:]).then_inc(a_x2s, 1)
                pool.wait_ge(a_x2T, i + 2)
                xs = bass.ds(i * PT, PT)
                a = loop.mark(G.tensor_copy(x2h[:, xs], x2T[:, xs]))
                loop.need(a)
                G.tensor_tensor(x2l[:, xs], x2T[:, xs], x2h[:, xs], ALU.subtract).then_inc(a_x2s, 1)

            with pool.Fori(0, PAIRS) as i:
                loop.turn(i)
                keep(i)

            pool.wait_ge(a_x2s, 2 * PAIRS)
            G.tensor_tensor(x2b, x2, par("beta", PT).unsqueeze(1).broadcast_to([PT, PAIRS, D]),
                            ALU.add).then_inc(m_x2b, 1)
            for x in (hh, hl):
                G.memset(x.rearrange("p s f j t -> p (s f j) t")[:, :, PT:HT], 0.0).then_inc(m_pad, 1)
            pool.wait_ge(m_hl, 8 * (E - 1) + 4)
            for n in range(4, 8):
                f, c = part(E - 1, n)
                pool.wait_ge(m_relu, 8 * (E - 1) + n + 1)
                w = slice(c * PPH, (c + 1) * PPH)
                G.tensor_tensor(hl[:, 1, f, w, 0:PT], hid[:, n % 4, :].rearrange("p (j t) -> p j t", j=PPH),
                                hh[:, 1, f, w, 0:PT], ALU.subtract).then_inc(m_hl, 1)
            pool.wait_ge(m_acc, 2 * E)
            for q in (2, 3):
                pool.wait_ge(f_scaled, q - 1)
                w = slice(2 * q, 2 * q + 2)
                G.tensor_tensor(acc[:, w, :], acc[:, w, :], x1[:, w, :], ALU.add).then_inc(f_acc, 1)

    return nc


def kernel(x, ctx_768, L0_attn_in_proj_w, L0_attn_conv_w, L0_attn_conv_b, L0_attn_theta, L0_attn_decay_slopes,
           L0_attn_anchor_slopes, L0_attn_score_scale, L0_attn_deriv_logits, L0_attn_norm_scale, L0_attn_W_re,
           L0_attn_W_im, L0_attn_out_proj_w, L0_xattn_Wq, L0_xattn_bq, L0_xattn_Wk, L0_xattn_bk, L0_xattn_Wv,
           L0_xattn_bv, L0_ffn_Wr, L0_ffn_br, L0_ffn_W1, L0_ffn_b1, L0_ffn_W2, L0_ffn_b2, L0_ffn_gamma,
           L0_ffn_beta):
    import concourse.bacc as bacc
    from concourse.bass_utils import run_bass_kernel_spmd

    def f32(a):
        return np.asarray(a)

    def rows(a):
        return np.broadcast_to(f32(a).reshape(1, -1), (128, f32(a).size))

    def pad(a):
        a = f32(a)
        return np.concatenate([a, np.zeros((128 - a.shape[0], a.shape[1]), a.dtype)])

    x = f32(x)
    w_in, cw, cb = f32(L0_attn_in_proj_w), f32(L0_attn_conv_w).reshape(TAPS, -1), f32(L0_attn_conv_b).reshape(1, -1)
    w_in, cw, cb = (np.concatenate([a[:, :2 * D], np.repeat(a[:, 2 * D:], H, axis=1)], axis=1) for a in (w_in, cw, cb))
    group = np.arange(128) // H
    pos = np.arange(L)
    dist = np.where((np.arange(128) < H * (K - 4))[:, None], (L - 1 - pos)[None], pos[None]).astype(np.float32)
    w_ri = np.concatenate([f32(L0_attn_W_re).reshape(H, M, H), f32(L0_attn_W_im).reshape(H, M, H)], axis=1)
    ns = f32(L0_attn_norm_scale).reshape(2, H, M).transpose(1, 0, 2).reshape(H, 2 * M)
    small = {
        "w_in": w_in,
        "conv_b": cb.reshape(3, 128).T,
        "theta": f32(L0_attn_theta).reshape(128, M),
        "slope": np.repeat(np.concatenate([f32(L0_attn_decay_slopes), f32(L0_attn_anchor_slopes)]), H)[:, None],
        "dist": dist,
        "score_scale": np.repeat(f32(L0_attn_score_scale), H)[:, None],
        "deriv": rows(L0_attn_deriv_logits),
        "norm_scale": np.tile(ns, (K, 1)),
        "w_ri": np.tile(w_ri.reshape(H, 2 * M * H), (K, 1)),
        "group_mask": (group[:, None] == group[None]).astype(np.float32),
        "ident": np.eye(128, dtype=np.float32),
        "w_out": f32(L0_attn_out_proj_w),
        "w_q": f32(L0_xattn_Wq),
        "b_q": f32(L0_xattn_bq)[:, None],
        "w_k": np.concatenate([f32(L0_xattn_Wk), f32(L0_xattn_bk)[None]]).T,
        "w_v": pad(np.concatenate([f32(L0_xattn_Wv), f32(L0_xattn_bv)[None]])),
        "w_r": f32(L0_ffn_Wr).T,
        "b_r": rows(L0_ffn_br),
        "gamma": rows(L0_ffn_gamma),
        "beta": rows(L0_ffn_beta),
        "b_1": f32(L0_ffn_b1).reshape(E * FC, 128).T,
        "b_2": pad(L0_ffn_b2),
        "iota": rows(np.arange(E, dtype=np.float32)),
    }
    ctx = f32(ctx_768)
    arrays = {
        "x_T": np.pad(x.transpose(2, 0, 1), ((0, 0), (0, 0), (TAPS - 1, 0))),
        "x_tok": x.reshape(PAIRS, PT, D).transpose(1, 0, 2),
        "ctx": ctx.reshape(B, KP, KC, DC),
        "ctx_T": ctx.reshape(B, KP, KC, DC).transpose(0, 3, 2, 1).reshape(B, DC, SK),
        "first": np.concatenate([small[name] for name, _ in FIRST], axis=1),
        "conv_w": cw.reshape(TAPS, 3, D).transpose(1, 0, 2).reshape(-1),
        "small": np.concatenate([small[name] for name, _ in SMALL], axis=1),
        "w_1": f32(L0_ffn_W1).transpose(0, 2, 1),
        "w_2": f32(L0_ffn_W2).reshape(E, D, FC, 128).transpose(0, 3, 2, 1).reshape(E, 128, FC * D),
    }
    arrays = {name: np.ascontiguousarray(a) for name, a in arrays.items()}
    nc = bacc.Bacc("TRN2", target_bir_lowering=False, num_devices=1)
    args = [nc.dram_tensor(name, a.shape, mybir.dt.from_np(a.dtype), kind="ExternalInput").ap()
            for name, a in arrays.items()]
    out = nc.dram_tensor("out", (PT, PAIRS, D), F32, kind="ExternalOutput").ap()
    decoder_kernel(nc, *args, out)
    ran = run_bass_kernel_spmd(nc, [arrays], core_ids=[0])
    return ran.results[0]["out"].transpose(1, 0, 2).reshape(B, L, D)
```
